# Optimizing a Trainium2 kernel written in Bass

```python
import numpy as np
import jax
import jax.numpy as jnp

def _softmax(x, axis=-1):
    return jax.nn.softmax(x, axis=axis)

def _gelu(x):
    return jax.nn.gelu(x, approximate=True)

def _silu(x):
    return jax.nn.silu(x)

def _sigmoid(x):
    return jax.nn.sigmoid(x)

def _layernorm(x, axis=-1, eps=1e-05):
    m = jnp.mean(x, axis=axis, keepdims=True)
    v = jnp.var(x, axis=axis, keepdims=True)
    return (x - m) / jnp.sqrt(v + eps)

def _scatter_add(tgt, idx, src, axis=0):
    return tgt.at[idx].add(src)

def _segment_sum(src, seg, n):
    return jax.ops.segment_sum(src, seg, n)
kernel_name = 'mk_seq_preln_d1_jaxref_r8_9fd931'

def setup_inputs(seed: int=0):
    np.random.seed(seed)
    _w = jnp.asarray

    def _L0_attn_setup():
        import jax, jax.numpy as jnp
        import numpy as np
        N_EMBD = 128
        N_HEAD = 16
        HEAD_DIM = N_EMBD // N_HEAD
        KV_RANK = 32
        Q_RANK = 64
        ROPE_DIM = 32
        B, T = (2, 256)
        EPS = 1e-06

        def _rope_tables(T, dim):
            inv_freq = 1.0 / 10000.0 ** (np.arange(0, dim, 2, dtype=np.float32) / dim)
            t = np.arange(T, dtype=np.float32)
            freqs = np.outer(t, inv_freq)
            emb = np.concatenate([freqs, freqs], -1)
            return (jnp.asarray(np.cos(emb)), jnp.asarray(np.sin(emb)))

        def _apply_rope(x, cos, sin):
            d2 = x.shape[-1] // 2
            x1, x2 = (x[..., :d2], x[..., d2:])
            rot = jnp.concatenate([-x2, x1], axis=-1)
            return x * cos[None, None, :, :] + rot * sin[None, None, :, :]
        key = jax.random.key(seed)
        ks = jax.random.split(key, 10)

        def w(k, fan_in, fan_out):
            return jax.random.normal(k, (fan_in, fan_out), dtype=jnp.float32) * fan_in ** (-0.5)
        return {'x': jax.random.normal(ks[0], (B, T, N_EMBD), dtype=jnp.float32), 'W_kv': w(ks[1], N_EMBD, KV_RANK), 'g_kv': jnp.ones((KV_RANK,), dtype=jnp.float32), 'W_kdec': w(ks[2], KV_RANK, N_HEAD * HEAD_DIM), 'W_vdec': w(ks[3], KV_RANK, N_HEAD * HEAD_DIM), 'W_q': w(ks[4], N_EMBD, Q_RANK), 'W_qdec': w(ks[5], Q_RANK, N_HEAD * HEAD_DIM), 'W_krope': w(ks[6], N_EMBD, N_HEAD * ROPE_DIM), 'W_qrope': w(ks[7], Q_RANK, N_HEAD * ROPE_DIM), 'W_o': w(ks[8], N_HEAD * HEAD_DIM, N_EMBD)}
    _L0_attn_in = _L0_attn_setup()

    def _L0_ffn_setup():
        import jax, jax.numpy as jnp
        import numpy as np
        T, Z, D_DIM = (8, 256, 128)
        N_EXP, P_SLOT, H = (64, 32, 128)
        LN_EPS = 1e-05
        key = jax.random.key(seed)
        k = jax.random.split(key, 5)
        s = 0.02
        return {'x': jax.random.normal(k[0], (T, Z, D_DIM), dtype=jnp.float32), 'phi_w': jax.random.normal(k[1], (N_EXP * P_SLOT, D_DIM), dtype=jnp.float32) * s, 'phi_b': jax.random.normal(k[2], (N_EXP * P_SLOT,), dtype=jnp.float32) * s, 'expert_w': jax.random.normal(k[3], (N_EXP, D_DIM, H), dtype=jnp.float32) * s, 'expert_b': jax.random.normal(k[4], (N_EXP, H), dtype=jnp.float32) * s}
    _L0_ffn_in = _L0_ffn_setup()
    _d = {'L0_attn_x': _L0_attn_in['x'], 'L0_attn_W_kv': _L0_attn_in['W_kv'], 'L0_attn_g_kv': _L0_attn_in['g_kv'], 'L0_attn_W_kdec': _L0_attn_in['W_kdec'], 'L0_attn_W_vdec': _L0_attn_in['W_vdec'], 'L0_attn_W_q': _L0_attn_in['W_q'], 'L0_attn_W_qdec': _L0_attn_in['W_qdec'], 'L0_attn_W_krope': _L0_attn_in['W_krope'], 'L0_attn_W_qrope': _L0_attn_in['W_qrope'], 'L0_attn_W_o': _L0_attn_in['W_o'], 'L0_ffn_phi_w': _L0_ffn_in['phi_w'], 'L0_ffn_phi_b': _L0_ffn_in['phi_b'], 'L0_ffn_expert_w': _L0_ffn_in['expert_w'], 'L0_ffn_expert_b': _L0_ffn_in['expert_b']}
    _x0 = _d['L0_attn_x']
    _d['L0_attn_x'] = jax.random.normal(jax.random.fold_in(jax.random.key(seed), 1), (16, 256, 128), dtype=_x0.dtype)
    del _x0
    return _d

def reference(L0_attn_x, L0_attn_W_kv, L0_attn_g_kv, L0_attn_W_kdec, L0_attn_W_vdec, L0_attn_W_q, L0_attn_W_qdec, L0_attn_W_krope, L0_attn_W_qrope, L0_attn_W_o, L0_ffn_phi_w, L0_ffn_phi_b, L0_ffn_expert_w, L0_ffn_expert_b):

    def _L0_attn_ref(x, W_kv, g_kv, W_kdec, W_vdec, W_q, W_qdec, W_krope, W_qrope, W_o):
        import jax, jax.numpy as jnp
        import numpy as np
        N_EMBD = 128
        N_HEAD = 16
        HEAD_DIM = N_EMBD // N_HEAD
        KV_RANK = 32
        Q_RANK = 64
        ROPE_DIM = 32
        B, T = (2, 256)
        EPS = 1e-06

        def _rope_tables(T, dim):
            inv_freq = 1.0 / 10000.0 ** (np.arange(0, dim, 2, dtype=np.float32) / dim)
            t = np.arange(T, dtype=np.float32)
            freqs = np.outer(t, inv_freq)
            emb = np.concatenate([freqs, freqs], -1)
            return (jnp.asarray(np.cos(emb)), jnp.asarray(np.sin(emb)))

        def _apply_rope(x, cos, sin):
            d2 = x.shape[-1] // 2
            x1, x2 = (x[..., :d2], x[..., d2:])
            rot = jnp.concatenate([-x2, x1], axis=-1)
            return x * cos[None, None, :, :] + rot * sin[None, None, :, :]
        Bx, Tx, C = x.shape
        kv_c = x @ W_kv
        kv_c = kv_c * jax.lax.rsqrt(jnp.mean(kv_c * kv_c, axis=-1, keepdims=True) + EPS) * g_kv
        q_c = x @ W_q

        def heads(y, d):
            return y.reshape(Bx, Tx, N_HEAD, d).transpose(0, 2, 1, 3)
        k_content = heads(kv_c @ W_kdec, HEAD_DIM)
        v = heads(kv_c @ W_vdec, HEAD_DIM)
        q_content = heads(q_c @ W_qdec, HEAD_DIM)
        k_rope = heads(x @ W_krope, ROPE_DIM)
        q_rope = heads(q_c @ W_qrope, ROPE_DIM)
        cos, sin = _rope_tables(Tx, ROPE_DIM)
        q_rope = _apply_rope(q_rope, cos, sin)
        k_rope = _apply_rope(k_rope, cos, sin)
        q = jnp.concatenate([q_content, q_rope], axis=-1)
        k = jnp.concatenate([k_content, k_rope], axis=-1)
        scale = 1.0 / jnp.sqrt(jnp.float32(q.shape[-1]))
        scores = jnp.einsum('bhqd,bhkd->bhqk', q, k) * scale
        causal = jnp.tril(jnp.ones((Tx, Tx), dtype=bool))
        scores = jnp.where(causal[None, None], scores, jnp.float32(-jnp.inf))
        attn = jax.nn.softmax(scores, axis=-1)
        out = jnp.einsum('bhqk,bhkd->bhqd', attn, v)
        out = out.transpose(0, 2, 1, 3).reshape(Bx, Tx, N_HEAD * HEAD_DIM)
        return out @ W_o

    def _L0_ffn_ref(x, phi_w, phi_b, expert_w, expert_b):
        import jax, jax.numpy as jnp
        import numpy as np
        T, Z, D_DIM = (8, 256, 128)
        N_EXP, P_SLOT, H = (64, 32, 128)
        LN_EPS = 1e-05
        t, z, d = x.shape
        n = expert_w.shape[0]
        p = phi_w.shape[0] // n
        logits = (jnp.einsum('tzd,ed->tze', x, phi_w) + phi_b).reshape(t, z, n, p)
        D = jax.nn.softmax(logits, axis=3)
        C = jax.nn.softmax(logits, axis=2)
        X_tilde = jnp.einsum('tznp,tzd->npd', D, x)
        X_tilde = jnp.clip(X_tilde, -33000.0, 65000.0)
        mu = jnp.mean(X_tilde, axis=-1, keepdims=True)
        var = jnp.mean(jnp.square(X_tilde - mu), axis=-1, keepdims=True)
        X_tilde = (X_tilde - mu) * jax.lax.rsqrt(var + LN_EPS)
        X_tilde = jnp.tanh(X_tilde)
        Y_tilde = jnp.einsum('npd,ndH->npH', X_tilde, expert_w) + expert_b[:, None, :]
        Y = jnp.einsum('tznp,npH->tzH', C, Y_tilde)
        return Y
    x = L0_attn_x
    x = x + _L0_attn_ref(_layernorm(x, axis=-1), L0_attn_W_kv, L0_attn_g_kv, L0_attn_W_kdec, L0_attn_W_vdec, L0_attn_W_q, L0_attn_W_qdec, L0_attn_W_krope, L0_attn_W_qrope, L0_attn_W_o)
    x = x + _L0_ffn_ref(_layernorm(x, axis=-1), L0_ffn_phi_w, L0_ffn_phi_b, L0_ffn_expert_w, L0_ffn_expert_b)
    return x

_drawn_inputs = setup_inputs


def setup_inputs(seed=0):
    import zlib

    import numpy as np

    out = dict(_drawn_inputs(seed))
    spreads = {'L0_attn_g_kv': (1.0, 0.2)}
    factors = {'L0_ffn_phi_b': 38.371}
    for name, (base, spread) in spreads.items():
        noise = np.random.default_rng([zlib.crc32(name.encode()), seed]).standard_normal(out[name].shape)
        drawn = base * np.exp(spread * noise) if base else spread * noise
        out[name] = jnp.asarray(drawn.astype(out[name].dtype))
    for name, factor in factors.items():
        out[name] = (out[name] * factor).astype(out[name].dtype)
    return out
```

```python
import concourse.bass as bass
from concourse import mybir
from contextlib import ExitStack

F32 = mybir.dt.float32
F32R = mybir.dt.float32r
BF16 = mybir.dt.bfloat16
F16 = mybir.dt.float16
ALU = mybir.AluOpType
ACT = mybir.ActivationFunctionType
AX = mybir.AxisListType

BATCH, T, D = 16, 256, 128
HEADS, HD, ROPE = 16, 8, 32
QR, KVR = 64, 32
SCALE = float(HD + ROPE) ** -0.5
GROUPS, PER = 4, 4
EXPERTS, SLOTS = 64, 32
NS = EXPERTS * SLOTS
HALF, HALF_E = NS // 2, EXPERTS // 2
TILES = BATCH * T // 128
LN_EPS, RMS_EPS = 1e-5, 1e-6
CLIP_LOW, CLIP_HIGH = -33000.0, 65000.0
UNITS = 9
STACKED = 16 * 30
PLACES = [{(0, 1): 0, (0, 0): 1, (1, 1): 2}, {(0, 0): 0, (1, 1): 1, (0, 1): 2}]
CHUNK = 512
STEPS = BATCH * T // CHUNK
NCH = NS // 128


def wait(eng, sem, value):
    if isinstance(value, int) and value <= 0:
        return
    eng.wait_ge(sem, value)


class Chain:

    def __init__(self, eng, sem):
        self.eng, self.sem, self.per, self.n, self.base = eng, sem, None, 0, 0

    def start(self, turn):
        if self.per is None and self.n:
            self.per = self.n
        self.base, self.n = (turn * self.per if self.per else 0), 0

    def link(self, ins):
        self.n += 1
        ins.then_inc(self.sem, 1)
        self.eng.wait_ge(self.sem, self.base + self.n)


def settle(eng, passed):
    eng.sem_inc(passed, 1)


def layernorm(dve, passed, link, src, stats, moments, var, rstd, var_ready, rstd_ready, turn, dst):
    for i in range(2):
        ins = dve.bn_stats(stats[:, i, :], src[:, i, :])
    link(ins)
    settle(dve, passed)
    for i in range(2):
        ins = dve.bn_aggr(moments[:, i, :], stats[:, i, :])
    link(ins)
    dve.tensor_scalar(var[:, :], moments[:, :, 1], LN_EPS, None, ALU.add).then_inc(var_ready, 1)
    wait(dve, rstd_ready, turn)
    for i in range(2):
        ins = dve.tensor_scalar(dst[:, i, :], src[:, i, :], moments[:, i, 0:1], rstd[:, i:i + 1],
                                ALU.subtract, ALU.mult)
    return ins


def layer_kernel(nc, x, w_qkv, w_k, w_q, w_kcv, w_qc, g_kv, w_o, phi_t, phi_b, exp_w, exp_b,
                 c_ident, c_rope, c_mask, c_ones, c_same, c_dshift, c_cshift, c_expert,
                 content_d, max_d, out):
    with ExitStack() as stack:
        def sb(name, shape, dt=F32):
            return stack.enter_context(nc.sbuf_tensor(name, shape, dt))
        x2 = sb("x2", [128, TILES, D])
        xn2 = sb("xn2", [128, TILES, D])
        xT2h = sb("xT2h", [128, TILES * 128], F32R)
        xT2l = sb("xT2l", [128, TILES * 128], F32R)
        ident = sb("ident", [128, 128])
        attention(nc, x, w_qkv, w_k, w_q, w_kcv, w_qc, g_kv, w_o, c_ident, c_rope, c_mask,
                  c_ones, content_d, max_d, x2, xn2, xT2h, xT2l, ident)
        phT_h = sb("phT_h", [128, NS], F32R)
        phT_l = sb("phT_l", [128, NS], F32R)
        mcT = sb("mcT", [3 * SLOTS, TILES * 128], BF16)
        yt = sb("yt", [128, NCH, D])
        dispatch(nc, phi_t, phi_b, exp_w, exp_b, c_dshift, c_expert, xn2, xT2h, xT2l, ident,
                 phT_h, phT_l, mcT, yt)
        combine(nc, phi_b, c_cshift, c_same, x2, xT2h, xT2l, ident, phT_h, phT_l, mcT, yt, out)


def attention(nc, x, w_qkv, w_k, w_q, w_kcv, w_qc, g_kv, w_o, c_ident, c_rope, c_mask,
              c_ones, content_d, max_d, x2, xn2, xT2h, xT2l, ident):
    with ExitStack() as stack:
        def sb(name, shape, dt=F32):
            return stack.enter_context(nc.sbuf_tensor(name, shape, dt))

        def pb(name, shape, dt=F32):
            return stack.enter_context(nc.psum_tensor(name, shape, dt))

        def sem(name):
            return stack.enter_context(nc.semaphore(name))

        wraw = sb("wraw", [128, 2, 1024])
        wkh, wkl = sb("wkh", [128, 1024], F32R), sb("wkl", [128, 1024], F32R)
        wqh, wql = sb("wqh", [128, 1024], F32R), sb("wql", [128, 1024], F32R)
        craw = sb("craw", [128, 3, 128])
        wqch, wqcl = sb("wqch", [128, 128], F32R), sb("wqcl", [128, 128], F32R)
        gain = sb("gain", [128, 1])
        cgain = sb("cgain", [128, 2, 128])
        cgain_hi = sb("cgain_hi", [128, 2, 128], F32R)
        wkcv = sb("wkcv", [128, 2, 128], F32R)
        wqkv = sb("wqkv", [128, QR + KVR])
        wo = sb("wo", [128, D])
        rope = sb("rope", [128, 2, T])
        maskf = sb("maskf", [128, 128])
        ident16 = sb("ident16", [128, 128], F16)
        identb = sb("identb", [128, 128], BF16)
        mask = sb("mask", [128, 2, 128], BF16)
        ones = sb("ones", [128, PER, 32])
        xt = sb("xt", [128, 2, 2, D])
        xr = sb("xr", [128, 2, D])
        stats, stats2 = sb("stats", [128, 2, 6]), sb("stats2", [128, 2, 6])
        moments, moments2 = sb("moments", [128, 2, 2]), sb("moments2", [128, 2, 2])
        rstd, rstd2 = sb("rstd", [128, 2]), sb("rstd2", [128, 2])
        xn = sb("xn", [128, 2, D])
        lat = sb("lat", [128, 2, QR + KVR])
        sq, kvn = sb("sq", [128, 2, KVR]), sb("kvn", [128, 2, KVR])
        ssum, mkv, rkv = sb("ssum", [128, 2]), sb("mkv", [128, 2]), sb("rkv", [128, 2])
        var, var2 = sb("var", [128, 2]), sb("var2", [128, 2])
        power = sb("power", [128, 2])
        lst = sb("lst", [128, 2, 256], F32R)
        mx = sb("mx", [128, 2, HEADS])
        mp = sb("mp", [128, 2, 2, HEADS], F16)
        x2s, xn2s = sb("x2s", [128, 2, D]), sb("xn2s", [128, 2, D])
        vp = sb("vp", [128, 2, 2, HEADS * 32 + 32])
        xT, xT2 = sb("xT", [128, T]), sb("xT2", [128, T])
        xTh, xTl = sb("xTh", [128, T], F32R), sb("xTl", [128, T], F32R)
        lT = sb("lT", [128, 4, 128], F32R)
        prod = sb("prod", [128, 2, 4, 2, T])
        rot = sb("rot", [128, 2, 4 * T])
        rh, rl = sb("rh", [128, 2, 4 * T], F16), sb("rl", [128, 2, 4 * T], F16)
        ch, cl = sb("ch", [128, 2 * T], F16), sb("cl", [128, 2 * T], F16)
        mT = sb("mT", [2 * HEADS, T], F16)
        qs = [sb(f"qs{i}", [128, HEADS, T], F16) for i in range(2)]
        ks = [sb(f"ks{i}", [128, HEADS, T], F16) for i in range(2)]
        pt = sb("pt", [128, 2, GROUPS, 384])
        rden, outT = sb("rden", [128, T]), sb("outT", [128, T])

        proj = pb("proj", [128, 2, 512])
        score = pb("score", [128, 4, 512])
        acc = pb("acc", [128, 512])
        misc = pb("misc", [128, 512])

        loaded, zeroed = sem("weights_loaded"), sem("zeroed")
        cast, weights_ready = sem("weights_cast"), sem("weights_ready")
        x_in = [sem("x_in0"), sem("x_in1")]
        xr_in = sem("xr_in")
        xn_ready, xT_ps = sem("xn_ready"), sem("xT_ps")
        xT_ready, xTl_ready = sem("xT_ready"), sem("xTl_ready")
        lat_ps, lat_read, lst_ready = sem("lat_ps"), sem("lat_read"), sem("lst_ready")
        lT_ps, lT_ready = sem("lT_ps"), sem("lT_ready")
        proj_done, proj_read = sem("proj_done"), sem("proj_read")
        content_hi, content_out = sem("content_hi"), sem("content_out")
        rope_sum, rope_hi, rope_lo = sem("rope_sum"), sem("rope_hi"), sem("rope_lo")
        stack_in = [sem("stack_in0"), sem("stack_in1")]
        rows_done, max_read, mp_ready = sem("rows_done"), sem("max_read"), sem("mp_ready")
        mT_ps, mT_ready, m_out, m_in = sem("mT_ps"), sem("mT_ready"), sem("m_out"), sem("m_in")
        st_done, exp_done, masked, pv_done = (sem("st_done"), sem("exp_done"), sem("masked"),
                                              sem("pv_done"))
        out_ready, y_ps, x2_ready = sem("out_ready"), sem("y_ps"), sem("x2_ready")
        v_ps, v_ready = sem("v_ps"), sem("v_ready")
        xn2_ready, xT2_ps, xT2_read = sem("xn2_ready"), sem("xT2_ps"), sem("xT2_read")
        xT2_done, kept = sem("xT2_done"), sem("kept")
        var_ready, rstd_ready = sem("var_ready"), sem("rstd_ready")
        var2_ready, rstd2_ready = sem("var2_ready"), sem("rstd2_ready")
        mkv_ready, rkv_ready = sem("mkv_ready"), sem("rkv_ready")
        c_set, c_ln1, c_lat = sem("chain_setup"), sem("chain_ln1"), sem("chain_latent")
        c_max, c_ln2, c_norm = sem("chain_max"), sem("chain_ln2"), sem("chain_norm")
        passed_dve, passed_pool = sem("passed_dve"), sem("passed_pool")
        LOADS = 19

        def steps(eng, step):
            step(-1, 1, False, False, True)
            step(0, 0, False, True, True)
            step(0, 1, True, True, True)
            with eng.Fori(1, BATCH // 2 - 1) as pair:
                step(pair, 0, True, True, True)
                step(pair, 1, True, True, True)
            step(BATCH // 2 - 1, 0, True, True, True)
            step(BATCH // 2 - 1, 1, True, True, False)
            step(BATCH // 2, 0, True, False, False)

        def unit_heads(u):
            return [PER * (2 * (u % 2) + e) + u // 2 for e in range(2)]

        with nc.Block() as block:
            @block.sync
            def _(sp):
                def x_of(b):
                    if isinstance(b, int):
                        return x[b].rearrange("(i p) d -> p i d", p=128)
                    return x[bass.ds(b, 1)].rearrange("a (i p) d -> p (a i) d", p=128)

                for dst, src in ((wqkv[:, :], w_qkv), (ident[:, :], c_ident),
                                 (wraw[:, 0, :], w_k), (rope[:, :, :], c_rope),
                                 (maskf[:, :], c_mask), (ones[:, :, :], c_ones), (wo[:, :], w_o)):
                    sp.dma_start(dst, src).then_inc(loaded, 16)
                for i in range(2):
                    sp.dma_start(wraw[64 * i:64 * i + 64, 1, :], w_q).then_inc(loaded, 16)
                for i in range(2):
                    sp.dma_start(craw[64 * i:64 * i + 64, 0, :], w_qc).then_inc(loaded, 16)
                for i in range(4):
                    sp.dma_start(craw[32 * i:32 * i + 32, 1:3, :], w_kcv).then_inc(loaded, 16)
                for i in range(3):
                    sp.dma_start(gain[32 * i:32 * i + 32, :], g_kv).then_inc(loaded, 16)
                sp.dma_start(gain[96:128, :], g_kv).then_inc(loaded, 16)

                def step(pair, par, prev, cur, nxt):
                    k = 2 * pair + par
                    if nxt:
                        wait(sp, xn_ready, k)
                        sp.dma_start(xt[:, 1 - par], x_of(k + 1)).then_inc(x_in[1 - par], 16)
                    if prev:
                        wait(sp, x2_ready, k - 1)
                        sp.dma_start(xr[:, :, :], x_of(k - 1)).then_inc(xr_in, 16)
                        wait(sp, mT_ready, k)
                        sp.dma_start(max_d, mT[:, :]).then_inc(m_out, 16)
                        wait(sp, m_out, 16 * k)
                        sp.dma_start(qs[1 - par][120:122, :, :],
                                     max_d.rearrange("(a h) t -> a h t", a=2)).then_inc(m_in, 16)
                    if cur:
                        def rotary(side, dst, part, ready, rows):
                            wait(sp, ready, 2 * k + side + 1)
                            for g in range(GROUPS):
                                for r in rows:
                                    sp.dma_start(dst[r:r + 32, PER * g:PER * g + PER, :],
                                                 part[32 * g:32 * g + 32, side, :]
                                                 .rearrange("p (c t) -> p c t", c=4)
                                                 ).then_inc(stack_in[par], 16)

                        wait(sp, st_done, 8 * (k - 1))
                        rotary(0, ks[par], rh, rope_hi, (0, 64))
                        rotary(0, ks[par], rl, rope_lo, (32,))
                        wait(sp, content_hi, k + 1)
                        sp.dma_start(content_d[0], ch[:, :]).then_inc(content_out, 16)
                        wait(sp, proj_read, UNITS * (k + 1))
                        sp.dma_start(content_d[1], cl[:, :]).then_inc(content_out, 16)
                        wait(sp, content_out, 32 * (k + 1))
                        for dst, side, parts in ((ks[par], 1, (0, 1, 0)), (qs[par], 0, (0, 0, 1))):
                            for i, part in enumerate(parts):
                                sp.dma_start(dst[96 + 8 * i:104 + 8 * i, :, :],
                                             content_d[part]
                                             .rearrange("(h d) (s t) -> s d h t", d=HD, s=2)[side]
                                             ).then_inc(stack_in[par], 16)
                        rotary(1, qs[par], rh, rope_hi, (0, 32))
                        rotary(1, qs[par], rl, rope_lo, (64,))
                    if prev:
                        wait(sp, xn2_ready, k)
                        for dst, src in ((x2, x2s), (xn2, xn2s)):
                            sp.dma_start(dst[:, bass.ds(2 * (k - 1), 2), :],
                                         src[:, :, :]).then_inc(kept, 16)
                steps(sp, step)
                sp.wait_ge(kept, 32 * BATCH)

            @block.gpsimd
            def _(pool):
                fills = [(power[:, :], -0.5)]
                for i in range(2):
                    fills += [(ks[i][96:128, :, :], -1.0), (qs[i][96:128, :, :], 0.0),
                              (vp[:, i], 0.0)]
                for n, (place, value) in enumerate(fills):
                    pool.memset(place, value).then_inc(zeroed, 1)
                    pool.wait_ge(zeroed, n + 1)

                def step(pair, par, prev, cur, nxt):
                    k = 2 * pair + par

                    def inverse_root(src, ready, dst, done, turn):
                        wait(pool, ready, turn)
                        pool.tensor_tensor(dst[:, :], src[:, :], power[:, :],
                                           ALU.pow).then_inc(done, 1)

                    def add(side):
                        wait(pool, proj_read, UNITS * k + 4 * side + 4)
                        wait(pool, rope_hi, 2 * (k - 1) + side + 1)
                        wait(pool, rope_lo, 2 * (k - 1) + side + 1)
                        pool.tensor_tensor(rot[:, side, :].rearrange("p (c t) -> p c t", c=4),
                                           prod[:, side, :, 0, :], prod[:, side, :, 1, :],
                                           ALU.add).then_inc(rope_sum, 1)

                    def low(side):
                        wait(pool, rope_sum, 2 * k + side + 1)
                        wait(pool, rope_hi, 2 * k + side + 1)
                        wait(pool, stack_in[1 - par], STACKED * (pair + par))
                        pool.tensor_tensor(rl[:, side, :], rot[:, side, :], rh[:, side, :],
                                           ALU.subtract).then_inc(rope_lo, 1)

                    def causal(g):
                        for u in (2 * g, 2 * g + 1):
                            wait(pool, exp_done, 8 * (k - 1) + u + 1)
                            settle(pool, passed_pool)
                            diag = pt[:, g % 2, 2 * (u % 2):2 * (u % 2) + 2, :].rearrange(
                                "p h t -> p (h t)")[:, 128:640].rearrange("p (b t) -> p b t", b=4)
                            pool.affine_select(out=diag, in_=diag, compare_op=ALU.is_ge, fill=0.0,
                                               base=0, pattern=[[0, 4], [1, 128]],
                                               channel_multiplier=-1).then_inc(masked, 1)
                    if cur:
                        add(0)
                        low(0)
                        add(1)
                    if nxt:
                        inverse_root(var, var_ready, rstd, rstd_ready, k + 2)
                    if prev:
                        causal(0)
                    if cur:
                        low(1)
                    if prev:
                        for g in range(1, 4):
                            causal(g)
                        inverse_root(var2, var2_ready, rstd2, rstd2_ready, k)
                    if nxt:
                        inverse_root(mkv, mkv_ready, rkv, rkv_ready, k + 2)
                steps(pool, step)

            @block.scalar
            def _(act):
                act.wait_ge(loaded, 16 * LOADS)
                act.activation(wkh[:, :], wraw[:, 0, :], ACT.Copy).then_inc(cast, 1)
                act.activation(wqh[:, :], wraw[:, 1, :], ACT.Copy).then_inc(cast, 1)
                act.activation(wqch[:, :], craw[:, 0, :], ACT.Copy).then_inc(cast, 1)
                act.activation(ident16[:, :], ident[:, :], ACT.Copy).then_inc(cast, 1)
                act.activation(identb[:, :], ident[:, :], ACT.Copy).then_inc(cast, 1)
                for i in range(2):
                    act.activation(mask[:, i, :], maskf[:, :], ACT.Copy).then_inc(cast, 1)
                act.wait_ge(zeroed, 7)

                def step(pair, par, prev, cur, nxt):
                    k = 2 * pair + par

                    def rotary_hi(side):
                        wait(act, rope_sum, 2 * k + side + 1)
                        wait(act, stack_in[1 - par], STACKED * (pair + par))
                        act.activation(rh[:, side, :], rot[:, side, :],
                                       ACT.Copy).then_inc(rope_hi, 1)

                    def exps(u):
                        wait(act, st_done, 8 * (k - 1) + u + 1)
                        wait(act, pv_done, 4 * (k - 1) + u // 2 - 1)
                        b = 2 * (u % 2)
                        act.activation(pt[:, (u // 2) % 2, b:b + 2, :], score[:, b:b + 2, 0:384],
                                       ACT.Exp, scale=SCALE).then_inc(exp_done, 1)
                    if prev:
                        wait(act, mT_ps, k)
                        wait(act, m_out, 16 * (k - 1))
                        act.activation(mT[:, :], misc[0:32, 0:128].bitcast(F16),
                                       ACT.Copy).then_inc(mT_ready, 1)
                    if cur:
                        rotary_hi(0)
                        wait(act, proj_done, UNITS * (k + 1))
                        wait(act, content_out, 32 * k)
                        act.activation(ch[:, :], proj[:, (UNITS - 1) % 2, :],
                                       ACT.Copy).then_inc(content_hi, 1)
                    if prev:
                        exps(0)
                        exps(1)
                    if cur:
                        rotary_hi(1)
                    if prev:
                        for u in range(2, 8):
                            exps(u)
                    if cur:
                        wait(act, v_ps, k + 1)
                        wait(act, pv_done, 4 * (k - 1))
                        for i in range(2):
                            for g in range(GROUPS):
                                at = 128 * g
                                ins = act.activation(
                                    vp[:, par, i, at:at + 160].rearrange(
                                        "p (m a) -> p m a", a=40)[:, :, 0:HD],
                                    misc[:, 128 * i + 32 * g:128 * i + 32 * g + 32]
                                    .rearrange("p (m d) -> p m d", m=PER), ACT.Copy)
                        ins.then_inc(v_ready, 1)
                    if nxt:
                        wait(act, xT_ps, k + 2)
                        wait(act, xTl_ready, k + 1)
                        wait(act, lat_ps, k + 1)
                        act.activation(xT[:, :], misc[:, 0:T], ACT.Copy)
                        wait(act, proj_done, UNITS * (k + 1))
                        act.activation(xTh[:, :], misc[:, 0:T], ACT.Copy).then_inc(xT_ready, 1)
                        wait(act, lT_ps, k + 2)
                        act.activation(lT[:, :, :].rearrange("p a t -> p (a t)"), misc[:, :],
                                       ACT.Copy).then_inc(lT_ready, 1)
                    if prev:
                        wait(act, xT2_ps, k)
                        wait(act, xT2_done, k - 1)
                        act.activation(xT2[:, :], misc[:, 0:T], ACT.Copy)
                        act.activation(xT2h[:, bass.ds(T * (k - 1), T)], misc[:, 0:T],
                                       ACT.Copy).then_inc(xT2_read, 1)
                steps(act, step)

            @block.vector
            def _(dve):
                setup = Chain(dve, c_set)
                ln1, lats = Chain(dve, c_ln1), Chain(dve, c_lat)
                maxs, ln2, norm = Chain(dve, c_max), Chain(dve, c_ln2), Chain(dve, c_norm)
                dve.wait_ge(loaded, 16 * LOADS)
                setup.link(dve.tensor_scalar(cgain[:, :, :], craw[:, 1:3, :], gain[:, 0:1], None,
                                             ALU.mult))
                setup.link(dve.tensor_copy(cgain_hi[:, :, :], cgain[:, :, :]))
                dve.tensor_copy(wkcv[0:64, :, :], cgain[0:64, :, :])
                dve.tensor_tensor(wkcv[64:128, :, :], cgain[64:128, :, :],
                                  cgain_hi[64:128, :, :].bitcast(F32), ALU.subtract)
                dve.wait_ge(cast, 7)
                for lo, raw, hi in ((wkl, wraw[:, 0, :], wkh), (wql, wraw[:, 1, :], wqh),
                                    (wqcl, craw[:, 0, :], wqch)):
                    ins = dve.tensor_tensor(lo[:, :], raw, hi[:, :].bitcast(F32), ALU.subtract)
                ins.then_inc(weights_ready, 1)

                def step(pair, par, prev, cur, nxt):
                    k = 2 * pair + par

                    def maxima(u):
                        wait(dve, rows_done, 8 * k + u + 1)
                        b, h = 2 * (u % 2), unit_heads(u)
                        at = slice(h[0], h[1] + 1, h[1] - h[0])
                        dve.tensor_reduce(mx[:, 0, at], score[:, b:b + 2, 0:128], AX.X, ALU.max)
                        dve.tensor_reduce(mx[:, 1, at], score[:, b:b + 2, 128:384], AX.X,
                                          ALU.max).then_inc(max_read, 1)
                    if cur:
                        for n in range(UNITS - 1):
                            side, c = n // 4, n % 4
                            wait(dve, proj_done, UNITS * k + n + 1)
                            if c == 0:
                                wait(dve, rope_sum, 2 * (k - 1) + side + 1)
                            dve.tensor_tensor(prod[:, side, c], proj[:, n % 2, :]
                                              .rearrange("p (a t) -> p a t", a=2), rope[:, :, :],
                                              ALU.mult).then_inc(proj_read, 1)
                        wait(dve, content_hi, k + 1)
                        wait(dve, content_out, 32 * k)
                        dve.tensor_tensor(cl[:, :], proj[:, (UNITS - 1) % 2, :], ch[:, :],
                                          ALU.subtract).then_inc(proj_read, 1)
                    if nxt:
                        ln1.start(k + 1)
                        wait(dve, x_in[1 - par], 16 * (pair + 1 + par))
                        wait(dve, xT_ps, k + 1)
                        wait(dve, xn_ready, k + 1)
                        layernorm(dve, passed_dve, ln1.link, xt[:, 1 - par], stats, moments, var, rstd,
                                  var_ready, rstd_ready, k + 2, xn).then_inc(xn_ready, 1)
                    if prev:
                        norm.start(k - 1)
                        wait(dve, pv_done, 4 * k)
                        wait(dve, y_ps, k - 1)
                        norm.link(dve.reciprocal(rden[:, :], acc[:, T:2 * T]))
                        dve.tensor_tensor(outT[:, :], acc[:, 0:T], rden[:, :],
                                          ALU.mult).then_inc(out_ready, 1)
                    if cur:
                        maxima(0)
                    if prev:
                        wait(dve, y_ps, k)
                        wait(dve, xr_in, 16 * k)
                        wait(dve, kept, 32 * (k - 1))
                        dve.tensor_tensor(x2s[:, :, :], misc[:, 0:2 * D]
                                          .rearrange("p (i d) -> p i d", i=2), xr[:, :, :],
                                          ALU.add).then_inc(x2_ready, 1)
                    if cur:
                        maxima(1)
                    if prev:
                        ln2.start(k - 1)
                        wait(dve, x2_ready, k)
                        wait(dve, xT2_ps, k - 1)
                        layernorm(dve, passed_dve, ln2.link, x2s, stats2, moments2, var2, rstd2,
                                  var2_ready, rstd2_ready, k, xn2s).then_inc(xn2_ready, 1)
                    if nxt:
                        wait(dve, xT_ready, k + 2)
                        dve.tensor_tensor(xTl[:, :], xT[:, :], xTh[:, :].bitcast(F32),
                                          ALU.subtract).then_inc(xTl_ready, 1)
                    if cur:
                        maxima(2)
                        maxima(3)
                    if nxt:
                        lats.start(k + 1)
                        link = lats.link
                        wait(dve, lat_ps, k + 2)
                        wait(dve, lT_ps, k + 1)
                        dve.tensor_copy(lat[:, :, :].rearrange("p i c -> p (i c)"),
                                        misc[:, 0:2 * (QR + KVR)]).then_inc(lat_read, 1)
                        wait(dve, lat_read, k + 2)
                        q, kv = lat[:, :, 0:QR], lat[:, :, QR:QR + KVR]
                        dve.tensor_copy(lst[:, :, 0:QR], q)
                        link(dve.tensor_tensor(sq[:, :, :], kv, kv, ALU.mult))
                        link(dve.tensor_reduce(ssum[:, :], sq[:, :, :], AX.X, ALU.add))
                        dve.tensor_tensor(lst[:, :, QR:2 * QR], q, lst[:, :, 0:QR].bitcast(F32),
                                          ALU.subtract)
                        dve.tensor_scalar(mkv[:, :], ssum[:, :], 1.0 / KVR, RMS_EPS,
                                          ALU.mult, ALU.add).then_inc(mkv_ready, 1)
                        wait(dve, rkv_ready, k + 2)
                        link(dve.tensor_tensor(kvn[:, :, :], kv, rkv[:, :].unsqueeze(2)
                                               .broadcast_to([128, 2, KVR]), ALU.mult))
                        parts = lst[:, :, 2 * QR:].rearrange("p i (r a c) -> p i r a c", r=2, a=2)
                        for r in range(2):
                            ins = dve.tensor_copy(parts[:, :, r, 0], kvn[:, :, :])
                        link(ins)
                        for r in range(2):
                            ins = dve.tensor_tensor(parts[:, :, r, 1], kvn[:, :, :],
                                                    parts[:, :, r, 0].bitcast(F32), ALU.subtract)
                        ins.then_inc(lst_ready, 1)
                    if cur:
                        for u in range(4, 8):
                            maxima(u)
                        maxs.start(k)
                        wait(dve, max_read, 8 * (k + 1))
                        wait(dve, mT_ps, k)
                        maxs.link(dve.tensor_copy(mp[:, :, 0, :], mx[:, :, :]))
                        dve.tensor_tensor(mp[:, :, 1, :], mx[:, :, :], mp[:, :, 0, :],
                                          ALU.subtract).then_inc(mp_ready, 1)
                    if prev:
                        wait(dve, xT2_read, k)
                        at = bass.ds(T * (k - 1), T)
                        dve.tensor_tensor(xT2l[:, at], xT2[:, :], xT2h[:, at].bitcast(F32),
                                          ALU.subtract).then_inc(xT2_done, 1)
                steps(dve, step)

            @block.tensor
            def _(pe):
                pe.wait_ge(loaded, 16 * LOADS)
                pe.wait_ge(zeroed, 7)
                pe.wait_ge(cast, 7)
                pe.wait_ge(weights_ready, 1)

                def step(pair, par, prev, cur, nxt):
                    k = 2 * pair + par

                    def project(n):
                        wait(pe, proj_read, UNITS * k + max(n - 1, 0))
                        bank = proj[:, n % 2, :]
                        xh, xl = xTh[:, :], xTl[:, :]
                        q = lT[:, 0:2, :].rearrange("p a t -> p (a t)")
                        kv = lT[:, 2:4, :].rearrange("p a t -> p (a t)")
                        for a in range(2):
                            if n < 4:
                                w = slice(256 * n + 128 * a, 256 * n + 128 * a + 128)
                                passes = ((wkh[:, w], xh), (wkh[:, w], xl), (wkl[:, w], xh))
                            elif n < 8:
                                w = slice(256 * (n - 4) + 128 * a, 256 * (n - 4) + 128 * a + 128)
                                passes = ((wqh[:, w], q), (wql[:, w], q))
                            elif a == 0:
                                passes = ((wqch[:, :], q), (wqcl[:, :], q))
                            else:
                                passes = ((wkcv[:, 0, :], kv),)
                            for i, (w, m) in enumerate(passes):
                                ins = pe.matmul(bank[:, T * a:T * a + T], w, m, start=(i == 0),
                                                stop=(i == len(passes) - 1))
                        ins.then_inc(proj_done, 1)

                    def keys_by_queries(u):
                        if u < 2:
                            wait(pe, max_read, 8 * k - 1 + u)
                        else:
                            wait(pe, exp_done, 8 * (k - 1) + u - 1)
                        for e, h in enumerate(unit_heads(u)):
                            bank = score[:, 2 * (u % 2) + e, :]
                            for i, j in ((0, 0), (0, 1), (1, 1)):
                                at = 128 * PLACES[e][i, j]
                                ins = pe.matmul(bank[:, at:at + 128],
                                                ks[1 - par][:, h, 128 * i:128 * i + 128],
                                                qs[1 - par][:, h, 128 * j:128 * j + 128],
                                                start=True, stop=True)
                        ins.then_inc(st_done, 1)

                    def queries_by_keys(u):
                        if u < 2:
                            wait(pe, exp_done, 8 * k - 1 + u)
                        else:
                            wait(pe, max_read, 8 * k + u - 1)
                        for e, h in enumerate(unit_heads(u)):
                            bank = score[:, 2 * (u % 2) + e, :]
                            pe.matmul(bank[:, 0:256], identb[:, :],
                                      mask[:, :, :].rearrange("p a t -> p (a t)"), start=True,
                                      stop=False, skip_group_check=True)
                            for i, j, at in ((0, 0, 0), (1, 1, 128), (1, 0, 256)):
                                ins = pe.matmul(bank[:, at:at + 128],
                                                qs[par][0:120, h, 128 * i:128 * i + 128],
                                                ks[par][0:120, h, 128 * j:128 * j + 128],
                                                start=False, stop=True, skip_group_check=True)
                        ins.then_inc(rows_done, 1)

                    def weigh(g):
                        wait(pe, masked, 8 * (k - 1) + 2 * g + 2)
                        for i, q in ((0, 0), (0, 1), (1, 1)):
                            for den in range(2):
                                for j in range(GROUPS):
                                    h = PER * j + g
                                    w = ones[:, g, :] if den else \
                                        vp[:, 1 - par, i, 32 * h:32 * h + 32]
                                    at = 128 * PLACES[j % 2][i, q]
                                    to = T * den + 128 * q
                                    ins = pe.matmul(
                                        acc[32 * j:32 * j + 32, to:to + 128], w,
                                        pt[:, g % 2, j, at:at + 128],
                                        start=(g == 0 and i == q == den == 0),
                                        stop=(g == 3 and i == q), skip_group_check=True)
                        ins.then_inc(pv_done, 1)

                    if cur:
                        wait(pe, xTl_ready, k + 1)
                        wait(pe, lT_ready, k + 1)
                        project(0)
                        project(1)
                    if prev:
                        wait(pe, mp_ready, k)
                        wait(pe, xT2_read, k - 1)
                        for i in range(2):
                            ins = pe.transpose(misc[0:32, 64 * i:64 * i + 64].bitcast(F16),
                                               mp[:, i].rearrange("p a h -> p (a h)"),
                                               ident16[:, :])
                        ins.then_inc(mT_ps, 1)
                    if cur:
                        for n in range(2, UNITS):
                            project(n)
                    if prev:
                        wait(pe, m_in, 16 * k)
                        for u in range(4):
                            keys_by_queries(u)
                        wait(pe, v_ready, k)
                        wait(pe, out_ready, k - 1)
                        weigh(0)
                        for g in range(1, 3):
                            keys_by_queries(2 * g + 2)
                            keys_by_queries(2 * g + 3)
                            weigh(g)
                        weigh(3)
                    if cur:
                        wait(pe, stack_in[par], STACKED * (pair + 1))
                        queries_by_keys(0)
                    if prev:
                        wait(pe, out_ready, k)
                        wait(pe, mT_ready, k)
                        for i in range(2):
                            ins = pe.matmul(misc[:, 128 * i:128 * i + 128],
                                            outT[:, 128 * i:128 * i + 128], wo[:, :],
                                            start=True, stop=True)
                        ins.then_inc(y_ps, 1)
                    if cur:
                        queries_by_keys(1)
                        wait(pe, x2_ready, k)
                        for i in range(2):
                            ins = pe.matmul(misc[:, 128 * i:128 * i + 128], lT[:, 2 + i, :],
                                            wkcv[:, 1, :], start=True, stop=True)
                        ins.then_inc(v_ps, 1)
                    if nxt:
                        wait(pe, xn_ready, k + 2)
                        wait(pe, v_ready, k + 1)
                        for i in range(2):
                            ins = pe.transpose(misc[:, 128 * i:128 * i + 128], xn[:, i, :],
                                               ident[:, :])
                        ins.then_inc(xT_ps, 1)
                    if cur:
                        queries_by_keys(2)
                    if nxt:
                        wait(pe, xT_ready, k + 2)
                        wait(pe, lat_read, k + 1)
                        for i in range(2):
                            ins = pe.matmul(misc[:, 96 * i:96 * i + 96],
                                            xT[:, 128 * i:128 * i + 128], wqkv[:, :],
                                            start=True, stop=True)
                        ins.then_inc(lat_ps, 1)
                    if cur:
                        for u in range(3, 6):
                            queries_by_keys(u)
                    if nxt:
                        wait(pe, lst_ready, k + 2)
                        for a in range(2):
                            for i in range(2):
                                ins = pe.transpose(
                                    misc[:, 256 * a + 128 * i:256 * a + 128 * i + 128],
                                    lst[:, i, 128 * a:128 * a + 128].bitcast(F32), ident[:, :])
                        ins.then_inc(lT_ps, 1)
                    if cur:
                        for u in range(6, 8):
                            queries_by_keys(u)
                    if prev:
                        wait(pe, xn2_ready, k)
                        if nxt:
                            wait(pe, lT_ready, k + 2)
                        elif cur:
                            wait(pe, v_ready, k + 1)
                        for i in range(2):
                            ins = pe.transpose(misc[:, 128 * i:128 * i + 128], xn2s[:, i, :],
                                               ident[:, :])
                        ins.then_inc(xT2_ps, 1)
                steps(pe, step)
                pe.wait_ge(xT2_done, BATCH)


def dispatch(nc, phi_t, phi_b, exp_w, exp_b, c_dshift, c_expert, xn2, xT2h, xT2l, ident, phT_h,
             phT_l, mcT, yt):
    with ExitStack() as stack:
        def sb(name, shape, dt=F32):
            return stack.enter_context(nc.sbuf_tensor(name, shape, dt))

        def pb(name, shape, dt=F32):
            return stack.enter_context(nc.psum_tensor(name, shape, dt))

        def sem(name):
            return stack.enter_context(nc.semaphore(name))

        ew = sb("ew", [128, EXPERTS, D])
        eb = sb("eb", [EXPERTS, D])
        e_rows = sb("e_rows", [EXPERTS, NCH, 128])
        xth = [sb(f"xth{i}", [128, 128], F32R) for i in range(4)]
        xtl = [sb(f"xtl{i}", [128, 128], F32R) for i in range(4)]
        xd = [sb(f"xd{i}", [128, D]) for i in range(4)]
        raw = sb("raw", [128, HALF])
        bias = sb("bias", [128, NS], BF16)
        bres = sb("bres", [96, NS])
        ones_b = sb("ones_b", [128, 128], BF16)
        shift = sb("shift", [3 * HALF_E, HALF], BF16)
        identb = sb("identb_d", [128, 128], BF16)
        md = sb("md", [128, HALF_E])
        res = sb("res_d", [128, HALF_E])
        mdp = sb("mdp", [128, 3, HALF_E], BF16)
        mdT = sb("mdT", [3 * HALF_E, 2, 128], BF16)
        mc = sb("mc", [128, TILES, SLOTS])
        mc2, mcm, resc = sb("mc2", [128, SLOTS]), sb("mcm", [128, SLOTS]), sb("resc", [128, SLOTS])
        mcp = sb("mcp", [128, 3, SLOTS], BF16)
        e = sb("e", [128, 2, HALF])
        den, rden = sb("den_d", [128, HALF_E]), sb("rden_d", [128, 2, HALF_E])
        xs = sb("xs", [128, NS])
        th = sb("th", [128, 2, 4, D])
        thT = sb("thT", [128, 2, 4, 128])
        st, mo = sb("st_d", [128, 4, 6]), sb("mo_d", [128, 4, 2])
        sv, power = sb("sv_d", [128, 2, 4]), sb("power_d", [128, 4])
        sr, nb = sb("sr_d", [128, 2, 4]), sb("nb_d", [128, 2, 4])

        lg = pb("lg", [128, 2, HALF])
        xacc = pb("xacc", [128, HALF])
        tp = pb("tp", [128, 2, 512])

        loaded, ew_in, filled, cast, setup_done = (sem("d_loaded"), sem("ew_in"), sem("d_filled"),
                                                   sem("d_cast"), sem("d_setup"))
        d_in = [sem(f"d_in{i}") for i in range(4)]
        lg_done, md_ready, mc_read, md_ps, mdT_ready = (sem("lg_done"), sem("md_ready"),
                                                        sem("mc_read"), sem("md_ps"),
                                                        sem("mdT_ready"))
        mcp_ready, mc_ps, mcT_ready = sem("mcp_ready"), sem("mc_ps"), sem("mcT_ready")
        shifted, exp_done, den_ready, scaled, summed = (sem("shifted"), sem("d_exp"),
                                                        sem("den_ready"), sem("scaled"),
                                                        sem("summed"))
        xs_ready = sem("xs_ready")
        c_set, c_md, c_mc, c_den, c_ex = (sem("d_chain_setup"), sem("d_chain_md"),
                                          sem("d_chain_mc"), sem("d_chain_den"),
                                          sem("d_chain_ex"))
        sv_ready, sr_ready = sem("sv_ready"), sem("sr_ready")
        x_ps, sx_ready, th_ready, th_ps, thT_ready, y_ps, y_ready = (
            sem("x_ps"), sem("sx_ready"), sem("th_ready"), sem("th_ps"), sem("thT_ready"),
            sem("d_y_ps"), sem("d_y_ready"))

        def steps(eng, step):
            for half in range(2):
                for r in range(4):
                    step(half, 0, r, True, r >= 1, r >= 2)
                with eng.Fori(1, TILES // 4) as quad:
                    for r in range(4):
                        step(half, quad, r, True, True, True)
                step(half, TILES // 4, 0, False, True, True)
                step(half, TILES // 4, 1, False, False, True)

        with nc.Block() as block:
            @block.sync
            def _(sp):
                sp.dma_start(raw[0:96, :], c_dshift).then_inc(loaded, 16)
                for i in range(3):
                    sp.dma_start(bres[32 * i:32 * i + 1, :],
                                 phi_b.rearrange("(a n) -> a n", a=1)).then_inc(loaded, 16)
                sp.dma_start(xs[:, :], phi_t).then_inc(loaded, 16)
                sp.dma_start(eb[:, :], exp_b).then_inc(ew_in, 16)
                sp.dma_start(e_rows[:, :, :], c_expert).then_inc(ew_in, 16)

                def step(half, quad, r, make, shifts, use):
                    t = 4 * quad + r
                    u = TILES * half + t
                    if make:
                        wait(sp, summed, u - 3)
                        turn = 8 * half + quad
                        at = bass.ds(128 * t, 128)
                        for dst, src in ((xth[r][:, :].bitcast(F32), xT2h[:, at].bitcast(F32)),
                                         (xtl[r][:, :].bitcast(F32), xT2l[:, at].bitcast(F32)),
                                         (xd[r][:, :], xn2[:, bass.ds(t, 1), :]
                                          .rearrange("p a d -> p (a d)"))):
                            sp.dma_start(dst, src).then_inc(d_in[r], 16)
                        if half == 0 and isinstance(quad, int) and r == 3:
                            sp.dma_start(ew[:, :, :], exp_w.rearrange("n d h -> d n h")
                                         ).then_inc(ew_in, 16)
                steps(sp, step)

            @block.gpsimd
            def _(pool):
                for n, (place, value) in enumerate(((bias[:, :], 0.0), (ones_b[:, :], 1.0),
                                                    (power[:, :], -0.5))):
                    pool.memset(place, value).then_inc(filled, 1)
                    pool.wait_ge(filled, n + 1)

                def step(half, quad, r, make, shifts, use):
                    t = 4 * quad + r
                    if shifts:
                        u = TILES * half + t - 1
                        b = (r - 1) % 2
                        wait(pool, den_ready, u + 1)
                        w = e[:, b, :].rearrange("p (n s) -> p n s", s=SLOTS)
                        pool.tensor_tensor(w, w, rden[:, b, :].unsqueeze(2)
                                           .broadcast_to([128, HALF_E, SLOTS]),
                                           ALU.mult).then_inc(scaled, 1)
                steps(pool, step)
                for g in range(4):
                    pool.wait_ge(sv_ready, g + 1)
                    pool.tensor_tensor(sr[:, g % 2, :], sv[:, g % 2, :], power[:, :],
                                       ALU.pow).then_inc(sr_ready, 1)

            @block.scalar
            def _(act):
                act.wait_ge(loaded, 80)
                act.activation(phT_h[:, :], xs[:, :], ACT.Copy).then_inc(cast, 1)
                act.activation(shift[:, :], raw[0:96, :], ACT.Copy).then_inc(cast, 1)
                act.activation(identb[:, :], ident[:, :], ACT.Copy).then_inc(cast, 1)

                def step(half, quad, r, make, shifts, use):
                    t = 4 * quad + r
                    if shifts:
                        u = TILES * half + t - 1
                        b = (r - 1) % 2
                        wait(act, md_ps, u + 1)
                        wait(act, shifted, u - 1)
                        act.activation(mdT[:, b, :], tp[0:96, 0, 0:64].bitcast(BF16),
                                       ACT.Copy).then_inc(mdT_ready, 1)
                        if half == 1:
                            at = bass.ds(128 * (t - 1), 128)
                            wait(act, mc_ps, t)
                            act.activation(mcT[:, at], tp[0:96, 1, 0:64].bitcast(BF16),
                                           ACT.Copy).then_inc(mcT_ready, 1)
                        wait(act, shifted, u + 1)
                        wait(act, summed, u - 1)
                        act.activation(e[:, b, :], lg[:, b, :], ACT.Exp).then_inc(exp_done, 1)
                steps(act, step)
                for g in range(4):
                    act.wait_ge(sx_ready, g + 1)
                    wait(act, th_ps, g - 1)
                    for i in range(4):
                        ins = act.activation(th[:, g % 2, i, :],
                                             lg[:, 0, 512 * (g % 2) + 128 * i:
                                                512 * (g % 2) + 128 * i + 128], ACT.Tanh,
                                             bias=nb[:, g % 2, i:i + 1],
                                             scale=sr[:, g % 2, i:i + 1])
                    ins.then_inc(th_ready, 1)
                    act.wait_ge(th_ps, g + 1)
                    wait(act, y_ps, g - 1)
                    act.activation(thT[:, g % 2].rearrange("p i t -> p (i t)"),
                                   lg[:, 1, 512 * (g % 2):512 * (g % 2) + 512],
                                   ACT.Copy).then_inc(thT_ready, 1)

            @block.vector
            def _(dve):
                setup, cmd, cmc = Chain(dve, c_set), Chain(dve, c_md), Chain(dve, c_mc)
                cden, cex = Chain(dve, c_den), Chain(dve, c_ex)
                dve.wait_ge(loaded, 80)
                dve.wait_ge(cast, 3)
                dve.wait_ge(filled, 3)
                dve.tensor_tensor(phT_l[:, :], xs[:, :], phT_h[:, :].bitcast(F32), ALU.subtract)
                for i in range(3):
                    row = slice(32 * i, 32 * i + 1)
                    for _n in range(i):
                        setup.link(dve.tensor_copy(bias[row, :], bres[row, :]))
                        setup.link(dve.tensor_tensor(bres[row, :], bres[row, :], bias[row, :],
                                                     ALU.subtract))
                    dve.tensor_copy(bias[row, :], bres[row, :]).then_inc(setup_done, 1)

                def split(link, m, parts, rest):
                    link(dve.tensor_copy(parts[:, 0, :], m))
                    link(dve.tensor_tensor(rest[:, :], m, parts[:, 0, :], ALU.subtract))
                    link(dve.tensor_copy(parts[:, 1, :], rest[:, :]))
                    return dve.tensor_tensor(parts[:, 2, :], rest[:, :], parts[:, 1, :],
                                             ALU.subtract)

                def step(half, quad, r, make, shifts, use):
                    t = 4 * quad + r
                    u = TILES * half + t
                    if make:
                        b = r % 2
                        by_slot = lg[:, b, :].rearrange("p (n s) -> p n s", s=SLOTS)
                        cmd.start(u)
                        wait(dve, lg_done, u + 1)
                        wait(dve, md_ps, u)
                        wait(dve, md_ready, u)
                        cmd.link(dve.tensor_reduce(md[:, :], by_slot, AX.X, ALU.max))
                        split(cmd.link, md[:, :], mdp, res).then_inc(md_ready, 1)
                        by_expert = lg[:, b, :].rearrange("p (n s) -> p s n", s=SLOTS)
                        if half == 0:
                            dve.tensor_reduce(mc[:, bass.ds(t, 1), :]
                                              .rearrange("p a s -> p (a s)"), by_expert, AX.X,
                                              ALU.max).then_inc(mc_read, 1)
                        else:
                            cmc.start(t)
                            dve.tensor_reduce(mc2[:, :], by_expert, AX.X,
                                              ALU.max).then_inc(mc_read, 1)
                            wait(dve, mc_read, u + 1)
                            wait(dve, mc_ps, t)
                            wait(dve, mcp_ready, t)
                            cmc.link(dve.tensor_tensor(
                                mcm[:, :], mc2[:, :], mc[:, bass.ds(t, 1), :]
                                .rearrange("p a s -> p (a s)"), ALU.max))
                            split(cmc.link, mcm[:, :], mcp, resc).then_inc(mcp_ready, 1)
                    if shifts:
                        u = TILES * half + t - 1
                        b = (r - 1) % 2
                        cden.start(u)
                        wait(dve, exp_done, u + 1)
                        wait(dve, scaled, u - 1)
                        wait(dve, den_ready, u)
                        cden.link(dve.tensor_reduce(
                            den[:, :], e[:, b, :].rearrange("p (n s) -> p n s", s=SLOTS), AX.X,
                            ALU.add))
                        dve.reciprocal(rden[:, b, :], den[:, :]).then_inc(den_ready, 1)
                    if use and not make and not shifts:
                        dve.wait_ge(summed, TILES * (half + 1))
                        dve.tensor_scalar(xs[:, HALF * half:HALF * half + HALF], xacc[:, :],
                                          CLIP_LOW, CLIP_HIGH, ALU.max,
                                          ALU.min).then_inc(xs_ready, 1)
                steps(dve, step)
                for g in range(4):
                    dve.wait_ge(x_ps, g + 1)
                    wait(dve, th_ready, g - 1)
                    src = lg[:, 0, 512 * (g % 2):512 * (g % 2) + 512]
                    for i in range(4):
                        ins = dve.bn_stats(st[:, i, :], src[:, 128 * i:128 * i + 128])
                    cex.link(ins)
                    for i in range(4):
                        ins = dve.bn_aggr(mo[:, i, :], st[:, i, :])
                    cex.link(ins)
                    dve.tensor_scalar(sv[:, g % 2, :], mo[:, :, 1], LN_EPS, None,
                                      ALU.add).then_inc(sv_ready, 1)
                    dve.wait_ge(sr_ready, g + 1)
                    dve.scalar_tensor_tensor(nb[:, g % 2, :], mo[:, :, 0], -1.0, sr[:, g % 2, :],
                                             ALU.mult, ALU.mult).then_inc(sx_ready, 1)
                    if g >= 1:
                        dve.wait_ge(y_ps, g)
                        dve.tensor_copy(yt[:, 4 * g - 4:4 * g, :].rearrange("p i h -> p (i h)"),
                                        xacc[:, 512 * ((g - 1) % 2):512 * ((g - 1) % 2) + 512]
                                        ).then_inc(y_ready, 1)
                dve.wait_ge(y_ps, 4)
                dve.tensor_copy(yt[:, 12:16, :].rearrange("p i h -> p (i h)"),
                                xacc[:, 512:1024]).then_inc(y_ready, 1)

            @block.tensor
            def _(pe):
                pe.wait_ge(cast, 3)
                pe.wait_ge(filled, 3)
                pe.wait_ge(setup_done, 3)

                def step(half, quad, r, make, shifts, use):
                    t = 4 * quad + r
                    u = TILES * half + t
                    if shifts:
                        b = (r - 1) % 2
                        wait(pe, md_ready, u)
                        wait(pe, mdT_ready, u - 1)
                        ins = pe.transpose(tp[0:96, 0, 0:64].bitcast(BF16),
                                           mdp[:, :, :].rearrange("p a n -> p (a n)"),
                                           identb[:, :])
                        ins.then_inc(md_ps, 1)
                        if half == 1:
                            wait(pe, mcp_ready, t)
                            wait(pe, mcT_ready, t - 1)
                            pe.transpose(tp[0:96, 1, 0:64].bitcast(BF16),
                                         mcp[:, :, :].rearrange("p a n -> p (a n)"),
                                         identb[:, :]).then_inc(mc_ps, 1)
                    if make:
                        b = r % 2
                        wait(pe, d_in[r], 48 * (8 * half + quad + 1))
                        wait(pe, exp_done, u - 1)
                        for j in range(2):
                            w = slice(HALF * half + 512 * j, HALF * half + 512 * j + 512)
                            bank = lg[:, b, 512 * j:512 * j + 512]
                            pe.matmul(bank, ones_b[:, :], bias[:, w], start=True, stop=False)
                            pe.matmul(bank, xth[r][:, :], phT_h[:, w], start=False, stop=False)
                            pe.matmul(bank, xth[r][:, :], phT_l[:, w], start=False, stop=False)
                            ins = pe.matmul(bank, xtl[r][:, :], phT_h[:, w], start=False,
                                            stop=True)
                        ins.then_inc(lg_done, 1)
                    if shifts:
                        b = (r - 1) % 2
                        wait(pe, mdT_ready, u)
                        wait(pe, mc_read, u)
                        for j in range(2):
                            ins = pe.matmul(lg[:, b, 512 * j:512 * j + 512], mdT[:, b, :],
                                            shift[:, 512 * j:512 * j + 512], start=False,
                                            stop=True, skip_group_check=True)
                        ins.then_inc(shifted, 1)
                    if use:
                        x_r = (r - 2) % 4
                        first = isinstance(quad, int) and quad == 0 and r == 2
                        last = not make and not shifts
                        wait(pe, scaled, u - 1)
                        if first:
                            wait(pe, xs_ready, half)
                        for j in range(2):
                            ins = pe.matmul(xacc[:, 512 * j:512 * j + 512], xd[x_r][:, :],
                                            e[:, r % 2, 512 * j:512 * j + 512], start=first,
                                            stop=last, skip_group_check=True)
                        ins.then_inc(summed, 1)
                steps(pe, step)
                pe.wait_ge(xs_ready, 2)
                pe.wait_ge(exp_done, 2 * TILES)
                pe.wait_ge(ew_in, 48)

                def slots(g):
                    wait(pe, th_ready, g - 1)
                    for i in range(4):
                        c = 4 * g + i
                        ins = pe.transpose(lg[:, 0, 512 * (g % 2) + 128 * i:
                                              512 * (g % 2) + 128 * i + 128],
                                           xs[:, 128 * c:128 * c + 128], ident[:, :])
                    ins.then_inc(x_ps, 1)
                slots(0)
                for g in range(4):
                    if g < 3:
                        slots(g + 1)
                    pe.wait_ge(th_ready, g + 1)
                    wait(pe, thT_ready, g - 1)
                    for i in range(4):
                        ins = pe.transpose(lg[:, 1, 512 * (g % 2) + 128 * i:
                                              512 * (g % 2) + 128 * i + 128],
                                           th[:, g % 2, i, :], ident[:, :])
                    ins.then_inc(th_ps, 1)
                    pe.wait_ge(thT_ready, g + 1)
                    wait(pe, y_ready, g - 1)
                    for i in range(4):
                        c = 4 * g + i
                        at = slice(512 * (g % 2) + 128 * i, 512 * (g % 2) + 128 * i + 128)
                        pe.matmul(xacc[:, at], e_rows[:, c, :], eb[:, :], start=True, stop=False,
                                  skip_group_check=True)
                        for n in range(4):
                            ins = pe.matmul(xacc[32 * n:32 * n + 32, at],
                                            thT[:, g % 2, i, 32 * n:32 * n + 32],
                                            ew[:, 4 * c + n, :], start=False, stop=True,
                                            skip_group_check=True)
                    ins.then_inc(y_ps, 1)
                pe.wait_ge(y_ready, 4)
                pe.wait_ge(mcT_ready, TILES)


def combine(nc, phi_b, c_cshift, c_same, x2, xT2h, xT2l, ident, phT_h, phT_l, mcT, yt, out):
    with ExitStack() as stack:
        def sb(name, shape, dt=F32):
            return stack.enter_context(nc.sbuf_tensor(name, shape, dt))

        def pb(name, shape, dt=F32):
            return stack.enter_context(nc.psum_tensor(name, shape, dt))

        def sem(name):
            return stack.enter_context(nc.semaphore(name))

        sbias = sb("sbias", [128, NCH])
        rawc = sb("rawc", [3 * SLOTS, 128])
        shift = sb("shift_c", [3 * SLOTS, 128], BF16)
        same = sb("same", [128, 128])
        e = [sb(f"ec{i}", [128, NCH, CHUNK]) for i in range(2)]
        esum = sb("esum", [128, CHUNK])
        rden = sb("rden_c", [128, CHUNK])
        yT = sb("yT", [128, CHUNK])
        res = sb("res_c", [128, 2, 4, D])

        lg = pb("lg_c", [128, 4, CHUNK])
        dps = pb("dps", [128, CHUNK])
        yps = pb("yps", [128, CHUNK])
        tps = pb("tps", [128, CHUNK])

        loaded, cast = sem("c_loaded"), sem("c_cast")
        lg_done, exp_done, sum_ready, den_ps = (sem("c_lg"), sem("c_exp"), sem("c_sum"),
                                                sem("c_den"))
        scaled, y_ps, yT_ready, t_ps, res_ready = (sem("c_scaled"), sem("c_y"), sem("c_yT"),
                                                   sem("c_t"), sem("c_res"))
        stored = [sem("stored0"), sem("stored1")]
        c_add, c_rec = sem("c_chain_add"), sem("c_chain_rec")
        out_v = out.rearrange("b (i p) d -> p (b i) d", p=128)

        def steps(eng, step):
            step(0, 0, True, False, False)
            step(0, 1, True, True, False)
            with eng.Fori(1, STEPS // 2) as pair:
                step(pair, 0, True, True, True)
                step(pair, 1, True, True, True)
            step(STEPS // 2, 0, False, True, True)
            step(STEPS // 2, 1, False, False, True)

        with nc.Block() as block:
            @block.sync
            def _(sp):
                sp.dma_start(rawc[:, :], c_cshift).then_inc(loaded, 16)
                sp.dma_start(same[:, :], c_same).then_inc(loaded, 16)
                sp.dma_start(sbias[:, :], phi_b.rearrange("(c s) -> s c", s=128),
                             allow_slow_non_contiguous=True).then_inc(loaded, 16)

                def step(pair, par, make, use, end):
                    q = 2 * pair + par
                    if end:
                        wait(sp, res_ready, q - 1)
                        sp.dma_start(out_v[:, bass.ds(4 * (q - 2), 4), :],
                                     res[:, par]).then_inc(stored[par], 16)
                steps(sp, step)
                for i in range(2):
                    sp.wait_ge(stored[i], 16 * STEPS // 2)

            @block.scalar
            def _(act):
                act.wait_ge(loaded, 48)
                act.activation(shift[:, :], rawc[:, :], ACT.Copy).then_inc(cast, 1)

                def step(pair, par, make, use, end):
                    q = 2 * pair + par
                    if end:
                        wait(act, y_ps, q - 1)
                        wait(act, t_ps, q - 2)
                        act.activation(yT[:, :], yps[:, :], ACT.Copy).then_inc(yT_ready, 1)
                    if make:
                        wait(act, y_ps, q - 1)
                        for c in range(NCH):
                            wait(act, lg_done, NCH * q + c + 1)
                            act.activation(e[par][:, c, :], lg[:, c % 4, :], ACT.Exp,
                                           bias=sbias[:, c:c + 1]).then_inc(exp_done, 1)
                steps(act, step)

            @block.vector
            def _(dve):
                adds, recs = Chain(dve, c_add), Chain(dve, c_rec)

                def step(pair, par, make, use, end):
                    q = 2 * pair + par

                    def add(c):
                        wait(dve, exp_done, NCH * q + c + 1)
                        if c == 1:
                            wait(dve, den_ps, q)
                        first = e[par][:, 0, :] if c == 1 else esum[:, :]
                        ins = dve.tensor_tensor(esum[:, :], first, e[par][:, c, :], ALU.add)
                        if c == NCH - 1:
                            ins.then_inc(sum_ready, 1)
                        else:
                            adds.link(ins)

                    def scale(j):
                        w = e[1 - par][:, 4 * j:4 * j + 4, :]
                        dve.tensor_tensor(w, w, rden[:, :].unsqueeze(1)
                                          .broadcast_to([128, 4, CHUNK]),
                                          ALU.mult).then_inc(scaled, 1)
                    adds.start(q)
                    if make:
                        add(1)
                    if use:
                        recs.start(q - 1)
                        wait(dve, den_ps, q)
                        wait(dve, scaled, 4 * (q - 1))
                        recs.link(dve.reciprocal(rden[:, :], dps[:, :]))
                    for j in range(4):
                        if use:
                            scale(j)
                        if make:
                            for c in range(2 + 3 * j, min(5 + 3 * j, 14)):
                                add(c)
                        if j == 1 and end:
                            wait(dve, t_ps, q - 1)
                            wait(dve, stored[par], 16 * (pair - 1))
                            dve.tensor_tensor(res[:, par], tps[:, :]
                                              .rearrange("p (i d) -> p i d", i=4),
                                              x2[:, bass.ds(4 * (q - 2), 4), :],
                                              ALU.add).then_inc(res_ready, 1)
                    if make:
                        add(14)
                        add(15)
                steps(dve, step)

            @block.tensor
            def _(pe):
                pe.wait_ge(cast, 1)
                pe.wait_ge(loaded, 48)

                def step(pair, par, make, use, end):
                    q = 2 * pair + par
                    at = bass.ds(CHUNK * q, CHUNK)

                    def logits(c):
                        wait(pe, exp_done, NCH * q + c - 3)
                        bank = lg[:, c % 4, :]
                        w = slice(128 * c, 128 * c + 128)
                        pe.matmul(bank, shift[:, :], mcT[:, at], start=True, stop=False)
                        pe.matmul(bank, phT_h[:, w], xT2h[:, at], start=False, stop=False)
                        pe.matmul(bank, phT_h[:, w], xT2l[:, at], start=False, stop=False)
                        pe.matmul(bank, phT_l[:, w], xT2h[:, at], start=False,
                                  stop=True).then_inc(lg_done, 1)

                    if make:
                        logits(0)
                        logits(1)
                    if end:
                        wait(pe, yT_ready, q - 1)
                        wait(pe, res_ready, q - 2)
                        for i in range(4):
                            ins = pe.transpose(tps[:, 128 * i:128 * i + 128],
                                               yT[:, 128 * i:128 * i + 128], ident[:, :])
                        ins.then_inc(t_ps, 1)
                    if use:
                        wait(pe, sum_ready, q)
                        wait(pe, scaled, 4 * (q - 1))
                        pe.matmul(dps[:, :], same[:, :], esum[:, :], start=True,
                                  stop=True).then_inc(den_ps, 1)
                    if make:
                        for c in range(2, 6):
                            logits(c)
                    for j in range(4):
                        if use:
                            wait(pe, scaled, 4 * (q - 1) + j + 1)
                            if j == 0:
                                wait(pe, yT_ready, q - 1)
                            for c in range(4 * j, 4 * j + 4):
                                ins = pe.matmul(yps[:, :], yt[:, c, :], e[1 - par][:, c, :],
                                                start=(c == 0), stop=(c == NCH - 1))
                            if j == 3:
                                ins.then_inc(y_ps, 1)
                        if make:
                            for c in range(6 + 3 * j, min(9 + 3 * j, NCH)):
                                logits(c)
                steps(pe, step)
                pe.wait_ge(res_ready, STEPS)


def kernel(**inputs):
    import numpy as np
    import concourse.bacc as bacc
    from concourse.bass_utils import run_bass_kernel_spmd as run

    a = {n: np.asarray(v) for n, v in inputs.items()}

    def rotary_columns(w):
        r = w.reshape(w.shape[0], GROUPS, PER, 2, ROPE // 2).transpose(0, 2, 1, 3, 4)
        both = np.stack([r, r[:, :, :, ::-1, :]], axis=2)
        return np.ascontiguousarray(both.reshape(w.shape[0], 2 * HEADS * ROPE))

    inv = 1.0 / 10000.0 ** (np.arange(0, ROPE, 2, dtype=np.float32) / ROPE)
    angle = np.outer(np.arange(T, dtype=np.float32), inv)
    angle = np.concatenate([angle, angle], -1)
    sign = np.where(np.arange(ROPE) < ROPE // 2, -1.0, 1.0).astype(np.float32)
    rope = np.stack([np.cos(angle).T, np.sin(angle).T * sign[:, None]], 1)
    rope = np.tile(rope, (GROUPS, 1, 1)).astype(np.float32)
    rows, slot = np.arange(128), np.arange(NS)
    mask = np.where(rows[None, :] > rows[:, None], -1e30, 0.0).astype(np.float32)
    ones = np.zeros((128, PER, 32), np.float32)
    for m in range(PER):
        ones[:, m, HD * m:HD * m + HD] = 1.0
    same = (rows[:, None] % SLOTS == rows[None, :] % SLOTS).astype(np.float32)
    parts = np.arange(96) % 32
    dshift = -(parts[:, None] == slot[None, :HALF] // SLOTS).astype(np.float32)
    cshift = -(parts[:, None] == rows[None, :] % SLOTS).astype(np.float32)
    expert = (np.arange(EXPERTS)[:, None] == slot[None, :] // SLOTS).astype(np.float32)

    arrays = {
        "x": a["L0_attn_x"],
        "w_qkv": np.concatenate([a["L0_attn_W_q"], a["L0_attn_W_kv"]], axis=1),
        "w_k": rotary_columns(a["L0_attn_W_krope"]),
        "w_q": rotary_columns(a["L0_attn_W_qrope"]),
        "w_kcv": np.stack([a["L0_attn_W_kdec"], a["L0_attn_W_vdec"]], axis=1),
        "w_qc": a["L0_attn_W_qdec"],
        "g_kv": a["L0_attn_g_kv"].reshape(KVR, 1),
        "w_o": a["L0_attn_W_o"],
        "phi_t": a["L0_ffn_phi_w"].T,
        "phi_b": a["L0_ffn_phi_b"],
        "exp_w": a["L0_ffn_expert_w"],
        "exp_b": a["L0_ffn_expert_b"],
        "c_ident": np.eye(128, dtype=np.float32),
        "c_rope": rope, "c_mask": mask, "c_ones": ones, "c_same": same, "c_dshift": dshift,
        "c_cshift": cshift, "c_expert": expert.reshape(EXPERTS, NCH, 128),
    }
    arrays = {n: np.ascontiguousarray(v) for n, v in arrays.items()}
    nc = bacc.Bacc("TRN2", target_bir_lowering=False, num_devices=1)
    args = [nc.dram_tensor(f"in_{n}", v.shape, F32, kind="ExternalInput").ap()
            for n, v in arrays.items()]
    content_d = nc.dram_tensor("content_d", (2, 128, 2 * T), F16, kind="Internal").ap()
    max_d = nc.dram_tensor("max_d", (2 * HEADS, T), F16, kind="Internal").ap()
    out = nc.dram_tensor("out", (BATCH, T, D), F32, kind="ExternalOutput").ap()
    layer_kernel(nc, *args, content_d, max_d, out)
    r = run(nc, [{f"in_{n}": v for n, v in arrays.items()}], core_ids=[0])
    return r.results[0]["out"]
```

```python
import concourse.bass as bass
from concourse import mybir
from contextlib import ExitStack

F32 = mybir.dt.float32
F32R = mybir.dt.float32r
BF16 = mybir.dt.bfloat16
F16 = mybir.dt.float16
ALU = mybir.AluOpType
ACT = mybir.ActivationFunctionType
AX = mybir.AxisListType

BATCH, T, D = 16, 256, 128
HEADS, HD, ROPE = 16, 8, 32
QR, KVR = 64, 32
SCALE = float(HD + ROPE) ** -0.5
GROUPS, PER = 4, 4
EXPERTS, SLOTS = 64, 32
NS = EXPERTS * SLOTS
HALF, HALF_E = NS // 2, EXPERTS // 2
TILES = BATCH * T // 128
LN_EPS, RMS_EPS = 1e-5, 1e-6
CLIP_LOW, CLIP_HIGH = -33000.0, 65000.0
UNITS = 9
STACKED = 16 * 12
PLACES = [{(0, 1): 0, (0, 0): 1, (1, 1): 2}, {(0, 0): 0, (1, 1): 1, (0, 1): 2}]
CHUNK = 512
STEPS = BATCH * T // CHUNK
NCH = NS // 128


def wait(eng, sem, value):
    if isinstance(value, int) and value <= 0:
        return
    eng.wait_ge(sem, value)


class Chain:

    def __init__(self, eng, sem):
        self.eng, self.sem, self.per, self.n, self.base = eng, sem, None, 0, 0

    def start(self, turn):
        if self.per is None and self.n:
            self.per = self.n
        self.base, self.n = (turn * self.per if self.per else 0), 0

    def link(self, ins):
        self.n += 1
        ins.then_inc(self.sem, 1)
        self.eng.wait_ge(self.sem, self.base + self.n)


def settle(eng, passed):
    eng.sem_inc(passed, 1)


def layernorm(dve, passed, link, src, stats, moments, var, rstd, var_ready, rstd_ready, turn, dst):
    for i in range(2):
        ins = dve.bn_stats(stats[:, i, :], src[:, i, :])
    link(ins)
    settle(dve, passed)
    for i in range(2):
        ins = dve.bn_aggr(moments[:, i, :], stats[:, i, :])
    link(ins)
    dve.tensor_scalar(var[:, :], moments[:, :, 1], LN_EPS, None, ALU.add).then_inc(var_ready, 1)
    wait(dve, rstd_ready, turn)
    for i in range(2):
        ins = dve.tensor_scalar(dst[:, i, :], src[:, i, :], moments[:, i, 0:1], rstd[:, i:i + 1],
                                ALU.subtract, ALU.mult)
    return ins


def layer_kernel(nc, x, w_qkv, w_k, w_q, w_kcv, w_qc, g_kv, w_o, phi_t, phi_b, exp_w, exp_b,
                 c_ident, c_rope, c_mask, c_ones, c_same, c_dshift, c_cshift, c_expert,
                 content_d, rope_d, max_d, out):
    with ExitStack() as stack:
        def sb(name, shape, dt=F32):
            return stack.enter_context(nc.sbuf_tensor(name, shape, dt))
        x2 = sb("x2", [128, TILES, D])
        xn2 = sb("xn2", [128, TILES, D])
        xT2h = sb("xT2h", [128, TILES * 128], F32R)
        xT2l = sb("xT2l", [128, TILES * 128], F32R)
        ident = sb("ident", [128, 128])
        attention(nc, x, w_qkv, w_k, w_q, w_kcv, w_qc, g_kv, w_o, c_ident, c_rope, c_mask,
                  c_ones, content_d, rope_d, max_d, x2, xn2, xT2h, xT2l, ident)
        phT_h = sb("phT_h", [128, NS], F32R)
        phT_l = sb("phT_l", [128, NS], F32R)
        mcT = sb("mcT", [3 * SLOTS, TILES * 128], BF16)
        yt = sb("yt", [128, NCH, D])
        dispatch(nc, phi_t, phi_b, exp_w, exp_b, c_dshift, c_expert, xn2, xT2h, xT2l, ident,
                 phT_h, phT_l, mcT, yt)
        combine(nc, phi_b, c_cshift, c_same, x2, xT2h, xT2l, ident, phT_h, phT_l, mcT, yt, out)


def attention(nc, x, w_qkv, w_k, w_q, w_kcv, w_qc, g_kv, w_o, c_ident, c_rope, c_mask,
              c_ones, content_d, rope_d, max_d, x2, xn2, xT2h, xT2l, ident):
    with ExitStack() as stack:
        def sb(name, shape, dt=F32):
            return stack.enter_context(nc.sbuf_tensor(name, shape, dt))

        def pb(name, shape, dt=F32):
            return stack.enter_context(nc.psum_tensor(name, shape, dt))

        def sem(name):
            return stack.enter_context(nc.semaphore(name))

        wraw = sb("wraw", [128, 2, 1024])
        wkh, wkl = sb("wkh", [128, 1024], F32R), sb("wkl", [128, 1024], F32R)
        wqh, wql = sb("wqh", [128, 1024], F32R), sb("wql", [128, 1024], F32R)
        craw = sb("craw", [128, 3, 128])
        wqch, wqcl = sb("wqch", [128, 128], F32R), sb("wqcl", [128, 128], F32R)
        gain = sb("gain", [128, 1])
        cgain = sb("cgain", [128, 2, 128])
        cgain_hi = sb("cgain_hi", [128, 2, 128], F32R)
        wkcv = sb("wkcv", [128, 2, 128], F32R)
        wqkv = sb("wqkv", [128, QR + KVR])
        wo = sb("wo", [128, D])
        rope = sb("rope", [128, 2, T])
        maskf = sb("maskf", [128, 128])
        ident16 = sb("ident16", [128, 128], F16)
        identb = sb("identb", [128, 128], BF16)
        mask = sb("mask", [128, 2, 128], BF16)
        ones = sb("ones", [128, PER, 32])
        xt = sb("xt", [128, 2, 2, D])
        xr = sb("xr", [128, 2, D])
        stats, stats2 = sb("stats", [128, 2, 6]), sb("stats2", [128, 2, 6])
        moments, moments2 = sb("moments", [128, 2, 2]), sb("moments2", [128, 2, 2])
        rstd, rstd2 = sb("rstd", [128, 2]), sb("rstd2", [128, 2])
        xn = sb("xn", [128, 2, D])
        lat = sb("lat", [128, 2, QR + KVR])
        sq, kvn = sb("sq", [128, 2, KVR]), sb("kvn", [128, 2, KVR])
        ssum, mkv, rkv = sb("ssum", [128, 2]), sb("mkv", [128, 2]), sb("rkv", [128, 2])
        var, var2 = sb("var", [128, 2]), sb("var2", [128, 2])
        power = sb("power", [128, 2])
        lst = sb("lst", [128, 2, 256], F32R)
        mx = sb("mx", [128, 2, HEADS])
        mp = sb("mp", [128, 2, 2, HEADS], F16)
        x2s, xn2s = sb("x2s", [128, 2, D]), sb("xn2s", [128, 2, D])
        vp = sb("vp", [128, 2, 2, HEADS * 32 + 32])
        xT, xT2 = sb("xT", [128, T]), sb("xT2", [128, T])
        xTh, xTl = sb("xTh", [128, T], F32R), sb("xTl", [128, T], F32R)
        lT = sb("lT", [128, 4, 128], F32R)
        prod = sb("prod", [128, 2, 4, 2, T])
        rot = sb("rot", [128, 2, 4 * T])
        rh, rl = sb("rh", [128, 2, 4 * T], F16), sb("rl", [128, 2, 4 * T], F16)
        ch, cl = sb("ch", [128, 2 * T], F16), sb("cl", [128, 2 * T], F16)
        mT = sb("mT", [2 * HEADS, T], F16)
        qs = [sb(f"qs{i}", [128, HEADS, T], F16) for i in range(2)]
        ks = [sb(f"ks{i}", [128, HEADS, T], F16) for i in range(2)]
        pt = sb("pt", [128, 2, GROUPS, 384])
        rden, outT = sb("rden", [128, T]), sb("outT", [128, T])

        proj = pb("proj", [128, 2, 512])
        score = pb("score", [128, 4, 512])
        acc = pb("acc", [128, 512])
        misc = pb("misc", [128, 512])

        loaded, zeroed = sem("weights_loaded"), sem("zeroed")
        cast, weights_ready = sem("weights_cast"), sem("weights_ready")
        x_in = [sem("x_in0"), sem("x_in1")]
        xr_in = sem("xr_in")
        xn_ready, xT_ps = sem("xn_ready"), sem("xT_ps")
        xT_ready, xTl_ready = sem("xT_ready"), sem("xTl_ready")
        lat_ps, lat_read, lst_ready = sem("lat_ps"), sem("lat_read"), sem("lst_ready")
        lT_ps, lT_ready = sem("lT_ps"), sem("lT_ready")
        proj_done, proj_read = sem("proj_done"), sem("proj_read")
        content_hi, content_out = sem("content_hi"), sem("content_out")
        rope_sum, rope_hi, rope_lo = sem("rope_sum"), sem("rope_hi"), sem("rope_lo")
        hi_out, lo_out = [sem("hi_out0"), sem("hi_out1")], [sem("lo_out0"), sem("lo_out1")]
        stack_in = [sem("stack_in0"), sem("stack_in1")]
        rows_done, max_read, mp_ready = sem("rows_done"), sem("max_read"), sem("mp_ready")
        mT_ps, mT_ready, m_out, m_in = sem("mT_ps"), sem("mT_ready"), sem("m_out"), sem("m_in")
        st_done, exp_done, masked, pv_done = (sem("st_done"), sem("exp_done"), sem("masked"),
                                              sem("pv_done"))
        out_ready, y_ps, x2_ready = sem("out_ready"), sem("y_ps"), sem("x2_ready")
        v_ps, v_ready = sem("v_ps"), sem("v_ready")
        xn2_ready, xT2_ps, xT2_read = sem("xn2_ready"), sem("xT2_ps"), sem("xT2_read")
        xT2_done, kept = sem("xT2_done"), sem("kept")
        var_ready, rstd_ready = sem("var_ready"), sem("rstd_ready")
        var2_ready, rstd2_ready = sem("var2_ready"), sem("rstd2_ready")
        mkv_ready, rkv_ready = sem("mkv_ready"), sem("rkv_ready")
        c_set, c_ln1, c_lat = sem("chain_setup"), sem("chain_ln1"), sem("chain_latent")
        c_max, c_ln2, c_norm = sem("chain_max"), sem("chain_ln2"), sem("chain_norm")
        passed_dve, passed_pool = sem("passed_dve"), sem("passed_pool")
        LOADS = 19

        def steps(eng, step):
            step(-1, 1, False, False, True)
            step(0, 0, False, True, True)
            step(0, 1, True, True, True)
            with eng.Fori(1, BATCH // 2 - 1) as pair:
                step(pair, 0, True, True, True)
                step(pair, 1, True, True, True)
            step(BATCH // 2 - 1, 0, True, True, True)
            step(BATCH // 2 - 1, 1, True, True, False)
            step(BATCH // 2, 0, True, False, False)

        def unit_heads(u):
            return [PER * (2 * (u % 2) + e) + u // 2 for e in range(2)]

        with nc.Block() as block:
            @block.sync
            def _(sp):
                def x_of(b):
                    if isinstance(b, int):
                        return x[b].rearrange("(i p) d -> p i d", p=128)
                    return x[bass.ds(b, 1)].rearrange("a (i p) d -> p (a i) d", p=128)

                for dst, src in ((wqkv[:, :], w_qkv), (ident[:, :], c_ident),
                                 (wraw[:, 0, :], w_k), (rope[:, :, :], c_rope),
                                 (maskf[:, :], c_mask), (ones[:, :, :], c_ones), (wo[:, :], w_o)):
                    sp.dma_start(dst, src).then_inc(loaded, 16)
                for i in range(2):
                    sp.dma_start(wraw[64 * i:64 * i + 64, 1, :], w_q).then_inc(loaded, 16)
                for i in range(2):
                    sp.dma_start(craw[64 * i:64 * i + 64, 0, :], w_qc).then_inc(loaded, 16)
                for i in range(4):
                    sp.dma_start(craw[32 * i:32 * i + 32, 1:3, :], w_kcv).then_inc(loaded, 16)
                for i in range(3):
                    sp.dma_start(gain[32 * i:32 * i + 32, :], g_kv).then_inc(loaded, 16)
                sp.dma_start(gain[96:128, :], g_kv).then_inc(loaded, 16)

                def step(pair, par, prev, cur, nxt):
                    k = 2 * pair + par
                    if nxt:
                        wait(sp, xn_ready, k)
                        sp.dma_start(xt[:, 1 - par], x_of(k + 1)).then_inc(x_in[1 - par], 16)
                    if prev:
                        wait(sp, x2_ready, k - 1)
                        sp.dma_start(xr[:, :, :], x_of(k - 1)).then_inc(xr_in, 16)
                        wait(sp, mT_ready, k)
                        sp.dma_start(max_d, mT[:, :]).then_inc(m_out, 16)
                        wait(sp, m_out, 16 * k)
                        sp.dma_start(qs[1 - par][120:122, :, :],
                                     max_d.rearrange("(a h) t -> a h t", a=2)).then_inc(m_in, 16)
                    if cur:
                        def send(dst, src, sent):
                            sp.dma_start(dst, src[:, :]).then_inc(sent, 16)

                        def rotary(dst, side, part, sent, rows):
                            wait(sp, sent, 16 * (k + 1))
                            for r in rows:
                                sp.dma_start(dst[r:r + 32, :, :].rearrange(
                                                 "p (g c) t -> p g (c t)", g=GROUPS),
                                             rope_d[side, part]
                                             .rearrange("(g r) n -> r g n", g=GROUPS)
                                             ).then_inc(stack_in[par], 16)

                        def content(dst, side, parts):
                            for i, part in enumerate(parts):
                                sp.dma_start(dst[96 + 8 * i:104 + 8 * i, :, :],
                                             content_d[part]
                                             .rearrange("(h d) (s t) -> s d h t", d=HD, s=2)[side]
                                             ).then_inc(stack_in[par], 16)

                        wait(sp, rope_hi, 2 * k + 1)
                        send(rope_d[0, 0], rh[:, 0], hi_out[0])
                        wait(sp, content_hi, k + 1)
                        send(content_d[0], ch, content_out)
                        wait(sp, proj_read, UNITS * (k + 1))
                        send(content_d[1], cl, content_out)
                        wait(sp, rope_lo, 2 * k + 1)
                        send(rope_d[0, 1], rl[:, 0], lo_out[0])
                        rotary(ks[par], 0, 0, hi_out[0], (0, 64))
                        wait(sp, rope_hi, 2 * k + 2)
                        send(rope_d[1, 0], rh[:, 1], hi_out[1])
                        rotary(ks[par], 0, 1, lo_out[0], (32,))
                        wait(sp, rope_lo, 2 * k + 2)
                        send(rope_d[1, 1], rl[:, 1], lo_out[1])
                        wait(sp, content_out, 32 * (k + 1))
                        content(ks[par], 1, (0, 1, 0))
                        rotary(qs[par], 1, 0, hi_out[1], (0, 32))
                        rotary(qs[par], 1, 1, lo_out[1], (64,))
                        content(qs[par], 0, (0, 0, 1))
                    if prev:
                        wait(sp, xn2_ready, k)
                        for dst, src in ((x2, x2s), (xn2, xn2s)):
                            sp.dma_start(dst[:, bass.ds(2 * (k - 1), 2), :],
                                         src[:, :, :]).then_inc(kept, 16)
                steps(sp, step)
                sp.wait_ge(kept, 32 * BATCH)

            @block.gpsimd
            def _(pool):
                fills = [(power[:, :], -0.5)]
                for i in range(2):
                    fills += [(ks[i][96:128, :, :], -1.0), (qs[i][96:128, :, :], 0.0),
                              (vp[:, i], 0.0)]
                for n, (place, value) in enumerate(fills):
                    pool.memset(place, value).then_inc(zeroed, 1)
                    pool.wait_ge(zeroed, n + 1)

                def step(pair, par, prev, cur, nxt):
                    k = 2 * pair + par

                    def inverse_root(src, ready, dst, done, turn):
                        wait(pool, ready, turn)
                        pool.tensor_tensor(dst[:, :], src[:, :], power[:, :],
                                           ALU.pow).then_inc(done, 1)

                    def add(side):
                        wait(pool, proj_read, UNITS * k + 4 * side + 4)
                        wait(pool, rope_hi, 2 * (k - 1) + side + 1)
                        wait(pool, rope_lo, 2 * (k - 1) + side + 1)
                        pool.tensor_tensor(rot[:, side, :].rearrange("p (c t) -> p c t", c=4),
                                           prod[:, side, :, 0, :], prod[:, side, :, 1, :],
                                           ALU.add).then_inc(rope_sum, 1)

                    def causal(g):
                        for u in (2 * g, 2 * g + 1):
                            wait(pool, exp_done, 8 * (k - 1) + u + 1)
                            settle(pool, passed_pool)
                            diag = pt[:, g % 2, 2 * (u % 2):2 * (u % 2) + 2, :].rearrange(
                                "p h t -> p (h t)")[:, 128:640].rearrange("p (b t) -> p b t", b=4)
                            pool.affine_select(out=diag, in_=diag, compare_op=ALU.is_ge, fill=0.0,
                                               base=0, pattern=[[0, 4], [1, 128]],
                                               channel_multiplier=-1).then_inc(masked, 1)
                    if cur:
                        add(0)
                        add(1)
                    if prev:
                        causal(0)
                    if nxt:
                        inverse_root(var, var_ready, rstd, rstd_ready, k + 2)
                    if prev:
                        causal(1)
                        causal(2)
                    if nxt:
                        inverse_root(mkv, mkv_ready, rkv, rkv_ready, k + 2)
                    if prev:
                        causal(3)
                        inverse_root(var2, var2_ready, rstd2, rstd2_ready, k)
                steps(pool, step)

            @block.scalar
            def _(act):
                act.wait_ge(loaded, 16 * LOADS)
                act.activation(wkh[:, :], wraw[:, 0, :], ACT.Copy).then_inc(cast, 1)
                act.activation(wqh[:, :], wraw[:, 1, :], ACT.Copy).then_inc(cast, 1)
                act.activation(wqch[:, :], craw[:, 0, :], ACT.Copy).then_inc(cast, 1)
                act.activation(ident16[:, :], ident[:, :], ACT.Copy).then_inc(cast, 1)
                act.activation(identb[:, :], ident[:, :], ACT.Copy).then_inc(cast, 1)
                for i in range(2):
                    act.activation(mask[:, i, :], maskf[:, :], ACT.Copy).then_inc(cast, 1)
                act.wait_ge(zeroed, 7)

                def step(pair, par, prev, cur, nxt):
                    k = 2 * pair + par

                    def rotary_hi(side):
                        wait(act, rope_sum, 2 * k + side + 1)
                        wait(act, rope_lo, 2 * (k - 1) + side + 1)
                        wait(act, stack_in[1 - par], STACKED * (pair + par))
                        act.activation(rh[:, side, :], rot[:, side, :],
                                       ACT.Copy).then_inc(rope_hi, 1)

                    def exps(u):
                        wait(act, st_done, 8 * (k - 1) + u + 1)
                        wait(act, pv_done, 4 * (k - 1) + u // 2 - 1)
                        b = 2 * (u % 2)
                        act.activation(pt[:, (u // 2) % 2, b:b + 2, :], score[:, b:b + 2, 0:384],
                                       ACT.Exp, scale=SCALE).then_inc(exp_done, 1)
                    if prev:
                        wait(act, mT_ps, k)
                        wait(act, m_out, 16 * (k - 1))
                        act.activation(mT[:, :], misc[0:32, 0:128].bitcast(F16),
                                       ACT.Copy).then_inc(mT_ready, 1)
                    if cur:
                        rotary_hi(0)
                        wait(act, proj_done, UNITS * (k + 1))
                        wait(act, content_out, 32 * k)
                        act.activation(ch[:, :], proj[:, (UNITS - 1) % 2, :],
                                       ACT.Copy).then_inc(content_hi, 1)
                    if prev:
                        exps(0)
                        exps(1)
                    if cur:
                        rotary_hi(1)
                    if prev:
                        exps(2)
                        exps(3)
                    if cur:
                        wait(act, v_ps, k + 1)
                        wait(act, pv_done, 4 * (k - 1))
                        for i in range(2):
                            for g in range(GROUPS):
                                at = 128 * g
                                ins = act.activation(
                                    vp[:, par, i, at:at + 160].rearrange(
                                        "p (m a) -> p m a", a=40)[:, :, 0:HD],
                                    misc[:, 128 * i + 32 * g:128 * i + 32 * g + 32]
                                    .rearrange("p (m d) -> p m d", m=PER), ACT.Copy)
                        ins.then_inc(v_ready, 1)
                    if nxt:
                        wait(act, xT_ps, k + 2)
                        wait(act, xTl_ready, k + 1)
                        wait(act, lat_ps, k + 1)
                        act.activation(xT[:, :], misc[:, 0:T], ACT.Copy)
                        wait(act, proj_done, UNITS * (k + 1))
                        act.activation(xTh[:, :], misc[:, 0:T], ACT.Copy).then_inc(xT_ready, 1)
                    if prev:
                        for u in range(4, 8):
                            exps(u)
                    if nxt:
                        wait(act, lT_ps, k + 2)
                        act.activation(lT[:, :, :].rearrange("p a t -> p (a t)"), misc[:, :],
                                       ACT.Copy).then_inc(lT_ready, 1)
                    if prev:
                        wait(act, xT2_ps, k)
                        wait(act, xT2_done, k - 1)
                        act.activation(xT2[:, :], misc[:, 0:T], ACT.Copy)
                        act.activation(xT2h[:, bass.ds(T * (k - 1), T)], misc[:, 0:T],
                                       ACT.Copy).then_inc(xT2_read, 1)
                steps(act, step)

            @block.vector
            def _(dve):
                setup = Chain(dve, c_set)
                ln1, lats = Chain(dve, c_ln1), Chain(dve, c_lat)
                maxs, ln2, norm = Chain(dve, c_max), Chain(dve, c_ln2), Chain(dve, c_norm)
                dve.wait_ge(loaded, 16 * LOADS)
                setup.link(dve.tensor_scalar(cgain[:, :, :], craw[:, 1:3, :], gain[:, 0:1], None,
                                             ALU.mult))
                setup.link(dve.tensor_copy(cgain_hi[:, :, :], cgain[:, :, :]))
                dve.tensor_copy(wkcv[0:64, :, :], cgain[0:64, :, :])
                dve.tensor_tensor(wkcv[64:128, :, :], cgain[64:128, :, :],
                                  cgain_hi[64:128, :, :].bitcast(F32), ALU.subtract)
                dve.wait_ge(cast, 7)
                for lo, raw, hi in ((wkl, wraw[:, 0, :], wkh), (wql, wraw[:, 1, :], wqh),
                                    (wqcl, craw[:, 0, :], wqch)):
                    ins = dve.tensor_tensor(lo[:, :], raw, hi[:, :].bitcast(F32), ALU.subtract)
                ins.then_inc(weights_ready, 1)

                def step(pair, par, prev, cur, nxt):
                    k = 2 * pair + par

                    def maxima(u):
                        wait(dve, rows_done, 8 * k + u + 1)
                        b, h = 2 * (u % 2), unit_heads(u)
                        at = slice(h[0], h[1] + 1, h[1] - h[0])
                        dve.tensor_reduce(mx[:, 0, at], score[:, b:b + 2, 0:128], AX.X, ALU.max)
                        dve.tensor_reduce(mx[:, 1, at], score[:, b:b + 2, 128:384], AX.X,
                                          ALU.max).then_inc(max_read, 1)
                    def low(side):
                        wait(dve, rope_hi, 2 * k + side + 1)
                        wait(dve, lo_out[side], 16 * k)
                        dve.tensor_tensor(rl[:, side, :], rot[:, side, :], rh[:, side, :],
                                          ALU.subtract).then_inc(rope_lo, 1)
                    if cur:
                        for n in range(UNITS - 1):
                            side, c = n // 4, n % 4
                            wait(dve, proj_done, UNITS * k + n + 1)
                            if c == 0:
                                wait(dve, rope_sum, 2 * (k - 1) + side + 1)
                            dve.tensor_tensor(prod[:, side, c], proj[:, n % 2, :]
                                              .rearrange("p (a t) -> p a t", a=2), rope[:, :, :],
                                              ALU.mult).then_inc(proj_read, 1)
                        wait(dve, content_hi, k + 1)
                        wait(dve, content_out, 32 * k)
                        dve.tensor_tensor(cl[:, :], proj[:, (UNITS - 1) % 2, :], ch[:, :],
                                          ALU.subtract).then_inc(proj_read, 1)
                        low(0)
                    if nxt:
                        ln1.start(k + 1)
                        wait(dve, x_in[1 - par], 16 * (pair + 1 + par))
                        wait(dve, xT_ps, k + 1)
                        wait(dve, xn_ready, k + 1)
                        layernorm(dve, passed_dve, ln1.link, xt[:, 1 - par], stats, moments, var, rstd,
                                  var_ready, rstd_ready, k + 2, xn).then_inc(xn_ready, 1)
                    if cur:
                        low(1)
                    if nxt:
                        wait(dve, xT_ready, k + 2)
                        dve.tensor_tensor(xTl[:, :], xT[:, :], xTh[:, :].bitcast(F32),
                                          ALU.subtract).then_inc(xTl_ready, 1)
                        lats.start(k + 1)
                        link = lats.link
                        wait(dve, lat_ps, k + 2)
                        wait(dve, lT_ps, k + 1)
                        dve.tensor_copy(lat[:, :, :].rearrange("p i c -> p (i c)"),
                                        misc[:, 0:2 * (QR + KVR)]).then_inc(lat_read, 1)
                        wait(dve, lat_read, k + 2)
                        q, kv = lat[:, :, 0:QR], lat[:, :, QR:QR + KVR]
                        dve.tensor_copy(lst[:, :, 0:QR], q)
                        link(dve.tensor_tensor(sq[:, :, :], kv, kv, ALU.mult))
                        link(dve.tensor_reduce(ssum[:, :], sq[:, :, :], AX.X, ALU.add))
                        dve.tensor_tensor(lst[:, :, QR:2 * QR], q, lst[:, :, 0:QR].bitcast(F32),
                                          ALU.subtract)
                        dve.tensor_scalar(mkv[:, :], ssum[:, :], 1.0 / KVR, RMS_EPS,
                                          ALU.mult, ALU.add).then_inc(mkv_ready, 1)
                        wait(dve, rkv_ready, k + 2)
                        link(dve.tensor_tensor(kvn[:, :, :], kv, rkv[:, :].unsqueeze(2)
                                               .broadcast_to([128, 2, KVR]), ALU.mult))
                        parts = lst[:, :, 2 * QR:].rearrange("p i (r a c) -> p i r a c", r=2, a=2)
                        for r in range(2):
                            ins = dve.tensor_copy(parts[:, :, r, 0], kvn[:, :, :])
                        link(ins)
                        for r in range(2):
                            ins = dve.tensor_tensor(parts[:, :, r, 1], kvn[:, :, :],
                                                    parts[:, :, r, 0].bitcast(F32), ALU.subtract)
                        ins.then_inc(lst_ready, 1)
                    if prev:
                        norm.start(k - 1)
                        wait(dve, pv_done, 4 * k)
                        wait(dve, y_ps, k - 1)
                        norm.link(dve.reciprocal(rden[:, :], acc[:, T:2 * T]))
                        dve.tensor_tensor(outT[:, :], acc[:, 0:T], rden[:, :],
                                          ALU.mult).then_inc(out_ready, 1)
                    if cur:
                        maxima(0)
                    if prev:
                        wait(dve, y_ps, k)
                        wait(dve, xr_in, 16 * k)
                        wait(dve, kept, 32 * (k - 1))
                        dve.tensor_tensor(x2s[:, :, :], misc[:, 0:2 * D]
                                          .rearrange("p (i d) -> p i d", i=2), xr[:, :, :],
                                          ALU.add).then_inc(x2_ready, 1)
                    if cur:
                        maxima(1)
                    if prev:
                        ln2.start(k - 1)
                        wait(dve, x2_ready, k)
                        wait(dve, xT2_ps, k - 1)
                        layernorm(dve, passed_dve, ln2.link, x2s, stats2, moments2, var2, rstd2,
                                  var2_ready, rstd2_ready, k, xn2s).then_inc(xn2_ready, 1)
                    if cur:
                        for u in range(2, 8):
                            maxima(u)
                        maxs.start(k)
                        wait(dve, max_read, 8 * (k + 1))
                        wait(dve, mT_ps, k)
                        maxs.link(dve.tensor_copy(mp[:, :, 0, :], mx[:, :, :]))
                        dve.tensor_tensor(mp[:, :, 1, :], mx[:, :, :], mp[:, :, 0, :],
                                          ALU.subtract).then_inc(mp_ready, 1)
                    if prev:
                        wait(dve, xT2_read, k)
                        at = bass.ds(T * (k - 1), T)
                        dve.tensor_tensor(xT2l[:, at], xT2[:, :], xT2h[:, at].bitcast(F32),
                                          ALU.subtract).then_inc(xT2_done, 1)
                steps(dve, step)

            @block.tensor
            def _(pe):
                pe.wait_ge(loaded, 16 * LOADS)
                pe.wait_ge(zeroed, 7)
                pe.wait_ge(cast, 7)
                pe.wait_ge(weights_ready, 1)

                def step(pair, par, prev, cur, nxt):
                    k = 2 * pair + par

                    def project(n):
                        wait(pe, proj_read, UNITS * k + max(n - 1, 0))
                        bank = proj[:, n % 2, :]
                        xh, xl = xTh[:, :], xTl[:, :]
                        q = lT[:, 0:2, :].rearrange("p a t -> p (a t)")
                        kv = lT[:, 2:4, :].rearrange("p a t -> p (a t)")
                        for a in range(2):
                            if n < 4:
                                w = slice(256 * n + 128 * a, 256 * n + 128 * a + 128)
                                passes = ((wkh[:, w], xh), (wkh[:, w], xl), (wkl[:, w], xh))
                            elif n < 8:
                                w = slice(256 * (n - 4) + 128 * a, 256 * (n - 4) + 128 * a + 128)
                                passes = ((wqh[:, w], q), (wql[:, w], q))
                            elif a == 0:
                                passes = ((wqch[:, :], q), (wqcl[:, :], q))
                            else:
                                passes = ((wkcv[:, 0, :], kv),)
                            for i, (w, m) in enumerate(passes):
                                ins = pe.matmul(bank[:, T * a:T * a + T], w, m, start=(i == 0),
                                                stop=(i == len(passes) - 1))
                        ins.then_inc(proj_done, 1)

                    def keys_by_queries(u):
                        if u < 2:
                            wait(pe, max_read, 8 * k - 1 + u)
                        else:
                            wait(pe, exp_done, 8 * (k - 1) + u - 1)
                        for e, h in enumerate(unit_heads(u)):
                            bank = score[:, 2 * (u % 2) + e, :]
                            for i, j in ((0, 0), (0, 1), (1, 1)):
                                at = 128 * PLACES[e][i, j]
                                ins = pe.matmul(bank[:, at:at + 128],
                                                ks[1 - par][:, h, 128 * i:128 * i + 128],
                                                qs[1 - par][:, h, 128 * j:128 * j + 128],
                                                start=True, stop=True)
                        ins.then_inc(st_done, 1)

                    def queries_by_keys(u):
                        if u < 2:
                            wait(pe, exp_done, 8 * k - 1 + u)
                        else:
                            wait(pe, max_read, 8 * k + u - 1)
                        for e, h in enumerate(unit_heads(u)):
                            bank = score[:, 2 * (u % 2) + e, :]
                            pe.matmul(bank[:, 0:256], identb[:, :],
                                      mask[:, :, :].rearrange("p a t -> p (a t)"), start=True,
                                      stop=False, skip_group_check=True)
                            for i, j, at in ((0, 0, 0), (1, 1, 128), (1, 0, 256)):
                                ins = pe.matmul(bank[:, at:at + 128],
                                                qs[par][0:120, h, 128 * i:128 * i + 128],
                                                ks[par][0:120, h, 128 * j:128 * j + 128],
                                                start=False, stop=True, skip_group_check=True)
                        ins.then_inc(rows_done, 1)

                    def weigh(g):
                        wait(pe, masked, 8 * (k - 1) + 2 * g + 2)
                        for i, q in ((0, 0), (0, 1), (1, 1)):
                            for den in range(2):
                                for j in range(GROUPS):
                                    h = PER * j + g
                                    w = ones[:, g, :] if den else \
                                        vp[:, 1 - par, i, 32 * h:32 * h + 32]
                                    at = 128 * PLACES[j % 2][i, q]
                                    to = T * den + 128 * q
                                    ins = pe.matmul(
                                        acc[32 * j:32 * j + 32, to:to + 128], w,
                                        pt[:, g % 2, j, at:at + 128],
                                        start=(g == 0 and i == q == den == 0),
                                        stop=(g == 3 and i == q), skip_group_check=True)
                        ins.then_inc(pv_done, 1)

                    if cur:
                        wait(pe, xTl_ready, k + 1)
                        wait(pe, lT_ready, k + 1)
                        project(0)
                        project(1)
                    if prev:
                        wait(pe, mp_ready, k)
                        wait(pe, xT2_read, k - 1)
                        for i in range(2):
                            ins = pe.transpose(misc[0:32, 64 * i:64 * i + 64].bitcast(F16),
                                               mp[:, i].rearrange("p a h -> p (a h)"),
                                               ident16[:, :])
                        ins.then_inc(mT_ps, 1)
                    if cur:
                        for n in range(2, UNITS):
                            project(n)
                    if prev:
                        wait(pe, m_in, 16 * k)
                        for u in range(4):
                            keys_by_queries(u)
                    if cur:
                        if prev:
                            wait(pe, mT_ready, k)
                        for i in range(2):
                            ins = pe.matmul(misc[:, 128 * i:128 * i + 128], lT[:, 2 + i, :],
                                            wkcv[:, 1, :], start=True, stop=True)
                        ins.then_inc(v_ps, 1)
                    if prev:
                        wait(pe, v_ready, k)
                        wait(pe, out_ready, k - 1)
                        weigh(0)
                        keys_by_queries(4)
                        keys_by_queries(5)
                    if nxt:
                        wait(pe, xn_ready, k + 2)
                        wait(pe, v_ready, k + 1)
                        for i in range(2):
                            ins = pe.transpose(misc[:, 128 * i:128 * i + 128], xn[:, i, :],
                                               ident[:, :])
                        ins.then_inc(xT_ps, 1)
                    if prev:
                        weigh(1)
                        keys_by_queries(6)
                        keys_by_queries(7)
                    if nxt:
                        wait(pe, xT_ready, k + 2)
                        for i in range(2):
                            ins = pe.matmul(misc[:, 96 * i:96 * i + 96],
                                            xT[:, 128 * i:128 * i + 128], wqkv[:, :],
                                            start=True, stop=True)
                        ins.then_inc(lat_ps, 1)
                    if prev:
                        weigh(2)
                        weigh(3)
                    if cur:
                        wait(pe, stack_in[par], STACKED * (pair + 1))
                        queries_by_keys(0)
                    if nxt:
                        wait(pe, lst_ready, k + 2)
                        wait(pe, lat_read, k + 2)
                        for a in range(2):
                            for i in range(2):
                                ins = pe.transpose(
                                    misc[:, 256 * a + 128 * i:256 * a + 128 * i + 128],
                                    lst[:, i, 128 * a:128 * a + 128].bitcast(F32), ident[:, :])
                        ins.then_inc(lT_ps, 1)
                    if cur:
                        queries_by_keys(1)
                    if prev:
                        wait(pe, out_ready, k)
                        if nxt:
                            wait(pe, lT_ready, k + 2)
                        elif cur:
                            wait(pe, v_ready, k + 1)
                        else:
                            wait(pe, mT_ready, k)
                        for i in range(2):
                            ins = pe.matmul(misc[:, 128 * i:128 * i + 128],
                                            outT[:, 128 * i:128 * i + 128], wo[:, :],
                                            start=True, stop=True)
                        ins.then_inc(y_ps, 1)
                    if cur:
                        for u in range(2, 8):
                            queries_by_keys(u)
                    if prev:
                        wait(pe, xn2_ready, k)
                        wait(pe, x2_ready, k)
                        for i in range(2):
                            ins = pe.transpose(misc[:, 128 * i:128 * i + 128], xn2s[:, i, :],
                                               ident[:, :])
                        ins.then_inc(xT2_ps, 1)
                steps(pe, step)
                pe.wait_ge(xT2_done, BATCH)


def dispatch(nc, phi_t, phi_b, exp_w, exp_b, c_dshift, c_expert, xn2, xT2h, xT2l, ident, phT_h,
             phT_l, mcT, yt):
    with ExitStack() as stack:
        def sb(name, shape, dt=F32):
            return stack.enter_context(nc.sbuf_tensor(name, shape, dt))

        def pb(name, shape, dt=F32):
            return stack.enter_context(nc.psum_tensor(name, shape, dt))

        def sem(name):
            return stack.enter_context(nc.semaphore(name))

        ew = sb("ew", [128, EXPERTS, D])
        eb = sb("eb", [EXPERTS, D])
        e_rows = sb("e_rows", [EXPERTS, NCH, 128])
        xth = [sb(f"xth{i}", [128, 128], F32R) for i in range(4)]
        xtl = [sb(f"xtl{i}", [128, 128], F32R) for i in range(4)]
        xd = [sb(f"xd{i}", [128, D]) for i in range(4)]
        raw = sb("raw", [128, HALF])
        bias = sb("bias", [128, NS], BF16)
        braw, brest = sb("braw", [128, NCH]), sb("brest", [128, NCH])
        bpart = sb("bpart", [128, 3, NCH], BF16)
        ones_b = sb("ones_b", [128, 128], BF16)
        shift = sb("shift", [3 * HALF_E, HALF], F32R)
        identb = sb("identb_d", [128, 128], BF16)
        md = sb("md", [128, HALF_E])
        mdp = sb("mdp", [128, 3, HALF_E], F32R)
        mdT = sb("mdT", [3 * HALF_E, 2, 128], F32R)
        mc = sb("mc", [128, TILES, SLOTS])
        mc2, mcm, resc = sb("mc2", [128, SLOTS]), sb("mcm", [128, 2, SLOTS]), sb("resc", [128, SLOTS])
        mcp = sb("mcp", [128, 3, SLOTS], BF16)
        e = sb("e", [128, 4, HALF])
        den, rden = sb("den_d", [128, HALF_E]), sb("rden_d", [128, 2, HALF_E])
        xs = sb("xs", [128, NS])
        th = sb("th", [128, 2, 4, D])
        thT = sb("thT", [128, 2, 4, 128])
        st, mo = sb("st_d", [128, 4, 6]), sb("mo_d", [128, 4, 2])
        sv, power = sb("sv_d", [128, 2, 4]), sb("power_d", [128, 4])
        sr, nb = sb("sr_d", [128, 2, 4]), sb("nb_d", [128, 2, 4])

        lg = pb("lg", [128, 2, HALF])
        xacc = pb("xacc", [128, HALF])
        tp = pb("tp", [128, 2, 512])

        loaded, ew_in, filled, cast, setup_done = (sem("d_loaded"), sem("ew_in"), sem("d_filled"),
                                                   sem("d_cast"), sem("d_setup"))
        d_in = [sem(f"d_in{i}") for i in range(4)]
        xd_in = [sem(f"xd_in{i}") for i in range(4)]
        b_in, bpart_ready, bias_in = sem("b_in"), sem("bpart_ready"), sem("bias_in")
        lg_done, md_ready, mc_read, md_ps, mdT_ready = (sem("lg_done"), sem("md_ready"),
                                                        sem("mc_read"), sem("md_ps"),
                                                        sem("mdT_ready"))
        mcm_ready, passed = sem("mcm_ready"), sem("d_passed")
        mcp_ready, mc_ps, mcT_ready = sem("mcp_ready"), sem("mc_ps"), sem("mcT_ready")
        shifted, exp_done, den_ready, scaled, summed = (sem("shifted"), sem("d_exp"),
                                                        sem("den_ready"), sem("scaled"),
                                                        sem("summed"))
        xs_ready = sem("xs_ready")
        c_set, c_md, c_mc, c_den, c_ex = (sem("d_chain_setup"), sem("d_chain_md"),
                                          sem("d_chain_mc"), sem("d_chain_den"),
                                          sem("d_chain_ex"))
        sv_ready, sr_ready = sem("sv_ready"), sem("sr_ready")
        x_ps, sx_ready, th_ready, th_ps, thT_ready, y_ps, y_ready = (
            sem("x_ps"), sem("sx_ready"), sem("th_ready"), sem("th_ps"), sem("thT_ready"),
            sem("d_y_ps"), sem("d_y_ready"))

        def steps(eng, step):
            def rounds(u):
                return [None if not 0 <= u - lag < 2 * TILES else int(u - lag >= TILES)
                        for lag in (0, 1, 3)]
            for rnd in range(2):
                first = 2 - rnd
                for t in range(4 * first):
                    step(rnd, t // 4, t % 4, *rounds(TILES * rnd + t))
                with eng.Fori(first, TILES // 4) as quad:
                    for r in range(4):
                        step(rnd, quad, r, rnd, rnd, rnd)
            for r in range(3):
                step(2, 0, r, *rounds(2 * TILES + r))

        with nc.Block() as block:
            @block.sync
            def _(sp):
                sp.dma_start(braw[:, :], phi_b.rearrange("(s c) -> s c", c=NCH)).then_inc(b_in, 16)
                sp.dma_start(xs[:, :], phi_t).then_inc(loaded, 16)
                sp.dma_start(raw[0:96, :], c_dshift).then_inc(loaded, 16)
                sp.dma_start(eb[:, :], exp_b).then_inc(ew_in, 16)
                sp.dma_start(e_rows[:, :, :], c_expert).then_inc(ew_in, 16)
                sp.wait_ge(filled, 1)
                for i in range(3):
                    sp.wait_ge(bpart_ready, i + 1)
                    sp.dma_start(bias[32 * i:32 * i + 1, :].rearrange("a (s c) -> a s c", c=NCH),
                                 bpart[:, i, :]).then_inc(bias_in, 16)

                def step(rnd, quad, r, make, shifts, use):
                    t = 4 * quad + r
                    u = TILES * rnd + t
                    if isinstance(u, int) and u == 4:
                        sp.wait_ge(lg_done, 1)
                    wait(sp, summed, u - 4)
                    if make is not None:
                        at = bass.ds(128 * t, 128)
                        for dst, src in ((xth[r][:, :], xT2h[:, at]), (xtl[r][:, :], xT2l[:, at])):
                            sp.dma_start(dst.bitcast(F32), src.bitcast(F32)).then_inc(d_in[r], 16)
                    if shifts is not None:
                        at = bass.ds(t - 1 + TILES * (rnd - shifts), 1)
                        sp.dma_start(xd[(r - 1) % 4][:, :], xn2[:, at, :]
                                     .rearrange("p a d -> p (a d)")).then_inc(xd_in[(r - 1) % 4], 16)
                    if isinstance(u, int) and u == 3:
                        sp.dma_start(ew[:, :, :], exp_w.rearrange("n d h -> d n h")
                                     ).then_inc(ew_in, 16)
                steps(sp, step)

            @block.gpsimd
            def _(pool):
                for n, (place, value) in enumerate(((bias[:, :], 0.0), (ones_b[:, :], 1.0),
                                                    (mdp[:, 2, :].bitcast(F32), 0.0),
                                                    (power[:, :], -0.5))):
                    pool.memset(place, value).then_inc(filled, 1)
                    pool.wait_ge(filled, n + 1)
                cmc = Chain(pool, c_mc)

                def step(rnd, quad, r, make, shifts, use):
                    t = 4 * quad + r
                    u = TILES * rnd + t
                    if make == 1:
                        cmc.start(t)
                        wait(pool, mcm_ready, t + 1)
                        wait(pool, mc_ps, t)
                        wait(pool, mcp_ready, t)
                        link = cmc.link
                        settle(pool, passed)
                        link(pool.tensor_copy(mcp[:, 0, :], mcm[:, r % 2, :]))
                        link(pool.tensor_tensor(resc[:, :], mcm[:, r % 2, :], mcp[:, 0, :],
                                                ALU.subtract))
                        settle(pool, passed)
                        link(pool.tensor_copy(mcp[:, 1, :], resc[:, :]))
                        pool.tensor_tensor(mcp[:, 2, :], resc[:, :], mcp[:, 1, :],
                                           ALU.subtract).then_inc(mcp_ready, 1)
                    if shifts is not None:
                        wait(pool, den_ready, u)
                        w = e[:, (r - 1) % 4, :].rearrange("p (n s) -> p n s", s=SLOTS)
                        pool.tensor_tensor(w, w, rden[:, (r - 1) % 2, :].unsqueeze(2)
                                           .broadcast_to([128, HALF_E, SLOTS]),
                                           ALU.mult).then_inc(scaled, 1)
                steps(pool, step)
                for g in range(4):
                    pool.wait_ge(sv_ready, g + 1)
                    pool.tensor_tensor(sr[:, g % 2, :], sv[:, g % 2, :], power[:, :],
                                       ALU.pow).then_inc(sr_ready, 1)

            @block.scalar
            def _(act):
                act.wait_ge(loaded, 32)
                act.activation(phT_h[:, :], xs[:, :], ACT.Copy).then_inc(cast, 1)
                act.activation(shift[:, :], raw[0:96, :], ACT.Copy).then_inc(cast, 1)
                act.activation(identb[:, :], ident[:, :], ACT.Copy).then_inc(cast, 1)

                def step(rnd, quad, r, make, shifts, use):
                    t = 4 * quad + r
                    u = TILES * rnd + t
                    if shifts is not None:
                        b = (r - 1) % 2
                        wait(act, md_ps, u)
                        wait(act, shifted, u - 2)
                        act.activation(mdT[:, b, :], tp[0:96, 0, 0:128],
                                       ACT.Copy).then_inc(mdT_ready, 1)
                        wait(act, shifted, u)
                        wait(act, summed, u - 4)
                        act.activation(e[:, (r - 1) % 4, :], lg[:, b, :],
                                       ACT.Exp).then_inc(exp_done, 1)
                        if shifts == 1:
                            tile = t - 1 + TILES * (rnd - shifts)
                            wait(act, mc_ps, tile + 1)
                            act.activation(mcT[:, bass.ds(128 * tile, 128)],
                                           tp[0:96, 1, 0:64].bitcast(BF16),
                                           ACT.Copy).then_inc(mcT_ready, 1)
                steps(act, step)
                for g in range(4):
                    act.wait_ge(sx_ready, g + 1)
                    wait(act, th_ps, g - 1)
                    for i in range(4):
                        ins = act.activation(th[:, g % 2, i, :],
                                             lg[:, 0, 512 * (g % 2) + 128 * i:
                                                512 * (g % 2) + 128 * i + 128], ACT.Tanh,
                                             bias=nb[:, g % 2, i:i + 1],
                                             scale=sr[:, g % 2, i:i + 1])
                    ins.then_inc(th_ready, 1)
                    act.wait_ge(th_ps, g + 1)
                    wait(act, y_ps, g - 1)
                    act.activation(thT[:, g % 2].rearrange("p i t -> p (i t)"),
                                   lg[:, 1, 512 * (g % 2):512 * (g % 2) + 512],
                                   ACT.Copy).then_inc(thT_ready, 1)

            @block.vector
            def _(dve):
                setup, cmd = Chain(dve, c_set), Chain(dve, c_md)
                cden, cex = Chain(dve, c_den), Chain(dve, c_ex)
                dve.wait_ge(b_in, 16)
                rest = braw
                for i in range(3):
                    dve.tensor_copy(bpart[:, i, :], rest[:, :]).then_inc(bpart_ready, 1)
                    if i < 2:
                        dve.wait_ge(bpart_ready, i + 1)
                        setup.link(dve.tensor_tensor(brest[:, :], rest[:, :], bpart[:, i, :],
                                                     ALU.subtract))
                        rest = brest
                dve.wait_ge(cast, 1)
                dve.tensor_tensor(phT_l[:, :], xs[:, :], phT_h[:, :].bitcast(F32),
                                  ALU.subtract).then_inc(setup_done, 1)

                def step(rnd, quad, r, make, shifts, use):
                    t = 4 * quad + r
                    u = TILES * rnd + t
                    if make is not None:
                        b = r % 2
                        by_slot = lg[:, b, :].rearrange("p (n s) -> p n s", s=SLOTS)
                        by_expert = lg[:, b, :].rearrange("p (n s) -> p s n", s=SLOTS)
                        cmd.start(u)
                        wait(dve, lg_done, u + 1)
                        wait(dve, md_ps, u)
                        wait(dve, md_ready, u)
                        cmd.link(dve.tensor_reduce(md[:, :], by_slot, AX.X, ALU.max))
                        cmd.link(dve.tensor_copy(mdp[:, 0, :], md[:, :]))
                        dve.tensor_tensor(mdp[:, 1, :], md[:, :], mdp[:, 0, :].bitcast(F32),
                                          ALU.subtract).then_inc(md_ready, 1)
                        mc_t = mc[:, bass.ds(t, 1), :].rearrange("p a s -> p (a s)")
                        if make == 1:
                            wait(dve, mcm_ready, t)
                        dve.tensor_reduce(mc_t if make == 0 else mc2[:, :], by_expert, AX.X,
                                          ALU.max).then_inc(mc_read, 1)
                    if shifts is not None:
                        cden.start(u - 1)
                        wait(dve, exp_done, u)
                        wait(dve, scaled, u - 2)
                        wait(dve, den_ready, u - 1)
                        cden.link(dve.tensor_reduce(
                            den[:, :], e[:, (r - 1) % 4, :].rearrange("p (n s) -> p n s", s=SLOTS),
                            AX.X, ALU.add))
                        dve.reciprocal(rden[:, (r - 1) % 2, :], den[:, :]).then_inc(den_ready, 1)
                    if make == 1:
                        wait(dve, mc_read, u + 1)
                        wait(dve, mcp_ready, t - 1)
                        dve.tensor_tensor(mcm[:, b, :], mc2[:, :], mc_t,
                                          ALU.max).then_inc(mcm_ready, 1)
                    if isinstance(t, int) and t == 2 and rnd > 0:
                        dve.wait_ge(summed, TILES * (use + 1))
                        dve.tensor_scalar(xs[:, HALF * use:HALF * use + HALF], xacc[:, :],
                                          CLIP_LOW, CLIP_HIGH, ALU.max,
                                          ALU.min).then_inc(xs_ready, 1)
                steps(dve, step)
                for g in range(4):
                    dve.wait_ge(x_ps, g + 1)
                    wait(dve, th_ready, g - 1)
                    src = lg[:, 0, 512 * (g % 2):512 * (g % 2) + 512]
                    for i in range(4):
                        ins = dve.bn_stats(st[:, i, :], src[:, 128 * i:128 * i + 128])
                    cex.link(ins)
                    for i in range(4):
                        ins = dve.bn_aggr(mo[:, i, :], st[:, i, :])
                    cex.link(ins)
                    dve.tensor_scalar(sv[:, g % 2, :], mo[:, :, 1], LN_EPS, None,
                                      ALU.add).then_inc(sv_ready, 1)
                    dve.wait_ge(sr_ready, g + 1)
                    dve.scalar_tensor_tensor(nb[:, g % 2, :], mo[:, :, 0], -1.0, sr[:, g % 2, :],
                                             ALU.mult, ALU.mult).then_inc(sx_ready, 1)
                    if g >= 1:
                        dve.wait_ge(y_ps, g)
                        dve.tensor_copy(yt[:, 4 * g - 4:4 * g, :].rearrange("p i h -> p (i h)"),
                                        xacc[:, 512 * ((g - 1) % 2):512 * ((g - 1) % 2) + 512]
                                        ).then_inc(y_ready, 1)
                dve.wait_ge(y_ps, 4)
                dve.tensor_copy(yt[:, 12:16, :].rearrange("p i h -> p (i h)"),
                                xacc[:, 512:1024]).then_inc(y_ready, 1)

            @block.tensor
            def _(pe):
                pe.wait_ge(cast, 3)
                pe.wait_ge(filled, 3)
                pe.wait_ge(setup_done, 1)
                pe.wait_ge(bias_in, 48)

                def step(rnd, quad, r, make, shifts, use):
                    t = 4 * quad + r
                    u = TILES * rnd + t
                    if shifts is not None:
                        wait(pe, md_ready, u)
                        wait(pe, mdT_ready, u - 1)
                        pe.transpose(tp[0:96, 0, 0:128],
                                     mdp[:, :, :].bitcast(F32).rearrange("p a n -> p (a n)"),
                                     ident[:, :]).then_inc(md_ps, 1)
                    if make is not None:
                        b = r % 2
                        turn = TILES // 4 * rnd + quad
                        wait(pe, d_in[r], 32 * (turn + 1))
                        wait(pe, exp_done, u - 1)
                        for j in range(2):
                            w = slice(HALF * make + 512 * j, HALF * make + 512 * j + 512)
                            bank = lg[:, b, 512 * j:512 * j + 512]
                            pe.matmul(bank, ones_b[:, :], bias[:, w], start=True, stop=False)
                            pe.matmul(bank, xth[r][:, :], phT_h[:, w], start=False, stop=False)
                            pe.matmul(bank, xth[r][:, :], phT_l[:, w], start=False, stop=False)
                            ins = pe.matmul(bank, xtl[r][:, :], phT_h[:, w], start=False,
                                            stop=True)
                        ins.then_inc(lg_done, 1)
                    if shifts is not None:
                        b = (r - 1) % 2
                        wait(pe, mdT_ready, u)
                        wait(pe, mc_read, u)
                        for j in range(2):
                            ins = pe.matmul(lg[:, b, 512 * j:512 * j + 512], mdT[:, b, :],
                                            shift[:, 512 * j:512 * j + 512], start=False,
                                            stop=True, skip_group_check=True)
                        ins.then_inc(shifted, 1)
                    if use is not None:
                        b = (r - 3) % 4
                        first = isinstance(t, int) and t == 3
                        last = isinstance(t, int) and t == 2 and rnd > 0
                        turn = TILES // 4 * rnd + quad
                        wait(pe, scaled, u - 2)
                        wait(pe, xd_in[b], 16 * (turn + (1 if r == 3 else 0)))
                        if first:
                            wait(pe, xs_ready, use)
                        for j in range(2):
                            ins = pe.matmul(xacc[:, 512 * j:512 * j + 512], xd[b][:, :],
                                            e[:, b, 512 * j:512 * j + 512], start=first,
                                            stop=last, skip_group_check=True)
                        ins.then_inc(summed, 1)
                    if shifts == 1:
                        tile = t - 1 + TILES * (rnd - shifts)
                        wait(pe, mcp_ready, tile + 1)
                        wait(pe, mcT_ready, tile)
                        pe.transpose(tp[0:96, 1, 0:64].bitcast(BF16),
                                     mcp[:, :, :].rearrange("p a n -> p (a n)"),
                                     identb[:, :]).then_inc(mc_ps, 1)
                steps(pe, step)
                pe.wait_ge(xs_ready, 2)
                pe.wait_ge(exp_done, 2 * TILES)
                pe.wait_ge(ew_in, 48)

                def slots(g):
                    wait(pe, th_ready, g - 1)
                    for i in range(4):
                        c = 4 * g + i
                        ins = pe.transpose(lg[:, 0, 512 * (g % 2) + 128 * i:
                                              512 * (g % 2) + 128 * i + 128],
                                           xs[:, 128 * c:128 * c + 128], ident[:, :])
                    ins.then_inc(x_ps, 1)
                slots(0)
                for g in range(4):
                    if g < 3:
                        slots(g + 1)
                    pe.wait_ge(th_ready, g + 1)
                    wait(pe, thT_ready, g - 1)
                    for i in range(4):
                        ins = pe.transpose(lg[:, 1, 512 * (g % 2) + 128 * i:
                                              512 * (g % 2) + 128 * i + 128],
                                           th[:, g % 2, i, :], ident[:, :])
                    ins.then_inc(th_ps, 1)
                    pe.wait_ge(thT_ready, g + 1)
                    wait(pe, y_ready, g - 1)
                    for i in range(4):
                        c = 4 * g + i
                        at = slice(512 * (g % 2) + 128 * i, 512 * (g % 2) + 128 * i + 128)
                        pe.matmul(xacc[:, at], e_rows[:, c, :], eb[:, :], start=True, stop=False,
                                  skip_group_check=True)
                        for n in range(4):
                            ins = pe.matmul(xacc[32 * n:32 * n + 32, at],
                                            thT[:, g % 2, i, 32 * n:32 * n + 32],
                                            ew[:, 4 * c + n, :], start=False, stop=True,
                                            skip_group_check=True)
                    ins.then_inc(y_ps, 1)
                pe.wait_ge(y_ready, 4)
                pe.wait_ge(mcT_ready, TILES)


def combine(nc, phi_b, c_cshift, c_same, x2, xT2h, xT2l, ident, phT_h, phT_l, mcT, yt, out):
    with ExitStack() as stack:
        def sb(name, shape, dt=F32):
            return stack.enter_context(nc.sbuf_tensor(name, shape, dt))

        def pb(name, shape, dt=F32):
            return stack.enter_context(nc.psum_tensor(name, shape, dt))

        def sem(name):
            return stack.enter_context(nc.semaphore(name))

        sbias = sb("sbias", [128, NCH])
        rawc = sb("rawc", [3 * SLOTS, 128])
        shift = sb("shift_c", [3 * SLOTS, 128], BF16)
        same = sb("same", [128, 128])
        e = [sb(f"ec{i}", [128, NCH, CHUNK]) for i in range(2)]
        esum = sb("esum", [128, CHUNK])
        rden = sb("rden_c", [128, CHUNK])
        yT = sb("yT", [128, CHUNK])
        res = sb("res_c", [128, 2, 4, D])

        lg = pb("lg_c", [128, 4, CHUNK])
        dps = pb("dps", [128, CHUNK])
        yps = pb("yps", [128, CHUNK])
        tps = pb("tps", [128, CHUNK])

        loaded, cast = sem("c_loaded"), sem("c_cast")
        lg_done, exp_done, sum_ready, den_ps = (sem("c_lg"), sem("c_exp"), sem("c_sum"),
                                                sem("c_den"))
        scaled, y_ps, yT_ready, t_ps, res_ready = (sem("c_scaled"), sem("c_y"), sem("c_yT"),
                                                   sem("c_t"), sem("c_res"))
        stored = [sem("stored0"), sem("stored1")]
        c_add, c_rec = sem("c_chain_add"), sem("c_chain_rec")
        out_v = out.rearrange("b (i p) d -> p (b i) d", p=128)

        def steps(eng, step):
            step(0, 0, True, False, False)
            step(0, 1, True, True, False)
            step(1, 0, True, True, True)
            step(1, 1, True, True, True)
            with eng.Fori(2, STEPS // 2) as pair:
                step(pair, 0, True, True, True)
                step(pair, 1, True, True, True)
            step(STEPS // 2, 0, False, True, True)
            step(STEPS // 2, 1, False, False, True)

        with nc.Block() as block:
            @block.sync
            def _(sp):
                sp.dma_start(rawc[:, :], c_cshift).then_inc(loaded, 16)
                sp.dma_start(same[:, :], c_same).then_inc(loaded, 16)
                sp.dma_start(sbias[:, :], phi_b.rearrange("(c s) -> s c", s=128),
                             allow_slow_non_contiguous=True).then_inc(loaded, 16)

                def step(pair, par, make, use, end):
                    q = 2 * pair + par
                    if end:
                        wait(sp, res_ready, q - 1)
                        sp.dma_start(out_v[:, bass.ds(4 * (q - 2), 4), :],
                                     res[:, par]).then_inc(stored[par], 16)
                steps(sp, step)
                for i in range(2):
                    sp.wait_ge(stored[i], 16 * STEPS // 2)

            @block.scalar
            def _(act):
                act.wait_ge(loaded, 48)
                act.activation(shift[:, :], rawc[:, :], ACT.Copy).then_inc(cast, 1)

                def step(pair, par, make, use, end):
                    q = 2 * pair + par
                    if end:
                        wait(act, y_ps, q - 1)
                        wait(act, t_ps, q - 2)
                        act.activation(yT[:, :], yps[:, :], ACT.Copy).then_inc(yT_ready, 1)
                    if make:
                        wait(act, y_ps, q - 1)
                        for c in range(NCH):
                            wait(act, lg_done, NCH * q + c + 1)
                            act.activation(e[par][:, c, :], lg[:, c % 4, :], ACT.Exp,
                                           bias=sbias[:, c:c + 1]).then_inc(exp_done, 1)
                steps(act, step)

            @block.vector
            def _(dve):
                adds, recs = Chain(dve, c_add), Chain(dve, c_rec)

                def step(pair, par, make, use, end):
                    q = 2 * pair + par

                    def add(c):
                        wait(dve, exp_done, NCH * q + c + 1)
                        if c == 1:
                            wait(dve, den_ps, q)
                        first = e[par][:, 0, :] if c == 1 else esum[:, :]
                        ins = dve.tensor_tensor(esum[:, :], first, e[par][:, c, :], ALU.add)
                        if c == NCH - 1:
                            ins.then_inc(sum_ready, 1)
                        else:
                            adds.link(ins)

                    def scale(j):
                        w = e[1 - par][:, 4 * j:4 * j + 4, :]
                        dve.tensor_tensor(w, w, rden[:, :].unsqueeze(1)
                                          .broadcast_to([128, 4, CHUNK]),
                                          ALU.mult).then_inc(scaled, 1)
                    adds.start(q)
                    if make:
                        add(1)
                    if use:
                        recs.start(q - 1)
                        wait(dve, den_ps, q)
                        wait(dve, scaled, 4 * (q - 1))
                        recs.link(dve.reciprocal(rden[:, :], dps[:, :]))
                    for j in range(4):
                        if use:
                            scale(j)
                        if make:
                            for c in range(2 + 3 * j, min(5 + 3 * j, 14)):
                                add(c)
                        if j == 1 and end:
                            wait(dve, t_ps, q - 1)
                            wait(dve, stored[par], 16 * (pair - 1))
                            dve.tensor_tensor(res[:, par], tps[:, :]
                                              .rearrange("p (i d) -> p i d", i=4),
                                              x2[:, bass.ds(4 * (q - 2), 4), :],
                                              ALU.add).then_inc(res_ready, 1)
                    if make:
                        add(14)
                        add(15)
                steps(dve, step)

            @block.tensor
            def _(pe):
                pe.wait_ge(cast, 1)
                pe.wait_ge(loaded, 48)

                def step(pair, par, make, use, end):
                    q = 2 * pair + par
                    at = bass.ds(CHUNK * q, CHUNK)

                    def logits(c):
                        wait(pe, exp_done, NCH * q + c - 3)
                        bank = lg[:, c % 4, :]
                        w = slice(128 * c, 128 * c + 128)
                        pe.matmul(bank, shift[:, :], mcT[:, at], start=True, stop=False)
                        pe.matmul(bank, phT_h[:, w], xT2h[:, at], start=False, stop=False)
                        pe.matmul(bank, phT_h[:, w], xT2l[:, at], start=False, stop=False)
                        pe.matmul(bank, phT_l[:, w], xT2h[:, at], start=False,
                                  stop=True).then_inc(lg_done, 1)

                    if make:
                        logits(0)
                        logits(1)
                    if end:
                        wait(pe, yT_ready, q - 1)
                        wait(pe, res_ready, q - 2)
                        for i in range(4):
                            ins = pe.transpose(tps[:, 128 * i:128 * i + 128],
                                               yT[:, 128 * i:128 * i + 128], ident[:, :])
                        ins.then_inc(t_ps, 1)
                    if use:
                        wait(pe, sum_ready, q)
                        wait(pe, scaled, 4 * (q - 1))
                        pe.matmul(dps[:, :], same[:, :], esum[:, :], start=True,
                                  stop=True).then_inc(den_ps, 1)
                    if make:
                        for c in range(2, 10):
                            logits(c)
                    for j in range(4):
                        if use:
                            wait(pe, scaled, 4 * (q - 1) + j + 1)
                            if j == 0:
                                wait(pe, yT_ready, q - 1)
                            for c in range(4 * j, 4 * j + 4):
                                ins = pe.matmul(yps[:, :], yt[:, c, :], e[1 - par][:, c, :],
                                                start=(c == 0), stop=(c == NCH - 1))
                            if j == 3:
                                ins.then_inc(y_ps, 1)
                        if make:
                            for c in range(10 + 2 * j, min(12 + 2 * j, NCH)):
                                logits(c)
                steps(pe, step)
                pe.wait_ge(res_ready, STEPS)


def kernel(**inputs):
    import numpy as np
    import concourse.bacc as bacc
    from concourse.bass_utils import run_bass_kernel_spmd as run

    a = {n: np.asarray(v) for n, v in inputs.items()}

    def rotary_columns(w):
        r = w.reshape(w.shape[0], GROUPS, PER, 2, ROPE // 2).transpose(0, 2, 1, 3, 4)
        both = np.stack([r, r[:, :, :, ::-1, :]], axis=2)
        return np.ascontiguousarray(both.reshape(w.shape[0], 2 * HEADS * ROPE))

    inv = 1.0 / 10000.0 ** (np.arange(0, ROPE, 2, dtype=np.float32) / ROPE)
    angle = np.outer(np.arange(T, dtype=np.float32), inv)
    angle = np.concatenate([angle, angle], -1)
    sign = np.where(np.arange(ROPE) < ROPE // 2, -1.0, 1.0).astype(np.float32)
    rope = np.stack([np.cos(angle).T, np.sin(angle).T * sign[:, None]], 1)
    rope = np.tile(rope, (GROUPS, 1, 1)).astype(np.float32)
    rows, slot = np.arange(128), np.arange(NS)
    mask = np.where(rows[None, :] > rows[:, None], -1e30, 0.0).astype(np.float32)
    ones = np.zeros((128, PER, 32), np.float32)
    for m in range(PER):
        ones[:, m, HD * m:HD * m + HD] = 1.0
    same = (rows[:, None] % SLOTS == rows[None, :] % SLOTS).astype(np.float32)
    parts = np.arange(96) % 32
    dshift = -(parts[:, None] == slot[None, :HALF] // SLOTS).astype(np.float32)
    cshift = -(parts[:, None] == rows[None, :] % SLOTS).astype(np.float32)
    expert = (np.arange(EXPERTS)[:, None] == slot[None, :] // SLOTS).astype(np.float32)

    arrays = {
        "x": a["L0_attn_x"],
        "w_qkv": np.concatenate([a["L0_attn_W_q"], a["L0_attn_W_kv"]], axis=1),
        "w_k": rotary_columns(a["L0_attn_W_krope"]),
        "w_q": rotary_columns(a["L0_attn_W_qrope"]),
        "w_kcv": np.stack([a["L0_attn_W_kdec"], a["L0_attn_W_vdec"]], axis=1),
        "w_qc": a["L0_attn_W_qdec"],
        "g_kv": a["L0_attn_g_kv"].reshape(KVR, 1),
        "w_o": a["L0_attn_W_o"],
        "phi_t": a["L0_ffn_phi_w"].T,
        "phi_b": a["L0_ffn_phi_b"],
        "exp_w": a["L0_ffn_expert_w"],
        "exp_b": a["L0_ffn_expert_b"],
        "c_ident": np.eye(128, dtype=np.float32),
        "c_rope": rope, "c_mask": mask, "c_ones": ones, "c_same": same, "c_dshift": dshift,
        "c_cshift": cshift, "c_expert": expert.reshape(EXPERTS, NCH, 128),
    }
    arrays = {n: np.ascontiguousarray(v) for n, v in arrays.items()}
    nc = bacc.Bacc("TRN2", target_bir_lowering=False, num_devices=1)
    args = [nc.dram_tensor(f"in_{n}", v.shape, F32, kind="ExternalInput").ap()
            for n, v in arrays.items()]
    content_d = nc.dram_tensor("content_d", (2, 128, 2 * T), F16, kind="Internal").ap()
    rope_d = nc.dram_tensor("rope_d", (2, 2, 128, PER * T), F16, kind="Internal").ap()
    max_d = nc.dram_tensor("max_d", (2 * HEADS, T), F16, kind="Internal").ap()
    out = nc.dram_tensor("out", (BATCH, T, D), F32, kind="ExternalOutput").ap()
    layer_kernel(nc, *args, content_d, rope_d, max_d, out)
    r = run(nc, [{f"in_{n}": v for n, v in arrays.items()}], core_ids=[0])
    return r.results[0]["out"]
```

```python
import concourse.bass as bass
from concourse import mybir
from contextlib import ExitStack

F32 = mybir.dt.float32
F32R = mybir.dt.float32r
BF16 = mybir.dt.bfloat16
F16 = mybir.dt.float16
ALU = mybir.AluOpType
ACT = mybir.ActivationFunctionType
AX = mybir.AxisListType

BATCH, T, D = 16, 256, 128
HEADS, HD, ROPE = 16, 8, 32
QR, KVR = 64, 32
SCALE = float(HD + ROPE) ** -0.5
GROUPS, PER = 4, 4
EXPERTS, SLOTS = 64, 32
NS = EXPERTS * SLOTS
HALF, HALF_E = NS // 2, EXPERTS // 2
TILES = BATCH * T // 128
LN_EPS, RMS_EPS = 1e-5, 1e-6
CLIP_LOW, CLIP_HIGH = -33000.0, 65000.0
UNITS = 9
STACKED = 16 * 12
PLACES = [{(0, 1): 0, (0, 0): 1, (1, 1): 2}, {(0, 0): 0, (1, 1): 1, (0, 1): 2}]
CHUNK = 512
STEPS = BATCH * T // CHUNK
NCH = NS // 128


def wait(eng, sem, value):
    if isinstance(value, int) and value <= 0:
        return
    eng.wait_ge(sem, value)


class Chain:

    def __init__(self, eng, sem):
        self.eng, self.sem, self.per, self.n, self.base = eng, sem, None, 0, 0

    def start(self, turn):
        if self.per is None and self.n:
            self.per = self.n
        self.base, self.n = (turn * self.per if self.per else 0), 0

    def link(self, ins, meanwhile=None):
        self.n += 1
        ins.then_inc(self.sem, 1)
        if meanwhile:
            meanwhile()
        self.eng.wait_ge(self.sem, self.base + self.n)


def settle(eng, passed):
    eng.sem_inc(passed, 1)


def layernorm(dve, passed, link, src, stats, moments, var, rstd, var_ready, rstd_ready, turn, dst,
              meanwhile=(None, None, None)):
    for i in range(2):
        ins = dve.bn_stats(stats[:, i, :], src[:, i, :])
    link(ins, meanwhile[0])
    settle(dve, passed)
    for i in range(2):
        ins = dve.bn_aggr(moments[:, i, :], stats[:, i, :])
    link(ins, meanwhile[1])
    dve.tensor_scalar(var[:, :], moments[:, :, 1], LN_EPS, None, ALU.add).then_inc(var_ready, 1)
    if meanwhile[2]:
        meanwhile[2]()
    wait(dve, rstd_ready, turn)
    for i in range(2):
        ins = dve.tensor_scalar(dst[:, i, :], src[:, i, :], moments[:, i, 0:1], rstd[:, i:i + 1],
                                ALU.subtract, ALU.mult)
    return ins


def layer_kernel(nc, x, w_qkv, w_k, w_q, w_kcv, w_qc, g_kv, w_o, phi_t, phi_b, exp_w, exp_b,
                 c_ident, c_rope, c_mask, c_ones, c_same, c_dshift, c_cshift, c_expert,
                 content_d, rope_d, max_d, out):
    with ExitStack() as stack:
        def sb(name, shape, dt=F32):
            return stack.enter_context(nc.sbuf_tensor(name, shape, dt))
        x2 = sb("x2", [128, TILES, D])
        xn2 = sb("xn2", [128, TILES, D])
        xT2h = sb("xT2h", [128, TILES * 128], F32R)
        xT2l = sb("xT2l", [128, TILES * 128], F32R)
        ident = sb("ident", [128, 128])
        raw = sb("raw", [128, NS])
        high, low = sb("high", [128, NS], F32R), sb("low", [128, NS], F32R)
        rot = sb("rot", [128, 2, NS // 2])
        bias = rot[:, 0, :].bitcast(BF16)
        shift_raw = rot[0:3 * HALF_E, 1, :]
        attention(nc, x, w_qkv, w_k, w_q, w_kcv, w_qc, g_kv, w_o, phi_t, phi_b, c_ident, c_rope,
                  c_mask, c_ones, c_dshift, content_d, rope_d, max_d, x2, xn2, xT2h, xT2l, ident,
                  raw, high, low, rot, bias, shift_raw)
        mcT = sb("mcT", [3 * SLOTS, TILES * 128], BF16)
        yt = sb("yt", [128, NCH, D])
        sbias = sb("sbias", [128, NCH])
        shift_c = sb("shift_c", [3 * SLOTS, 128], BF16)
        same = sb("same", [128, 128])
        dispatch(nc, phi_b, exp_w, exp_b, c_cshift, c_same, c_expert, xn2, xT2h, xT2l, ident,
                 high, low, bias, shift_raw, raw, mcT, yt, sbias, shift_c, same)
        combine(nc, x2, xT2h, xT2l, ident, high, low, mcT, yt, sbias, shift_c, same, out)


def attention(nc, x, w_qkv, w_k, w_q, w_kcv, w_qc, g_kv, w_o, phi_t, phi_b, c_ident, c_rope,
              c_mask, c_ones, c_dshift, content_d, rope_d, max_d, x2, xn2, xT2h, xT2l, ident,
              raw, high, low, rot, bias, shift_raw):
    with ExitStack() as stack:
        def sb(name, shape, dt=F32):
            return stack.enter_context(nc.sbuf_tensor(name, shape, dt))

        def pb(name, shape, dt=F32):
            return stack.enter_context(nc.psum_tensor(name, shape, dt))

        def sem(name):
            return stack.enter_context(nc.semaphore(name))

        wkh, wkl, wqh, wql = high[:, 0:1024], low[:, 0:1024], high[:, 1024:], low[:, 1024:]
        craw = sb("craw", [128, 3, 128])
        wqch, wqcl = sb("wqch", [128, 128], F32R), sb("wqcl", [128, 128], F32R)
        gain = sb("gain", [128, 1])
        cgain = sb("cgain", [128, 2, 128])
        cgain_hi = sb("cgain_hi", [128, 2, 128], F32R)
        wkcv = sb("wkcv", [128, 2, 128], F32R)
        wqkv = sb("wqkv", [128, QR + KVR])
        wo = sb("wo", [128, D])
        rope = sb("rope", [128, 2, T])
        maskf = sb("maskf", [128, 128])
        ident16 = sb("ident16", [128, 128], F16)
        identb = sb("identb", [128, 128], BF16)
        mask = sb("mask", [128, 2, 128], BF16)
        ones = sb("ones", [128, PER, 32])
        xt = sb("xt", [128, 2, 2, D])
        xr = sb("xr", [128, 2, D])
        stats, stats2 = sb("stats", [128, 2, 6]), sb("stats2", [128, 2, 6])
        moments, moments2 = sb("moments", [128, 2, 2]), sb("moments2", [128, 2, 2])
        rstd, rstd2 = sb("rstd", [128, 2]), sb("rstd2", [128, 2])
        xn = sb("xn", [128, 2, D])
        lat = sb("lat", [128, 2, QR + KVR])
        sq, kvn = sb("sq", [128, 2, KVR]), sb("kvn", [128, 2, KVR])
        ssum, mkv, rkv = sb("ssum", [128, 2]), sb("mkv", [128, 2]), sb("rkv", [128, 2])
        var, var2 = sb("var", [128, 2]), sb("var2", [128, 2])
        power = sb("power", [128, 2])
        lst = sb("lst", [128, 2, 256], F32R)
        mx = sb("mx", [128, 2, HEADS])
        mp = sb("mp", [128, 2, 2, HEADS], F16)
        x2s, xn2s = sb("x2s", [128, 2, D]), sb("xn2s", [128, 2, D])
        vp = sb("vp", [128, 2, 2, HEADS * 32 + 32])
        xT, xT2 = sb("xT", [128, T]), sb("xT2", [128, T])
        xTh, xTl = sb("xTh", [128, T], F32R), sb("xTl", [128, T], F32R)
        lT = [sb(f"lT{i}", [128, 4, 128], F32R) for i in range(2)]
        prod = sb("prod", [128, 2, 4, 2, T])
        braw, brest = sb("braw", [128, NCH]), sb("brest", [128, NCH])
        bpart = sb("bpart", [128, 3, NCH], BF16)
        rh, rl = sb("rh", [128, 2, 4 * T], F16), sb("rl", [128, 2, 4 * T], F16)
        ch, cl = sb("ch", [128, 2 * T], F16), sb("cl", [128, 2 * T], F16)
        mT = sb("mT", [2 * HEADS, T], F16)
        qs = [sb(f"qs{i}", [128, HEADS, T], F16) for i in range(2)]
        ks = [sb(f"ks{i}", [128, HEADS, T], F16) for i in range(2)]
        pt = sb("pt", [128, 2, GROUPS, 384])
        rden, outT = sb("rden", [128, T]), sb("outT", [128, T])

        proj = pb("proj", [128, 2, 512])
        score = pb("score", [128, 4, 512])
        acc = pb("acc", [128, 512])
        misc = pb("misc", [128, 512])

        loaded, zeroed, filled = sem("weights_loaded"), sem("zeroed"), sem("stacks_filled")
        cast, weights_ready = sem("weights_cast"), sem("weights_ready")
        x_in = [sem("x_in0"), sem("x_in1")]
        xr_in = sem("xr_in")
        xn_ready, xT_ps = sem("xn_ready"), sem("xT_ps")
        xT_ready, xTl_ready = sem("xT_ready"), sem("xTl_ready")
        lat_ps, lat_read, lst_ready = sem("lat_ps"), sem("lat_read"), sem("lst_ready")
        lT_ps, lT_ready = sem("lT_ps"), sem("lT_ready")
        proj_done, proj_read = sem("proj_done"), sem("proj_read")
        content_hi, content_out = sem("content_hi"), sem("content_out")
        rope_sum, rope_hi, rope_lo = sem("rope_sum"), sem("rope_hi"), sem("rope_lo")
        hi_out, lo_out = [sem("hi_out0"), sem("hi_out1")], [sem("lo_out0"), sem("lo_out1")]
        stack_in = [sem("stack_in0"), sem("stack_in1")]
        rows_done, max_read, mp_ready = sem("rows_done"), sem("max_read"), sem("mp_ready")
        mT_ps, mT_ready, m_out, m_in = sem("mT_ps"), sem("mT_ready"), sem("m_out"), sem("m_in")
        st_done, exp_done, masked, pv_done = (sem("st_done"), sem("exp_done"), sem("masked"),
                                              sem("pv_done"))
        out_ready, y_ps, x2_ready = sem("out_ready"), sem("y_ps"), sem("x2_ready")
        v_ps, v_ready = sem("v_ps"), sem("v_ready")
        xn2_ready, xT2_ps, xT2_read = sem("xn2_ready"), sem("xT2_ps"), sem("xT2_read")
        xT2_done, x2_kept, xn2_kept = sem("xT2_done"), sem("x2_kept"), sem("xn2_kept")
        var_ready, rstd_ready = sem("var_ready"), sem("rstd_ready")
        var2_ready, rstd2_ready = sem("var2_ready"), sem("rstd2_ready")
        mkv_ready, rkv_ready = sem("mkv_ready"), sem("rkv_ready")
        c_set, c_ln1, c_lat = sem("chain_setup"), sem("chain_ln1"), sem("chain_latent")
        c_max, c_ln2, c_norm = sem("chain_max"), sem("chain_ln2"), sem("chain_norm")
        passed_dve, passed_pool = sem("passed_dve"), sem("passed_pool")
        phi_in, b_in, bpart_ready = sem("phi_in"), sem("b_in"), sem("bpart_ready")
        bias_zero, bias_in, shift_in = sem("bias_zero"), sem("bias_in"), sem("shift_in")
        high_ready, low_ready = sem("high_ready"), sem("low_ready")
        first_loaded, c_bias = sem("first_loaded"), sem("chain_bias")
        LOADS = 17

        def steps(eng, step):
            def flags(k):
                return [0 <= k + lead < BATCH for lead in range(-2, 3)]
            for k in range(-2, 4):
                step(k // 2, k % 2, *flags(k))
            with eng.Fori(2, BATCH // 2 - 1) as pair:
                for par in range(2):
                    step(pair, par, True, True, True, True, True)
            for k in range(BATCH - 2, BATCH + 2):
                step(k // 2, k % 2, *flags(k))

        def unit_heads(u):
            return [PER * (2 * (u % 2) + e) + u // 2 for e in range(2)]

        with nc.Block() as block:
            @block.sync
            def _(sp):
                def x_of(b):
                    if isinstance(b, int):
                        return x[b].rearrange("(i p) d -> p i d", p=128)
                    return x[bass.ds(b, 1)].rearrange("a (i p) d -> p (a i) d", p=128)

                for dst, src in ((ident[:, :], c_ident), (wqkv[:, :], w_qkv)):
                    sp.dma_start(dst, src).then_inc(first_loaded, 16)
                sp.dma_start(xt[:, 0], x_of(0)).then_inc(x_in[0], 16)
                for dst, src in ((raw[:, 0:1024], w_k), (rope[:, :, :], c_rope),
                                 (maskf[:, :], c_mask), (ones[:, :, :], c_ones), (wo[:, :], w_o)):
                    sp.dma_start(dst, src).then_inc(loaded, 16)
                for i in range(2):
                    sp.dma_start(raw[64 * i:64 * i + 64, 1024:], w_q).then_inc(loaded, 16)
                for i in range(2):
                    sp.dma_start(craw[64 * i:64 * i + 64, 0, :], w_qc).then_inc(loaded, 16)
                for i in range(4):
                    sp.dma_start(craw[32 * i:32 * i + 32, 1:3, :], w_kcv).then_inc(loaded, 16)
                for i in range(3):
                    sp.dma_start(gain[32 * i:32 * i + 32, :], g_kv).then_inc(loaded, 16)
                sp.dma_start(gain[96:128, :], g_kv).then_inc(loaded, 16)

                def step(pair, par, late, prev, cur, nxt, ahead):
                    k = 2 * pair + par
                    if ahead and not (isinstance(k, int) and k == -2):
                        wait(sp, xn_ready, k + 1)
                        sp.dma_start(xt[:, par], x_of(k + 2)).then_inc(x_in[par], 16)
                    if nxt:
                        rope_k, content_k = rope_d[1 - par], content_d[1 - par]

                        def send(dst, src, sent):
                            sp.dma_start(dst, src[:, :]).then_inc(sent, 16)

                        def rotary(dst, side, part, rows):
                            for r in rows:
                                sp.dma_start(dst[r:r + 32, :, :].rearrange(
                                                 "p (g c) t -> p g (c t)", g=GROUPS),
                                             rope_k[side, part]
                                             .rearrange("(g r) n -> r g n", g=GROUPS)
                                             ).then_inc(stack_in[1 - par], 16)

                        def content(dst, side, parts):
                            for i, part in enumerate(parts):
                                sp.dma_start(dst[96 + 8 * i:104 + 8 * i, :, :],
                                             content_k[part]
                                             .rearrange("(h d) (s t) -> s d h t", d=HD, s=2)[side]
                                             ).then_inc(stack_in[1 - par], 16)

                        wait(sp, rope_hi, 2 * k + 3)
                        send(rope_k[0, 0], rh[:, 0], hi_out[0])
                        wait(sp, content_hi, k + 2)
                        send(content_k[0], ch, content_out)
                        wait(sp, proj_read, UNITS * (k + 2))
                        send(content_k[1], cl, content_out)
                        wait(sp, rope_lo, 2 * k + 3)
                        send(rope_k[0, 1], rl[:, 0], lo_out[0])
                        wait(sp, rope_hi, 2 * k + 4)
                        send(rope_k[1, 0], rh[:, 1], hi_out[1])
                        wait(sp, rope_lo, 2 * k + 4)
                        send(rope_k[1, 1], rl[:, 1], lo_out[1])
                        wait(sp, hi_out[0], 16 * (k + 2))
                    if isinstance(k, int) and k == BATCH - 1:
                        sp.dma_start(raw[:, :], phi_t).then_inc(phi_in, 16)
                        sp.dma_start(braw[:, :],
                                     phi_b.rearrange("(s c) -> s c", c=NCH)).then_inc(b_in, 16)
                        sp.wait_ge(rope_lo, 2 * BATCH)
                        sp.dma_start(shift_raw, c_dshift).then_inc(shift_in, 16)
                        sp.wait_ge(bias_zero, 1)
                        for i in range(3):
                            sp.wait_ge(bpart_ready, i + 1)
                            sp.dma_start(bias[32 * i:32 * i + 1, :]
                                         .rearrange("a (s c) -> a s c", c=NCH),
                                         bpart[:, i, :]).then_inc(bias_in, 16)
                    if prev:
                        if not nxt:
                            wait(sp, x2_ready, k - 1)
                        sp.dma_start(xr[:, :, :], x_of(k - 1)).then_inc(xr_in, 16)
                    if isinstance(k, int) and k == -1:
                        sp.wait_ge(filled, 4)
                    if nxt:
                        wait(sp, st_done, 8 * k)
                        rotary(ks[1 - par], 0, 0, (0, 64))
                        wait(sp, content_out, 32 * (k + 2))
                        content(ks[1 - par], 1, (0, 1, 0))
                        wait(sp, lo_out[0], 16 * (k + 2))
                        rotary(ks[1 - par], 0, 1, (32,))
                        wait(sp, hi_out[1], 16 * (k + 2))
                        rotary(qs[1 - par], 1, 0, (0, 32))
                        content(qs[1 - par], 0, (0, 0, 1))
                        wait(sp, lo_out[1], 16 * (k + 2))
                        rotary(qs[1 - par], 1, 1, (64,))
                steps(sp, step)
                sp.wait_ge(x2_kept, BATCH)
                sp.wait_ge(xn2_kept, BATCH)
                sp.wait_ge(bias_in, 48)
                sp.wait_ge(shift_in, 16)

            @block.gpsimd
            def _(pool):
                fills = [(power[:, :], -0.5), (vp[:, 0], 0.0), (vp[:, 1], 0.0)]
                for n, (place, value) in enumerate(fills):
                    pool.memset(place, value).then_inc(zeroed, 1)
                    pool.wait_ge(zeroed, n + 1)

                def step(pair, par, late, prev, cur, nxt, ahead):
                    k = 2 * pair + par
                    if isinstance(k, int) and k == BATCH - 1:
                        pool.wait_ge(rope_lo, 2 * BATCH)
                        pool.wait_ge(rope_hi, 2 * BATCH)
                        pool.memset(bias, 0.0).then_inc(bias_zero, 1)

                    def inverse_root(src, ready, dst, done, turn):
                        wait(pool, ready, turn)
                        pool.tensor_tensor(dst[:, :], src[:, :], power[:, :],
                                           ALU.pow).then_inc(done, 1)

                    def add(side):
                        wait(pool, proj_read, UNITS * (k + 2) + 4 * side + 4)
                        wait(pool, rope_hi, 2 * k + side + 3)
                        wait(pool, rope_lo, 2 * k + side + 3)
                        pool.tensor_tensor(rot[:, side, :].rearrange("p (c t) -> p c t", c=4),
                                           prod[:, side, :, 0, :], prod[:, side, :, 1, :],
                                           ALU.add).then_inc(rope_sum, 1)

                    def causal(g):
                        for u in (2 * g, 2 * g + 1):
                            wait(pool, exp_done, 8 * (k - 1) + u + 1)
                            settle(pool, passed_pool)
                            diag = pt[:, g % 2, 2 * (u % 2):2 * (u % 2) + 2, :].rearrange(
                                "p h t -> p (h t)")[:, 128:640].rearrange("p (b t) -> p b t", b=4)
                            pool.affine_select(out=diag, in_=diag, compare_op=ALU.is_ge, fill=0.0,
                                               base=0, pattern=[[0, 4], [1, 128]],
                                               channel_multiplier=-1).then_inc(masked, 1)
                    if prev:
                        causal(0)
                    if ahead:
                        inverse_root(var, var_ready, rstd, rstd_ready, k + 3)
                    if prev:
                        causal(1)
                    if late:
                        inverse_root(var2, var2_ready, rstd2, rstd2_ready, k - 1)
                    if ahead:
                        inverse_root(mkv, mkv_ready, rkv, rkv_ready, k + 3)
                    if prev:
                        causal(2)
                    if nxt:
                        for side in range(2):
                            wait(pool, rope_hi, 2 * k + side + 3)
                            wait(pool, lo_out[side], 16 * (k + 1))
                            pool.tensor_tensor(rl[:, side, :], rot[:, side, :], rh[:, side, :],
                                               ALU.subtract).then_inc(rope_lo, 1)
                    if prev:
                        causal(3)
                    if ahead:
                        add(0)
                        add(1)
                steps(pool, step)

            @block.scalar
            def _(act):
                def prepare():
                    act.wait_ge(loaded, 16 * LOADS)
                    act.activation(wkh, raw[:, 0:1024], ACT.Copy).then_inc(cast, 1)
                    act.activation(wqh, raw[:, 1024:], ACT.Copy).then_inc(cast, 1)
                    act.activation(wqch[:, :], craw[:, 0, :], ACT.Copy).then_inc(cast, 1)
                    act.activation(ident16[:, :], ident[:, :], ACT.Copy).then_inc(cast, 1)
                    act.activation(identb[:, :], ident[:, :], ACT.Copy).then_inc(cast, 1)
                    for i in range(2):
                        act.activation(mask[:, i, :], maskf[:, :], ACT.Copy).then_inc(cast, 1)

                def step(pair, par, late, prev, cur, nxt, ahead):
                    k = 2 * pair + par

                    def rotary_hi(side, turn):
                        wait(act, rope_sum, 2 * turn + side + 1)
                        wait(act, hi_out[side], 16 * turn)
                        act.activation(rh[:, side, :], rot[:, side, :],
                                       ACT.Copy).then_inc(rope_hi, 1)

                    def exps(u):
                        wait(act, st_done, 8 * (k - 1) + u + 1)
                        wait(act, pv_done, 4 * (k - 1) + u // 2 - 1)
                        b = 2 * (u % 2)
                        act.activation(pt[:, (u // 2) % 2, b:b + 2, :], score[:, 0:2, 0:384],
                                       ACT.Exp, scale=SCALE).then_inc(exp_done, 1)
                    if prev:
                        exps(0)
                    if nxt:
                        wait(act, proj_done, UNITS * (k + 2))
                        wait(act, content_out, 32 * (k + 1))
                        act.activation(ch[:, :], proj[:, (UNITS - 1) % 2, :],
                                       ACT.Copy).then_inc(content_hi, 1)
                    if prev:
                        exps(1)
                    if nxt:
                        rotary_hi(1, k + 1)
                    if prev:
                        exps(2)
                    if ahead:
                        wait(act, xT_ps, k + 3)
                        wait(act, xTl_ready, k + 2)
                        wait(act, lat_ps, k + 2)
                        act.activation(xT[:, :], misc[:, 0:T], ACT.Copy)
                        wait(act, proj_done, UNITS * (k + 1) + 4)
                        act.activation(xTh[:, :], misc[:, 0:T], ACT.Copy).then_inc(xT_ready, 1)
                        if isinstance(k, int) and k == -2:
                            prepare()
                    if prev:
                        for u in range(3, 6):
                            exps(u)
                    if late:
                        wait(act, xT2_ps, k - 1)
                        wait(act, xT2_done, k - 2)
                        act.activation(xT2[:, :], misc[:, 0:T], ACT.Copy)
                        act.activation(xT2h[:, bass.ds(T * (k - 2), T)], misc[:, 0:T],
                                       ACT.Copy).then_inc(xT2_read, 1)
                        act.activation(xn2[:, bass.ds(2 * (k - 2), 2), :], xn2s[:, :, :],
                                       ACT.Copy).then_inc(xn2_kept, 1)
                    if prev:
                        exps(6)
                        exps(7)
                    if ahead:
                        wait(act, lT_ps, k + 3)
                        act.activation(lT[par][:, :, :].rearrange("p a t -> p (a t)"),
                                       misc[:, :], ACT.Copy).then_inc(lT_ready, 1)
                    if cur:
                        wait(act, mT_ps, k + 1)
                        act.activation(mT[:, :], misc[0:32, 0:128].bitcast(F16),
                                       ACT.Copy).then_inc(mT_ready, 1)
                        wait(act, mT_ready, k + 1)
                        act.dma_start(max_d, mT[:, :]).then_inc(m_out, 16)
                    if nxt:
                        wait(act, v_ps, k + 2)
                        wait(act, pv_done, 4 * k)
                        for i in range(2):
                            for g in range(GROUPS):
                                at = 128 * g
                                ins = act.activation(
                                    vp[:, 1 - par, i, at:at + 160].rearrange(
                                        "p (m a) -> p m a", a=40)[:, :, 0:HD],
                                    misc[:, 128 * i + 32 * g:128 * i + 32 * g + 32]
                                    .rearrange("p (m d) -> p m d", m=PER), ACT.Copy)
                        ins.then_inc(v_ready, 1)
                    if cur:
                        wait(act, m_out, 16 * (k + 1))
                        act.dma_start(qs[par][120:122, :, :],
                                      max_d.rearrange("(a h) t -> a h t", a=2)).then_inc(m_in, 16)
                    if ahead:
                        rotary_hi(0, k + 2)
                    if prev:
                        wait(act, x2_ready, k)
                        act.activation(x2[:, bass.ds(2 * (k - 1), 2), :], x2s[:, :, :],
                                       ACT.Copy).then_inc(x2_kept, 1)
                    if isinstance(k, int) and k == BATCH - 1:
                        act.wait_ge(phi_in, 16)
                        act.wait_ge(proj_done, UNITS * BATCH)
                        act.activation(high[:, :], raw[:, :], ACT.Copy).then_inc(high_ready, 1)
                steps(act, step)

            @block.vector
            def _(dve):
                setup, bias_chain = Chain(dve, c_set), Chain(dve, c_bias)
                ln1, lats = Chain(dve, c_ln1), Chain(dve, c_lat)
                maxs, ln2, norm = Chain(dve, c_max), Chain(dve, c_ln2), Chain(dve, c_norm)
                for i in range(2):
                    dve.memset(ks[i][96:128, :, :], -1.0).then_inc(filled, 1)
                    dve.memset(qs[i][96:128, :, :], 0.0).then_inc(filled, 1)

                def prepare():
                    dve.wait_ge(loaded, 16 * LOADS)
                    setup.link(dve.tensor_scalar(cgain[:, :, :], craw[:, 1:3, :], gain[:, 0:1],
                                                 None, ALU.mult))
                    setup.link(dve.tensor_copy(cgain_hi[:, :, :], cgain[:, :, :]))
                    dve.tensor_copy(wkcv[0:64, :, :], cgain[0:64, :, :])
                    dve.tensor_tensor(wkcv[64:128, :, :], cgain[64:128, :, :],
                                      cgain_hi[64:128, :, :].bitcast(F32), ALU.subtract)
                    dve.wait_ge(cast, 7)
                    for lo, whole, hi in ((wkl, raw[:, 0:1024], wkh), (wql, raw[:, 1024:], wqh),
                                          (wqcl[:, :], craw[:, 0, :], wqch[:, :])):
                        ins = dve.tensor_tensor(lo, whole, hi.bitcast(F32), ALU.subtract)
                    ins.then_inc(weights_ready, 1)

                def step(pair, par, late, prev, cur, nxt, ahead):
                    k = 2 * pair + par

                    def maxima(u):
                        wait(dve, rows_done, 8 * k + u + 1)
                        h = unit_heads(u)
                        at = slice(h[0], h[1] + 1, h[1] - h[0])
                        dve.tensor_reduce(mx[:, 0, at], score[:, 2:4, 0:128], AX.X, ALU.max)
                        dve.tensor_reduce(mx[:, 1, at], score[:, 2:4, 128:384], AX.X,
                                          ALU.max).then_inc(max_read, 1)

                    def rotate(n):
                        side, c = n // 4, n % 4
                        wait(dve, proj_done, UNITS * (k + 2) + n + 1)
                        if c == 0:
                            wait(dve, rope_sum, 2 * k + side + 3)
                        dve.tensor_tensor(prod[:, side, c], proj[:, n % 2, :]
                                          .rearrange("p (a t) -> p a t", a=2), rope[:, :, :],
                                          ALU.mult).then_inc(proj_read, 1)

                    def content_lo():
                        if nxt:
                            wait(dve, content_hi, k + 2)
                            wait(dve, content_out, 32 * (k + 1))
                            dve.tensor_tensor(cl[:, :], proj[:, (UNITS - 1) % 2, :], ch[:, :],
                                              ALU.subtract).then_inc(proj_read, 1)

                    def second_maxima():
                        if cur:
                            maxima(1)

                    if cur:
                        maxima(0)
                    if ahead:
                        ln1.start(k + 2)
                        wait(dve, x_in[par], 16 * (pair + 2))
                        wait(dve, xT_ps, k + 2)
                        wait(dve, xn_ready, k + 2)
                        layernorm(dve, passed_dve, ln1.link, xt[:, par], stats, moments, var, rstd,
                                  var_ready, rstd_ready, k + 3, xn,
                                  (second_maxima, None, content_lo)).then_inc(xn_ready, 1)
                    else:
                        second_maxima()
                        content_lo()
                    if cur:
                        maxima(2)
                    if ahead:
                        wait(dve, xT_ready, k + 3)
                        dve.tensor_tensor(xTl[:, :], xT[:, :], xTh[:, :].bitcast(F32),
                                          ALU.subtract).then_inc(xTl_ready, 1)
                    def third_maxima():
                        if cur:
                            maxima(3)

                    def latents():
                        wait(dve, lat_ps, k + 3)
                        wait(dve, lT_ps, k + 2)
                        dve.tensor_copy(lat[:, :, :].rearrange("p i c -> p (i c)"),
                                        misc[:, 0:2 * (QR + KVR)]).then_inc(lat_read, 1)
                        wait(dve, lat_read, k + 3)
                        dve.tensor_copy(lst[:, :, 0:QR], q)
                        link(dve.tensor_tensor(sq[:, :, :], kv, kv, ALU.mult))
                        link(dve.tensor_reduce(ssum[:, :], sq[:, :, :], AX.X, ALU.add))
                        dve.tensor_tensor(lst[:, :, QR:2 * QR], q, lst[:, :, 0:QR].bitcast(F32),
                                          ALU.subtract)
                        dve.tensor_scalar(mkv[:, :], ssum[:, :], 1.0 / KVR, RMS_EPS,
                                          ALU.mult, ALU.add).then_inc(mkv_ready, 1)
                    q, kv = lat[:, :, 0:QR], lat[:, :, QR:QR + KVR]
                    if ahead:
                        lats.start(k + 2)
                        link = lats.link
                    if late:
                        ln2.start(k - 2)
                        wait(dve, x2_ready, k - 1)
                        wait(dve, xT2_ps, k - 2)
                        wait(dve, xn2_kept, k - 2)
                        layernorm(dve, passed_dve, ln2.link, x2s, stats2, moments2, var2, rstd2,
                                  var2_ready, rstd2_ready, k - 1, xn2s,
                                  (third_maxima, None, latents if ahead else None)
                                  ).then_inc(xn2_ready, 1)
                    else:
                        third_maxima()
                        if ahead:
                            latents()
                    if cur:
                        maxima(4)
                        maxima(5)
                    if ahead:
                        wait(dve, rkv_ready, k + 3)
                        link(dve.tensor_tensor(kvn[:, :, :], kv, rkv[:, :].unsqueeze(2)
                                               .broadcast_to([128, 2, KVR]), ALU.mult))
                        parts = lst[:, :, 2 * QR:].rearrange("p i (r a c) -> p i r a c", r=2, a=2)
                        for r in range(2):
                            ins = dve.tensor_copy(parts[:, :, r, 0], kvn[:, :, :])
                        link(ins)
                        for r in range(2):
                            ins = dve.tensor_tensor(parts[:, :, r, 1], kvn[:, :, :],
                                                    parts[:, :, r, 0].bitcast(F32), ALU.subtract)
                        ins.then_inc(lst_ready, 1)
                        if isinstance(k, int) and k == -2:
                            prepare()
                    if cur:
                        for u in range(6, 8):
                            maxima(u)
                    if cur:
                        maxs.start(k)
                        wait(dve, max_read, 8 * (k + 1))
                        wait(dve, mT_ps, k)
                        maxs.link(dve.tensor_copy(mp[:, :, 0, :], mx[:, :, :]))
                        dve.tensor_tensor(mp[:, :, 1, :], mx[:, :, :], mp[:, :, 0, :],
                                          ALU.subtract).then_inc(mp_ready, 1)
                    if late:
                        wait(dve, xT2_read, k - 1)
                        at = bass.ds(T * (k - 2), T)
                        dve.tensor_tensor(xT2l[:, at], xT2[:, :], xT2h[:, at].bitcast(F32),
                                          ALU.subtract).then_inc(xT2_done, 1)
                    if isinstance(k, int) and k == BATCH - 1:
                        dve.wait_ge(b_in, 16)
                        rest = braw
                        for i in range(3):
                            dve.tensor_copy(bpart[:, i, :], rest[:, :]).then_inc(bpart_ready, 1)
                            if i < 2:
                                dve.wait_ge(bpart_ready, i + 1)
                                bias_chain.link(dve.tensor_tensor(brest[:, :], rest[:, :],
                                                                  bpart[:, i, :], ALU.subtract))
                                rest = brest
                    if ahead:
                        rotate(0)
                        rotate(1)
                        rotate(2)
                        rotate(3)
                    if prev:
                        norm.start(k - 1)
                        wait(dve, pv_done, 4 * k)
                        wait(dve, y_ps, k - 1)
                        norm.link(dve.reciprocal(rden[:, :], acc[:, T:2 * T]))
                        dve.tensor_tensor(outT[:, :], acc[:, 0:T], rden[:, :],
                                          ALU.mult).then_inc(out_ready, 1)
                    if ahead:
                        rotate(4)
                        rotate(5)
                    if prev:
                        wait(dve, y_ps, k)
                        wait(dve, xr_in, 16 * k)
                        wait(dve, x2_kept, k - 1)
                        wait(dve, xn2_ready, k - 1)
                        dve.tensor_tensor(x2s[:, :, :], misc[:, 0:2 * D]
                                          .rearrange("p (i d) -> p i d", i=2), xr[:, :, :],
                                          ALU.add).then_inc(x2_ready, 1)
                    if ahead:
                        rotate(6)
                        rotate(7)
                    if isinstance(k, int) and k == BATCH - 1:
                        dve.wait_ge(high_ready, 1)
                        dve.tensor_tensor(low[:, :], raw[:, :], high[:, :].bitcast(F32),
                                          ALU.subtract).then_inc(low_ready, 1)
                steps(dve, step)

            @block.tensor
            def _(pe):
                pe.wait_ge(first_loaded, 32)

                def step(pair, par, late, prev, cur, nxt, ahead):
                    k = 2 * pair + par

                    def project(n, lead=2):
                        wait(pe, proj_read, UNITS * (k + lead) + max(n - 1, 0))
                        bank = proj[:, n % 2, :]
                        xh, xl = xTh[:, :], xTl[:, :]
                        lT_n = lT[par if lead == 2 else 1 - par]
                        q = lT_n[:, 0:2, :].rearrange("p a t -> p (a t)")
                        kv = lT_n[:, 2:4, :].rearrange("p a t -> p (a t)")
                        for a in range(2):
                            if n < 4:
                                w = slice(256 * n + 128 * a, 256 * n + 128 * a + 128)
                                passes = ((wkh[:, w], xh), (wkh[:, w], xl), (wkl[:, w], xh))
                            elif n < 8:
                                w = slice(256 * (n - 4) + 128 * a, 256 * (n - 4) + 128 * a + 128)
                                passes = ((wqh[:, w], q), (wql[:, w], q))
                            elif a == 0:
                                passes = ((wqch[:, :], q), (wqcl[:, :], q))
                            else:
                                passes = ((wkcv[:, 0, :], kv),)
                            for i, (w, m) in enumerate(passes):
                                ins = pe.matmul(bank[:, T * a:T * a + T], w, m, start=(i == 0),
                                                stop=(i == len(passes) - 1))
                        ins.then_inc(proj_done, 1)

                    def keys_by_queries(u):
                        wait(pe, exp_done, 8 * (k - 1) + u)
                        for e, h in enumerate(unit_heads(u)):
                            bank = score[:, e, :]
                            for i, j in ((0, 0), (0, 1), (1, 1)):
                                at = 128 * PLACES[e][i, j]
                                ins = pe.matmul(bank[:, at:at + 128],
                                                ks[1 - par][:, h, 128 * i:128 * i + 128],
                                                qs[1 - par][:, h, 128 * j:128 * j + 128],
                                                start=True, stop=True)
                        ins.then_inc(st_done, 1)

                    def queries_by_keys(u):
                        wait(pe, max_read, 8 * k + u)
                        for e, h in enumerate(unit_heads(u)):
                            bank = score[:, 2 + e, :]
                            pe.matmul(bank[:, 0:256], identb[:, :],
                                      mask[:, :, :].rearrange("p a t -> p (a t)"), start=True,
                                      stop=False, skip_group_check=True)
                            for i, j, at in ((0, 0, 0), (1, 1, 128), (1, 0, 256)):
                                ins = pe.matmul(bank[:, at:at + 128],
                                                qs[par][0:120, h, 128 * i:128 * i + 128],
                                                ks[par][0:120, h, 128 * j:128 * j + 128],
                                                start=False, stop=True, skip_group_check=True)
                        ins.then_inc(rows_done, 1)

                    def weigh(g, den):
                        wait(pe, masked, 8 * (k - 1) + 2 * g + 2)
                        for i, q in ((0, 0), (0, 1), (1, 1)):
                            for j in range(GROUPS):
                                h = PER * j + g
                                w = ones[:, g, :] if den else \
                                    vp[:, 1 - par, i, 32 * h:32 * h + 32]
                                at = 128 * PLACES[j % 2][i, q]
                                to = T * den + 128 * q
                                ins = pe.matmul(
                                    acc[32 * j:32 * j + 32, to:to + 128], w,
                                    pt[:, g % 2, j, at:at + 128],
                                    start=(g == 0 and i == q == den == 0),
                                    stop=(g == 3 and i == q), skip_group_check=True)
                        if den:
                            ins.then_inc(pv_done, 1)

                    if prev:
                        wait(pe, m_in, 16 * k)
                    for u in range(8):
                        if prev:
                            keys_by_queries(u)
                        if cur:
                            if u == 0:
                                wait(pe, stack_in[par], STACKED * (pair + 1))
                            queries_by_keys(u)
                        if nxt and u == 0:
                            project(UNITS - 1, 1)
                        if prev and u >= 2:
                            if u == 2:
                                wait(pe, v_ready, k)
                                wait(pe, out_ready, k - 1)
                            weigh(u // 2 - 1, u % 2)
                        if ahead and u == 2:
                            wait(pe, xn_ready, k + 3)
                            wait(pe, v_ready, k + 1)
                            wait(pe, x2_ready, k - 1)
                            for i in range(2):
                                ins = pe.transpose(misc[:, 128 * i:128 * i + 128], xn[:, i, :],
                                                   ident[:, :])
                            ins.then_inc(xT_ps, 1)
                        if ahead and u == 3:
                            wait(pe, xT_ready, k + 3)
                            for i in range(2):
                                ins = pe.matmul(misc[:, 96 * i:96 * i + 96],
                                                xT[:, 128 * i:128 * i + 128], wqkv[:, :],
                                                start=True, stop=True)
                            ins.then_inc(lat_ps, 1)
                        if late and u == 5:
                            wait(pe, xn2_ready, k - 1)
                            if ahead:
                                wait(pe, lat_read, k + 3)
                            else:
                                wait(pe, x2_ready, k - 1)
                            for i in range(2):
                                ins = pe.transpose(misc[:, 128 * i:128 * i + 128], xn2s[:, i, :],
                                                   ident[:, :])
                            ins.then_inc(xT2_ps, 1)
                        if ahead and u == 6:
                            wait(pe, lst_ready, k + 3)
                            if late:
                                wait(pe, xT2_read, k - 1)
                            else:
                                wait(pe, lat_read, k + 3)
                            for a in range(2):
                                for i in range(2):
                                    ins = pe.transpose(
                                        misc[:, 256 * a + 128 * i:256 * a + 128 * i + 128],
                                        lst[:, i, 128 * a:128 * a + 128].bitcast(F32),
                                        ident[:, :])
                            ins.then_inc(lT_ps, 1)
                    if isinstance(k, int) and k == -2:
                        pe.wait_ge(loaded, 16 * LOADS)
                        pe.wait_ge(zeroed, 3)
                        pe.wait_ge(filled, 4)
                        pe.wait_ge(cast, 7)
                        pe.wait_ge(weights_ready, 1)
                    if ahead:
                        wait(pe, xTl_ready, k + 3)
                        project(0)
                        project(1)
                    if cur:
                        wait(pe, mp_ready, k + 1)
                        if ahead:
                            wait(pe, lT_ready, k + 3)
                        else:
                            wait(pe, xT2_read, k - 1)
                        for i in range(2):
                            ins = pe.transpose(misc[0:32, 64 * i:64 * i + 64].bitcast(F16),
                                               mp[:, i].rearrange("p a h -> p (a h)"),
                                               ident16[:, :])
                        ins.then_inc(mT_ps, 1)
                    if prev:
                        weigh(3, 0)
                    if ahead:
                        project(2)
                    if prev:
                        weigh(3, 1)
                    if ahead:
                        project(3)
                    if nxt:
                        if cur:
                            wait(pe, mT_ready, k + 1)
                        elif ahead:
                            wait(pe, lT_ready, k + 3)
                        for i in range(2):
                            ins = pe.matmul(misc[:, 128 * i:128 * i + 128],
                                            lT[1 - par][:, 2 + i, :], wkcv[:, 1, :],
                                            start=True, stop=True)
                        ins.then_inc(v_ps, 1)
                    if ahead:
                        wait(pe, lT_ready, k + 3)
                        project(4)
                        project(5)
                    if prev:
                        wait(pe, out_ready, k)
                        if nxt:
                            wait(pe, v_ready, k + 2)
                        elif cur:
                            wait(pe, mT_ready, k + 1)
                        else:
                            wait(pe, xT2_read, k - 1)
                        for i in range(2):
                            ins = pe.matmul(misc[:, 128 * i:128 * i + 128],
                                            outT[:, 128 * i:128 * i + 128], wo[:, :],
                                            start=True, stop=True)
                        ins.then_inc(y_ps, 1)
                    if ahead:
                        project(6)
                        project(7)
                steps(pe, step)
                pe.wait_ge(xT2_done, BATCH)
                pe.wait_ge(low_ready, 1)


def dispatch(nc, phi_b, exp_w, exp_b, c_cshift, c_same, c_expert, xn2, xT2h, xT2l, ident,
             phT_h, phT_l, bias, shift_raw, xs, mcT, yt, sbias, shift_c, same):
    with ExitStack() as stack:
        def sb(name, shape, dt=F32):
            return stack.enter_context(nc.sbuf_tensor(name, shape, dt))

        def pb(name, shape, dt=F32):
            return stack.enter_context(nc.psum_tensor(name, shape, dt))

        def sem(name):
            return stack.enter_context(nc.semaphore(name))

        ew = sb("ew", [128, EXPERTS, D])
        eb = sb("eb", [EXPERTS, D])
        e_rows = sb("e_rows", [EXPERTS, NCH, 128])
        xth = [sb(f"xth{i}", [128, 128], F32R) for i in range(4)]
        xtl = [sb(f"xtl{i}", [128, 128], F32R) for i in range(4)]
        xd = [sb(f"xd{i}", [128, D]) for i in range(4)]
        ones_b = sb("ones_b", [128, 128], BF16)
        identb = sb("identb_d", [128, 128], BF16)
        md = sb("md", [128, HALF_E])
        mdp = sb("mdp", [128, 3, HALF_E], F32R)
        mdT = sb("mdT", [3 * HALF_E, 2, 128], F32R)
        mc = sb("mc", [128, TILES, SLOTS])
        mc2, mcm, resc = sb("mc2", [128, SLOTS]), sb("mcm", [128, 2, SLOTS]), sb("resc", [128, SLOTS])
        mcp = sb("mcp", [128, 3, SLOTS], BF16)
        e = sb("e", [128, 4, HALF])
        den, rden = sb("den_d", [128, HALF_E]), sb("rden_d", [128, 2, HALF_E])
        shift = sb("shift", [3 * HALF_E, HALF], F32R)
        rawc = sb("rawc", [3 * SLOTS, 128])
        th = sb("th", [128, NCH, D])
        thT = sb("thT", [128, 2, 4, 128])
        st, mo = sb("st_d", [128, 8, 6]), sb("mo_d", [128, 8, 2])
        sv, power = sb("sv_d", [128, 2, 8]), sb("power_d", [128, 8])
        sr, nb = sb("sr_d", [128, 2, 8]), sb("nb_d", [128, 2, 8])

        lg = pb("lg", [128, 2, HALF])
        xacc = pb("xacc", [128, HALF])
        tp = pb("tp", [128, 2, 512])

        ew_in, filled, cast, c_in = (sem("ew_in"), sem("d_filled"), sem("d_cast"),
                                     sem("tables_in"))
        d_in = [sem(f"d_in{i}") for i in range(4)]
        xd_in = [sem(f"xd_in{i}") for i in range(4)]
        lg_done, md_ready, mc_read, md_ps, mdT_ready = (sem("lg_done"), sem("md_ready"),
                                                        sem("mc_read"), sem("md_ps"),
                                                        sem("mdT_ready"))
        mcm_ready, passed = sem("mcm_ready"), sem("d_passed")
        mcp_ready, mc_ps, mcT_ready = sem("mcp_ready"), sem("mc_ps"), sem("mcT_ready")
        shifted, exp_done, den_ready, scaled, summed = (sem("shifted"), sem("d_exp"),
                                                        sem("den_ready"), sem("scaled"),
                                                        sem("summed"))
        xs_ready = sem("xs_ready")
        c_md, c_mc, c_ex = sem("d_chain_md"), sem("d_chain_mc"), sem("d_chain_ex")
        den_sum = sem("den_sum")
        sv_ready, sr_ready = sem("sv_ready"), sem("sr_ready")
        x_ps, sx_ready, th_ready, th_ps, thT_ready, y_ps, y_ready = (
            sem("x_ps"), sem("sx_ready"), sem("th_ready"), sem("th_ps"), sem("thT_ready"),
            sem("d_y_ps"), sem("d_y_ready"))

        def steps(eng, step):
            def rounds(u):
                return [None if not 0 <= u - lag < 2 * TILES else int(u - lag >= TILES)
                        for lag in range(4)]
            for rnd in range(2):
                first = 2 - rnd
                for t in range(4 * first):
                    step(rnd, t // 4, t % 4, *rounds(TILES * rnd + t))
                with eng.Fori(first, TILES // 4) as quad:
                    for r in range(4):
                        step(rnd, quad, r, rnd, rnd, rnd, rnd)
            for r in range(3):
                step(2, 0, r, *rounds(2 * TILES + r))

        with nc.Block() as block:
            @block.sync
            def _(sp):
                def step(rnd, quad, r, make, shifts, norm, use):
                    t = 4 * quad + r
                    u = TILES * rnd + t
                    if isinstance(u, int) and u == 4:
                        sp.wait_ge(lg_done, 1)
                    wait(sp, summed, u - 4)
                    if make is not None:
                        at = bass.ds(128 * t, 128)
                        for dst, src in ((xth[r][:, :], xT2h[:, at]), (xtl[r][:, :], xT2l[:, at])):
                            sp.dma_start(dst.bitcast(F32), src.bitcast(F32)).then_inc(d_in[r], 16)
                    if shifts is not None:
                        at = bass.ds(t - 1 + TILES * (rnd - shifts), 1)
                        sp.dma_start(xd[(r - 1) % 4][:, :], xn2[:, at, :]
                                     .rearrange("p a d -> p (a d)")).then_inc(xd_in[(r - 1) % 4], 16)
                    if isinstance(u, int) and u == 3:
                        sp.dma_start(ew[:, :, :], exp_w.rearrange("n d h -> d n h")
                                     ).then_inc(ew_in, 16)
                        sp.dma_start(eb[:, :], exp_b).then_inc(ew_in, 16)
                        sp.dma_start(e_rows[:, :, :], c_expert).then_inc(ew_in, 16)
                        sp.dma_start(rawc[:, :], c_cshift).then_inc(c_in, 16)
                        sp.dma_start(same[:, :], c_same).then_inc(c_in, 16)
                        sp.dma_start(sbias[:, :], phi_b.rearrange("(c s) -> s c", s=128),
                                     allow_slow_non_contiguous=True).then_inc(c_in, 16)
                steps(sp, step)

            @block.gpsimd
            def _(pool):
                for n, (place, value) in enumerate(((ones_b[:, :], 1.0),
                                                    (mdp[:, 2, :].bitcast(F32), 0.0),
                                                    (power[:, :], -0.5))):
                    pool.memset(place, value).then_inc(filled, 1)
                    pool.wait_ge(filled, n + 1)
                cmc = Chain(pool, c_mc)

                def step(rnd, quad, r, make, shifts, norm, use):
                    t = 4 * quad + r
                    u = TILES * rnd + t
                    if norm is not None:
                        wait(pool, den_ready, u - 1)
                        w = e[:, (r - 2) % 4, :].rearrange("p (n s) -> p n s", s=SLOTS)
                        pool.tensor_tensor(w, w, rden[:, r % 2, :].unsqueeze(2)
                                           .broadcast_to([128, HALF_E, SLOTS]),
                                           ALU.mult).then_inc(scaled, 1)
                    if make == 1:
                        cmc.start(t)
                        wait(pool, mcm_ready, t + 1)
                        wait(pool, mc_ps, t)
                        wait(pool, mcp_ready, t)
                        link = cmc.link
                        settle(pool, passed)
                        link(pool.tensor_copy(mcp[:, 0, :], mcm[:, r % 2, :]))
                        link(pool.tensor_tensor(resc[:, :], mcm[:, r % 2, :], mcp[:, 0, :],
                                                ALU.subtract))
                        settle(pool, passed)
                        link(pool.tensor_copy(mcp[:, 1, :], resc[:, :]))
                        pool.tensor_tensor(mcp[:, 2, :], resc[:, :], mcp[:, 1, :],
                                           ALU.subtract).then_inc(mcp_ready, 1)
                steps(pool, step)
                for half in range(2):
                    pool.wait_ge(sv_ready, half + 1)
                    pool.tensor_tensor(sr[:, half, :], sv[:, half, :], power[:, :],
                                       ALU.pow).then_inc(sr_ready, 1)

            @block.scalar
            def _(act):
                act.activation(identb[:, :], ident[:, :], ACT.Copy).then_inc(cast, 1)
                act.activation(shift[:, :], shift_raw, ACT.Copy).then_inc(cast, 1)

                def step(rnd, quad, r, make, shifts, norm, use):
                    t = 4 * quad + r
                    u = TILES * rnd + t
                    if shifts is not None:
                        b = (r - 1) % 2
                        wait(act, md_ps, u)
                        wait(act, shifted, u - 2)
                        act.activation(mdT[:, b, :], tp[0:96, 0, 0:128],
                                       ACT.Copy).then_inc(mdT_ready, 1)
                        wait(act, shifted, u)
                        wait(act, summed, u - 4)
                        act.activation(e[:, (r - 1) % 4, :], lg[:, b, :],
                                       ACT.Exp).then_inc(exp_done, 1)
                        if shifts == 1:
                            tile = t - 1 + TILES * (rnd - shifts)
                            wait(act, mc_ps, tile + 1)
                            act.activation(mcT[:, bass.ds(128 * tile, 128)],
                                           tp[0:96, 1, 0:64].bitcast(BF16),
                                           ACT.Copy).then_inc(mcT_ready, 1)
                steps(act, step)
                act.wait_ge(c_in, 48)
                act.activation(shift_c[:, :], rawc[:, :], ACT.Copy).then_inc(cast, 1)

                def tanh(g):
                    half = g // 2
                    act.wait_ge(sx_ready, half + 1)
                    for c in range(4 * g, 4 * g + 4):
                        i = c % 8
                        ins = act.activation(th[:, c, :], lg[:, half, 128 * i:128 * i + 128],
                                             ACT.Tanh, bias=nb[:, half, i:i + 1],
                                             scale=sr[:, half, i:i + 1])
                    ins.then_inc(th_ready, 1)

                def turned(g):
                    act.wait_ge(th_ps, g + 1)
                    wait(act, y_ps, g - 1)
                    act.activation(thT[:, g % 2].rearrange("p i t -> p (i t)"), tp[:, g % 2, :],
                                   ACT.Copy).then_inc(thT_ready, 1)
                tanh(0)
                tanh(1)
                turned(0)
                turned(1)
                tanh(2)
                turned(2)
                tanh(3)
                turned(3)

            @block.vector
            def _(dve):
                cmd = Chain(dve, c_md)
                cex = Chain(dve, c_ex)
                def moments(half):
                    dve.wait_ge(x_ps, half + 1)
                    for i in range(8):
                        ins = dve.bn_stats(st[:, i, :], lg[:, half, 128 * i:128 * i + 128])
                    cex.link(ins)
                    for i in range(8):
                        ins = dve.bn_aggr(mo[:, i, :], st[:, i, :])
                    cex.link(ins)
                    dve.tensor_scalar(sv[:, half, :], mo[:, :, 1], LN_EPS, None,
                                      ALU.add).then_inc(sv_ready, 1)
                    dve.wait_ge(sr_ready, half + 1)
                    dve.scalar_tensor_tensor(nb[:, half, :], mo[:, :, 0], -1.0, sr[:, half, :],
                                             ALU.mult, ALU.mult).then_inc(sx_ready, 1)

                def step(rnd, quad, r, make, shifts, norm, use):
                    t = 4 * quad + r
                    u = TILES * rnd + t
                    def reciprocal():
                        if norm is not None:
                            wait(dve, den_sum, u - 1)
                            wait(dve, scaled, u - 3)
                            dve.reciprocal(rden[:, r % 2, :], den[:, :]).then_inc(den_ready, 1)
                    if make is None:
                        reciprocal()
                    if make is not None:
                        b = r % 2
                        by_slot = lg[:, b, :].rearrange("p (n s) -> p n s", s=SLOTS)
                        by_expert = lg[:, b, :].rearrange("p (n s) -> p s n", s=SLOTS)
                        cmd.start(u)
                        wait(dve, lg_done, u + 1)
                        wait(dve, md_ps, u)
                        wait(dve, md_ready, u)
                        cmd.link(dve.tensor_reduce(md[:, :], by_slot, AX.X, ALU.max), reciprocal)
                        cmd.link(dve.tensor_copy(mdp[:, 0, :], md[:, :]))
                        dve.tensor_tensor(mdp[:, 1, :], md[:, :], mdp[:, 0, :].bitcast(F32),
                                          ALU.subtract).then_inc(md_ready, 1)
                        mc_t = mc[:, bass.ds(t, 1), :].rearrange("p a s -> p (a s)")
                        if make == 1:
                            wait(dve, mcm_ready, t)
                        dve.tensor_reduce(mc_t if make == 0 else mc2[:, :], by_expert, AX.X,
                                          ALU.max).then_inc(mc_read, 1)
                    if shifts is not None:
                        wait(dve, exp_done, u)
                        wait(dve, den_ready, u - 1)
                        dve.tensor_reduce(
                            den[:, :], e[:, (r - 1) % 4, :].rearrange("p (n s) -> p n s", s=SLOTS),
                            AX.X, ALU.add).then_inc(den_sum, 1)
                    if make == 1:
                        wait(dve, mc_read, u + 1)
                        wait(dve, mcp_ready, t - 1)
                        dve.tensor_tensor(mcm[:, b, :], mc2[:, :], mc_t,
                                          ALU.max).then_inc(mcm_ready, 1)
                    if rnd == 2 and r == 1:
                        moments(0)
                    if isinstance(t, int) and t == 2 and rnd > 0:
                        dve.wait_ge(summed, TILES * (use + 1))
                        dve.tensor_scalar(xs[:, HALF * use:HALF * use + HALF], xacc[:, :],
                                          CLIP_LOW, CLIP_HIGH, ALU.max,
                                          ALU.min).then_inc(xs_ready, 1)
                steps(dve, step)
                moments(1)
                for g in range(4):
                    dve.wait_ge(y_ps, g + 1)
                    dve.tensor_copy(yt[:, 4 * g:4 * g + 4, :].rearrange("p i h -> p (i h)"),
                                    xacc[:, 512 * (g % 2):512 * (g % 2) + 512]
                                    ).then_inc(y_ready, 1)

            @block.tensor
            def _(pe):
                pe.wait_ge(cast, 1)
                pe.wait_ge(filled, 2)

                def slots(half):
                    pe.wait_ge(xs_ready, half + 1)
                    pe.wait_ge(exp_done, 2 * TILES - 1 + half)
                    for i in range(8):
                        c = 8 * half + i
                        ins = pe.transpose(lg[:, half, 128 * i:128 * i + 128],
                                           xs[:, 128 * c:128 * c + 128], ident[:, :])
                    ins.then_inc(x_ps, 1)

                def step(rnd, quad, r, make, shifts, norm, use):
                    t = 4 * quad + r
                    u = TILES * rnd + t
                    if shifts is not None:
                        wait(pe, md_ready, u)
                        wait(pe, mdT_ready, u - 1)
                        pe.transpose(tp[0:96, 0, 0:128],
                                     mdp[:, :, :].bitcast(F32).rearrange("p a n -> p (a n)"),
                                     ident[:, :]).then_inc(md_ps, 1)
                    if make is not None:
                        b = r % 2
                        turn = TILES // 4 * rnd + quad
                        wait(pe, d_in[r], 32 * (turn + 1))
                        wait(pe, exp_done, u - 1)
                        for j in range(2):
                            w = slice(HALF * make + 512 * j, HALF * make + 512 * j + 512)
                            bank = lg[:, b, 512 * j:512 * j + 512]
                            pe.matmul(bank, ones_b[:, :], bias[:, w], start=True, stop=False)
                            pe.matmul(bank, xth[r][:, :], phT_h[:, w], start=False, stop=False)
                            pe.matmul(bank, xth[r][:, :], phT_l[:, w], start=False, stop=False)
                            ins = pe.matmul(bank, xtl[r][:, :], phT_h[:, w], start=False,
                                            stop=True)
                        ins.then_inc(lg_done, 1)
                    if shifts is not None:
                        b = (r - 1) % 2
                        if isinstance(u, int) and u == 1:
                            pe.wait_ge(cast, 2)
                        wait(pe, mdT_ready, u)
                        wait(pe, mc_read, u)
                        for j in range(2):
                            ins = pe.matmul(lg[:, b, 512 * j:512 * j + 512], mdT[:, b, :],
                                            shift[:, 512 * j:512 * j + 512], start=False,
                                            stop=True, skip_group_check=True)
                        ins.then_inc(shifted, 1)
                    if rnd == 2 and r == 0:
                        slots(0)
                    if use is not None:
                        b = (r - 3) % 4
                        first = isinstance(t, int) and t == 3
                        last = isinstance(t, int) and t == 2 and rnd > 0
                        turn = TILES // 4 * rnd + quad
                        wait(pe, scaled, u - 2)
                        wait(pe, xd_in[b], 16 * (turn + (1 if r == 3 else 0)))
                        if first:
                            wait(pe, xs_ready, use)
                        for j in range(2):
                            ins = pe.matmul(xacc[:, 512 * j:512 * j + 512], xd[b][:, :],
                                            e[:, b, 512 * j:512 * j + 512], start=first,
                                            stop=last, skip_group_check=True)
                        ins.then_inc(summed, 1)
                    if shifts == 1:
                        tile = t - 1 + TILES * (rnd - shifts)
                        wait(pe, mcp_ready, tile + 1)
                        wait(pe, mcT_ready, tile)
                        pe.transpose(tp[0:96, 1, 0:64].bitcast(BF16),
                                     mcp[:, :, :].rearrange("p a n -> p (a n)"),
                                     identb[:, :]).then_inc(mc_ps, 1)
                steps(pe, step)
                pe.wait_ge(ew_in, 48)
                pe.wait_ge(mcT_ready, TILES)
                pe.wait_ge(mdT_ready, 2 * TILES)

                def turn(g):
                    pe.wait_ge(th_ready, g + 1)
                    wait(pe, thT_ready, g - 1)
                    for i in range(4):
                        ins = pe.transpose(tp[:, g % 2, 128 * i:128 * i + 128],
                                           th[:, 4 * g + i, :], ident[:, :])
                    ins.then_inc(th_ps, 1)

                def expert(g):
                    pe.wait_ge(thT_ready, g + 1)
                    wait(pe, y_ready, g - 1)
                    for i in range(4):
                        c = 4 * g + i
                        at = slice(512 * (g % 2) + 128 * i, 512 * (g % 2) + 128 * i + 128)
                        pe.matmul(xacc[:, at], e_rows[:, c, :], eb[:, :], start=True, stop=False,
                                  skip_group_check=True)
                        for n in range(4):
                            ins = pe.matmul(xacc[32 * n:32 * n + 32, at],
                                            thT[:, g % 2, i, 32 * n:32 * n + 32],
                                            ew[:, 4 * c + n, :], start=False, stop=True,
                                            skip_group_check=True)
                    ins.then_inc(y_ps, 1)
                turn(0)
                slots(1)
                turn(1)
                expert(0)
                expert(1)
                turn(2)
                expert(2)
                turn(3)
                expert(3)
                pe.wait_ge(y_ready, 4)
                pe.wait_ge(mcT_ready, TILES)


def combine(nc, x2, xT2h, xT2l, ident, phT_h, phT_l, mcT, yt, sbias, shift, same, out):
    with ExitStack() as stack:
        def sb(name, shape, dt=F32):
            return stack.enter_context(nc.sbuf_tensor(name, shape, dt))

        def pb(name, shape, dt=F32):
            return stack.enter_context(nc.psum_tensor(name, shape, dt))

        def sem(name):
            return stack.enter_context(nc.semaphore(name))

        e = [sb(f"ec{i}", [128, NCH, CHUNK]) for i in range(2)]
        esum = sb("esum", [128, CHUNK])
        rden = sb("rden_c", [128, CHUNK])
        yT = sb("yT", [128, CHUNK])
        res = sb("res_c", [128, 2, 4, D])

        lg = pb("lg_c", [128, 4, CHUNK])
        dps = pb("dps", [128, CHUNK])
        yps = pb("yps", [128, CHUNK])
        tps = pb("tps", [128, CHUNK])

        lg_done, exp_done, sum_ready, den_ps = (sem("c_lg"), sem("c_exp"), sem("c_sum"),
                                                sem("c_den"))
        scaled, y_ps, yT_ready, t_ps, res_ready = (sem("c_scaled"), sem("c_y"), sem("c_yT"),
                                                   sem("c_t"), sem("c_res"))
        stored = [sem("stored0"), sem("stored1")]
        c_add, c_rec = sem("c_chain_add"), sem("c_chain_rec")
        out_v = out.rearrange("b (i p) d -> p (b i) d", p=128)

        def steps(eng, step):
            step(0, 0, True, False, False)
            step(0, 1, True, True, False)
            step(1, 0, True, True, True)
            step(1, 1, True, True, True)
            with eng.Fori(2, STEPS // 2) as pair:
                step(pair, 0, True, True, True)
                step(pair, 1, True, True, True)
            step(STEPS // 2, 0, False, True, True)
            step(STEPS // 2, 1, False, False, True)

        with nc.Block() as block:
            @block.sync
            def _(sp):
                def step(pair, par, make, use, end):
                    q = 2 * pair + par
                    if end:
                        wait(sp, res_ready, q - 1)
                        sp.dma_start(out_v[:, bass.ds(4 * (q - 2), 4), :],
                                     res[:, par]).then_inc(stored[par], 16)
                steps(sp, step)
                for i in range(2):
                    sp.wait_ge(stored[i], 16 * STEPS // 2)

            @block.scalar
            def _(act):
                def step(pair, par, make, use, end):
                    q = 2 * pair + par
                    if end:
                        wait(act, y_ps, q - 1)
                        wait(act, t_ps, q - 2)
                        act.activation(yT[:, :], yps[:, :], ACT.Copy).then_inc(yT_ready, 1)
                    if make:
                        wait(act, y_ps, q - 1)
                        for c in range(NCH):
                            wait(act, lg_done, NCH * q + c + 1)
                            act.activation(e[par][:, c, :], lg[:, c % 4, :], ACT.Exp,
                                           bias=sbias[:, c:c + 1]).then_inc(exp_done, 1)
                steps(act, step)

            @block.vector
            def _(dve):
                adds, recs = Chain(dve, c_add), Chain(dve, c_rec)

                def step(pair, par, make, use, end):
                    q = 2 * pair + par

                    def add(c):
                        wait(dve, exp_done, NCH * q + c + 1)
                        if c == 1:
                            wait(dve, den_ps, q)
                        first = e[par][:, 0, :] if c == 1 else esum[:, :]
                        ins = dve.tensor_tensor(esum[:, :], first, e[par][:, c, :], ALU.add)
                        if c == NCH - 1:
                            ins.then_inc(sum_ready, 1)
                        else:
                            adds.link(ins)

                    def scale(j):
                        w = e[1 - par][:, 4 * j:4 * j + 4, :]
                        dve.tensor_tensor(w, w, rden[:, :].unsqueeze(1)
                                          .broadcast_to([128, 4, CHUNK]),
                                          ALU.mult).then_inc(scaled, 1)
                    adds.start(q)
                    if make:
                        add(1)
                    if use:
                        recs.start(q - 1)
                        wait(dve, den_ps, q)
                        wait(dve, scaled, 4 * (q - 1))
                        recs.link(dve.reciprocal(rden[:, :], dps[:, :]))
                    for j in range(4):
                        if use:
                            scale(j)
                        if make:
                            for c in range(2 + 3 * j, min(5 + 3 * j, 14)):
                                add(c)
                        if j == 1 and end:
                            wait(dve, t_ps, q - 1)
                            wait(dve, stored[par], 16 * (pair - 1))
                            dve.tensor_tensor(res[:, par], tps[:, :]
                                              .rearrange("p (i d) -> p i d", i=4),
                                              x2[:, bass.ds(4 * (q - 2), 4), :],
                                              ALU.add).then_inc(res_ready, 1)
                    if make:
                        add(14)
                        add(15)
                steps(dve, step)

            @block.tensor
            def _(pe):
                def step(pair, par, make, use, end):
                    q = 2 * pair + par
                    at = bass.ds(CHUNK * q, CHUNK)

                    def logits(c):
                        wait(pe, exp_done, NCH * q + c - 3)
                        bank = lg[:, c % 4, :]
                        w = slice(128 * c, 128 * c + 128)
                        pe.matmul(bank, shift[:, :], mcT[:, at], start=True, stop=False)
                        pe.matmul(bank, phT_h[:, w], xT2h[:, at], start=False, stop=False)
                        pe.matmul(bank, phT_h[:, w], xT2l[:, at], start=False, stop=False)
                        pe.matmul(bank, phT_l[:, w], xT2h[:, at], start=False,
                                  stop=True).then_inc(lg_done, 1)

                    if make:
                        logits(0)
                        logits(1)
                    if end:
                        wait(pe, yT_ready, q - 1)
                        wait(pe, res_ready, q - 2)
                        for i in range(4):
                            ins = pe.transpose(tps[:, 128 * i:128 * i + 128],
                                               yT[:, 128 * i:128 * i + 128], ident[:, :])
                        ins.then_inc(t_ps, 1)
                    if use:
                        wait(pe, sum_ready, q)
                        wait(pe, scaled, 4 * (q - 1))
                        pe.matmul(dps[:, :], same[:, :], esum[:, :], start=True,
                                  stop=True).then_inc(den_ps, 1)
                    if make:
                        for c in range(2, 10):
                            logits(c)
                    for j in range(4):
                        if use:
                            wait(pe, scaled, 4 * (q - 1) + j + 1)
                            if j == 0:
                                wait(pe, yT_ready, q - 1)
                            for c in range(4 * j, 4 * j + 4):
                                ins = pe.matmul(yps[:, :], yt[:, c, :], e[1 - par][:, c, :],
                                                start=(c == 0), stop=(c == NCH - 1))
                            if j == 3:
                                ins.then_inc(y_ps, 1)
                        if make:
                            for c in range(10 + 2 * j, min(12 + 2 * j, NCH)):
                                logits(c)
                steps(pe, step)
                pe.wait_ge(res_ready, STEPS)


def kernel(**inputs):
    import numpy as np
    import concourse.bacc as bacc
    from concourse.bass_utils import run_bass_kernel_spmd as run

    a = {n: np.asarray(v) for n, v in inputs.items()}

    def rotary_columns(w):
        r = w.reshape(w.shape[0], GROUPS, PER, 2, ROPE // 2).transpose(0, 2, 1, 3, 4)
        both = np.stack([r, r[:, :, :, ::-1, :]], axis=2)
        return np.ascontiguousarray(both.reshape(w.shape[0], 2 * HEADS * ROPE))

    inv = 1.0 / 10000.0 ** (np.arange(0, ROPE, 2, dtype=np.float32) / ROPE)
    angle = np.outer(np.arange(T, dtype=np.float32), inv)
    angle = np.concatenate([angle, angle], -1)
    sign = np.where(np.arange(ROPE) < ROPE // 2, -1.0, 1.0).astype(np.float32)
    rope = np.stack([np.cos(angle).T, np.sin(angle).T * sign[:, None]], 1)
    rope = np.tile(rope, (GROUPS, 1, 1)).astype(np.float32)
    rows, slot = np.arange(128), np.arange(NS)
    mask = np.where(rows[None, :] > rows[:, None], -1e30, 0.0).astype(np.float32)
    ones = np.zeros((128, PER, 32), np.float32)
    for m in range(PER):
        ones[:, m, HD * m:HD * m + HD] = 1.0
    same = (rows[:, None] % SLOTS == rows[None, :] % SLOTS).astype(np.float32)
    parts = np.arange(96) % 32
    dshift = -(parts[:, None] == slot[None, :HALF] // SLOTS).astype(np.float32)
    cshift = -(parts[:, None] == rows[None, :] % SLOTS).astype(np.float32)
    expert = (np.arange(EXPERTS)[:, None] == slot[None, :] // SLOTS).astype(np.float32)

    arrays = {
        "x": a["L0_attn_x"],
        "w_qkv": np.concatenate([a["L0_attn_W_q"], a["L0_attn_W_kv"]], axis=1),
        "w_k": rotary_columns(a["L0_attn_W_krope"]),
        "w_q": rotary_columns(a["L0_attn_W_qrope"]),
        "w_kcv": np.stack([a["L0_attn_W_kdec"], a["L0_attn_W_vdec"]], axis=1),
        "w_qc": a["L0_attn_W_qdec"],
        "g_kv": a["L0_attn_g_kv"].reshape(KVR, 1),
        "w_o": a["L0_attn_W_o"],
        "phi_t": a["L0_ffn_phi_w"].T,
        "phi_b": a["L0_ffn_phi_b"],
        "exp_w": a["L0_ffn_expert_w"],
        "exp_b": a["L0_ffn_expert_b"],
        "c_ident": np.eye(128, dtype=np.float32),
        "c_rope": rope, "c_mask": mask, "c_ones": ones, "c_same": same, "c_dshift": dshift,
        "c_cshift": cshift, "c_expert": expert.reshape(EXPERTS, NCH, 128),
    }
    arrays = {n: np.ascontiguousarray(v) for n, v in arrays.items()}
    nc = bacc.Bacc("TRN2", target_bir_lowering=False, num_devices=1)
    args = [nc.dram_tensor(f"in_{n}", v.shape, F32, kind="ExternalInput").ap()
            for n, v in arrays.items()]
    content_d = nc.dram_tensor("content_d", (2, 2, 128, 2 * T), F16, kind="Internal").ap()
    rope_d = nc.dram_tensor("rope_d", (2, 2, 2, 128, PER * T), F16, kind="Internal").ap()
    max_d = nc.dram_tensor("max_d", (2 * HEADS, T), F16, kind="Internal").ap()
    out = nc.dram_tensor("out", (BATCH, T, D), F32, kind="ExternalOutput").ap()
    layer_kernel(nc, *args, content_d, rope_d, max_d, out)
    r = run(nc, [{f"in_{n}": v for n, v in arrays.items()}], core_ids=[0])
    return r.results[0]["out"]
```
